# Optimizing a Trainium2 kernel written in Bass

```python
import numpy as np
import jax
import jax.numpy as jnp

def _softmax(x, axis=-1):
    return jax.nn.softmax(x, axis=axis)

def _gelu(x):
    return jax.nn.gelu(x, approximate=True)

def _silu(x):
    return jax.nn.silu(x)

def _sigmoid(x):
    return jax.nn.sigmoid(x)

def _layernorm(x, axis=-1, eps=1e-05):
    m = jnp.mean(x, axis=axis, keepdims=True)
    v = jnp.var(x, axis=axis, keepdims=True)
    return (x - m) / jnp.sqrt(v + eps)

def _scatter_add(tgt, idx, src, axis=0):
    return tgt.at[idx].add(src)

def _segment_sum(src, seg, n):
    return jax.ops.segment_sum(src, seg, n)
kernel_name = 'mk_xattn_ffn_d2_seqx_r4_3674b4'

def setup_inputs(seed: int=0):
    np.random.seed(seed)
    _w = jnp.asarray

    def _rec_inputs():
        import jax
        import jax.numpy as jnp
        _rk = jax.random.key(seed)
        x = -0.0002928 + 1 * jax.random.normal(jax.random.fold_in(_rk, 1), (32, 256, 256), jnp.float32)
        _lenS = 256 - jax.random.randint(jax.random.fold_in(_rk, 7), (32,), 0, max(1, 256 // 4) + 1, jnp.int32)
        _lenS2 = 120 - jax.random.randint(jax.random.fold_in(_rk, 8), (32,), 0, max(1, 120 // 4) + 1, jnp.int32)
        _ctx_1024P = jax.random.normal(jax.random.fold_in(_rk, 11), (32, 16, 256), jnp.float32)
        _ctx_1024c = jax.random.dirichlet(jax.random.fold_in(_rk, 511), 0.3 * jnp.ones((16,), jnp.float32), (32, 120))
        _ctx_1024t = jnp.einsum('bsk,bkd->bsd', _ctx_1024c, _ctx_1024P)
        _ctx_1024t = _ctx_1024t * jax.lax.rsqrt(jnp.mean(jnp.square(_ctx_1024t)) + 1e-12) * 0.953939
        ctx_1024 = -1.39393e-06 + 0.999914 * (_ctx_1024t + 0.3 * jax.random.normal(jax.random.fold_in(_rk, 611), (32, 120, 256), jnp.float32))
        _validS = jnp.arange(256)[None, :] < _lenS[:, None]
        _validS2 = jnp.arange(120)[None, :] < _lenS2[:, None]
        _causal = jnp.tril(jnp.ones((256, 256), dtype=bool))
        mask_BxS2_ik0 = jnp.where(jnp.broadcast_to(_validS2[:, :], (32, 120)), 0, 1).astype(jnp.int32)
        return (x, ctx_1024, mask_BxS2_ik0)
    x, ctx_1024, mask_BxS2_ik0 = _rec_inputs()

    def _L0_xattn_setup():
        import jax, jax.numpy as jnp
        import numpy as np
        DIM = 256
        NUM_HEADS = 16
        HEAD_DIM = DIM // NUM_HEADS
        SCALE = HEAD_DIM ** (-0.5)
        key = jax.random.key(seed)
        ks = jax.random.split(key, 8)
        B, QL, KL = (2, 512, 512)
        s = DIM ** (-0.5)
        return {'q': jax.random.normal(ks[0], (B, QL, DIM), jnp.float32), 'k': jax.random.normal(ks[1], (B, KL, DIM), jnp.float32), 'v': jax.random.normal(ks[2], (B, KL, DIM), jnp.float32), 'Wq': jax.random.normal(ks[3], (DIM, DIM), jnp.float32) * s, 'Wk': jax.random.normal(ks[4], (DIM, DIM), jnp.float32) * s, 'Wv': jax.random.normal(ks[5], (DIM, DIM), jnp.float32) * s, 'Wo': jax.random.normal(ks[6], (DIM, DIM), jnp.float32) * s, 'bo': jax.random.normal(ks[7], (DIM,), jnp.float32) * 0.02}
    _L0_xattn_all = _L0_xattn_setup()
    _L0_xattn_in = {k: v for k, v in _L0_xattn_all.items() if k in ('Wq', 'Wk', 'Wv', 'Wo', 'bo')}
    del _L0_xattn_all

    def _L0_ffn_setup():
        import jax, jax.numpy as jnp
        import numpy as np
        E = 16
        K = 4
        NG = 4
        TG = 2
        SCALE = 2.5
        NORM_TOPK = True
        H = 256
        I = 128
        SH_I = I * 2
        B, S = (2, 512)
        key = jax.random.key(seed)
        ks = jax.random.split(key, 9)

        def w(k, shape, fan_in):
            return jax.random.normal(k, shape, jnp.float32) * (1.0 / np.sqrt(fan_in))
        return {'hidden_states': jax.random.normal(ks[0], (B, S, H), jnp.float32), 'gate_w': w(ks[1], (E, H), H), 'gate_bias': jnp.zeros((E,), jnp.float32), 'Wg': w(ks[2], (E, I, H), H), 'Wu': w(ks[3], (E, I, H), H), 'Wd': w(ks[4], (E, H, I), I), 'Ws_g': w(ks[5], (SH_I, H), H), 'Ws_u': w(ks[6], (SH_I, H), H), 'Ws_d': w(ks[7], (H, SH_I), SH_I)}
    _L0_ffn_all = _L0_ffn_setup()
    _L0_ffn_in = {k: v for k, v in _L0_ffn_all.items() if k in ('gate_w', 'gate_bias', 'Wg', 'Wu', 'Wd', 'Ws_g', 'Ws_u', 'Ws_d')}
    del _L0_ffn_all

    def _L1_xattn_setup():
        import jax, jax.numpy as jnp
        import numpy as np
        B, LQ, LK, D = (4, 512, 512, 256)
        H = 16
        HD = D // H

        def _split_heads(x):
            b, l, _ = x.shape
            return x.reshape(b, l, H, HD).transpose(0, 2, 1, 3)
        key = jax.random.key(seed)
        ks = jax.random.split(key, 10)
        s = 0.02
        return {'hidden_states': jax.random.normal(ks[0], (B, LQ, D), jnp.float32), 'context': jax.random.normal(ks[1], (B, LK, D), jnp.float32), 'attention_mask': jax.random.randint(ks[2], (B, LK), 0, 2, jnp.int32), 'q_w': jax.random.normal(ks[3], (D, D), jnp.float32) * s, 'q_b': jnp.zeros((D,), jnp.float32), 'k_w': jax.random.normal(ks[4], (D, D), jnp.float32) * s, 'k_b': jnp.zeros((D,), jnp.float32), 'v_w': jax.random.normal(ks[5], (D, D), jnp.float32) * s, 'v_b': jnp.zeros((D,), jnp.float32)}
    _L1_xattn_all = _L1_xattn_setup()
    _L1_xattn_in = {k: v for k, v in _L1_xattn_all.items() if k in ('q_w', 'q_b', 'k_w', 'k_b', 'v_w', 'v_b')}
    del _L1_xattn_all

    def _L1_ffn_setup():
        import jax, jax.numpy as jnp
        import numpy as np
        B, S, D = (2, 512, 256)
        E, K, F = (16, 2, 128)
        FS = 256
        key = jax.random.key(seed)
        ks = jax.random.split(key, 8)

        def w(k, shape, fan_in):
            return jax.random.normal(k, shape, jnp.float32) / np.sqrt(fan_in).astype(np.float32)
        return {'x': jax.random.normal(ks[0], (B, S, D), jnp.float32), 'Wr': w(ks[1], (D, E), D), 'Wg': w(ks[2], (E, D, F), D), 'Wu': w(ks[3], (E, D, F), D), 'Wd': w(ks[4], (E, F, D), F), 'Sg': w(ks[5], (D, FS), D), 'Su': w(ks[6], (D, FS), D), 'Sd': w(ks[7], (FS, D), FS)}
    _L1_ffn_all = _L1_ffn_setup()
    _L1_ffn_in = {k: v for k, v in _L1_ffn_all.items() if k in ('Wr', 'Wg', 'Wu', 'Wd', 'Sg', 'Su', 'Sd')}
    del _L1_ffn_all
    return {'x': x, 'ctx_1024': ctx_1024, 'mask_BxS2_ik0': mask_BxS2_ik0, 'L0_xattn_Wq': _L0_xattn_in['Wq'], 'L0_xattn_Wk': _L0_xattn_in['Wk'], 'L0_xattn_Wv': _L0_xattn_in['Wv'], 'L0_xattn_Wo': _L0_xattn_in['Wo'], 'L0_xattn_bo': _L0_xattn_in['bo'], 'L0_ffn_gate_w': _L0_ffn_in['gate_w'], 'L0_ffn_gate_bias': _L0_ffn_in['gate_bias'], 'L0_ffn_Wg': _L0_ffn_in['Wg'], 'L0_ffn_Wu': _L0_ffn_in['Wu'], 'L0_ffn_Wd': _L0_ffn_in['Wd'], 'L0_ffn_Ws_g': _L0_ffn_in['Ws_g'], 'L0_ffn_Ws_u': _L0_ffn_in['Ws_u'], 'L0_ffn_Ws_d': _L0_ffn_in['Ws_d'], 'L1_xattn_q_w': _L1_xattn_in['q_w'], 'L1_xattn_q_b': _L1_xattn_in['q_b'], 'L1_xattn_k_w': _L1_xattn_in['k_w'], 'L1_xattn_k_b': _L1_xattn_in['k_b'], 'L1_xattn_v_w': _L1_xattn_in['v_w'], 'L1_xattn_v_b': _L1_xattn_in['v_b'], 'L1_ffn_Wr': _L1_ffn_in['Wr'], 'L1_ffn_Wg': _L1_ffn_in['Wg'], 'L1_ffn_Wu': _L1_ffn_in['Wu'], 'L1_ffn_Wd': _L1_ffn_in['Wd'], 'L1_ffn_Sg': _L1_ffn_in['Sg'], 'L1_ffn_Su': _L1_ffn_in['Su'], 'L1_ffn_Sd': _L1_ffn_in['Sd']}

def reference(x, ctx_1024, mask_BxS2_ik0, L0_xattn_Wq, L0_xattn_Wk, L0_xattn_Wv, L0_xattn_Wo, L0_xattn_bo, L0_ffn_gate_w, L0_ffn_gate_bias, L0_ffn_Wg, L0_ffn_Wu, L0_ffn_Wd, L0_ffn_Ws_g, L0_ffn_Ws_u, L0_ffn_Ws_d, L1_xattn_q_w, L1_xattn_q_b, L1_xattn_k_w, L1_xattn_k_b, L1_xattn_v_w, L1_xattn_v_b, L1_ffn_Wr, L1_ffn_Wg, L1_ffn_Wu, L1_ffn_Wd, L1_ffn_Sg, L1_ffn_Su, L1_ffn_Sd):
    import jax
    import jax.numpy as jnp

    def _L0_xattn_ref(q, k, v, Wq, Wk, Wv, Wo, bo):
        import jax, jax.numpy as jnp
        import numpy as np
        DIM = 256
        NUM_HEADS = 16
        HEAD_DIM = DIM // NUM_HEADS
        SCALE = HEAD_DIM ** (-0.5)
        B, QL, _ = q.shape
        KL = k.shape[1]
        qh = (q @ Wq.T).reshape(B, QL, NUM_HEADS, HEAD_DIM)
        kh = (k @ Wk.T).reshape(B, KL, NUM_HEADS, HEAD_DIM)
        vh = (v @ Wv.T).reshape(B, KL, NUM_HEADS, HEAD_DIM)
        attn = jnp.einsum('bnhc,bmhc->bhnm', qh, kh) * SCALE
        attn = jax.nn.softmax(attn, axis=-1)
        out = jnp.einsum('bhnm,bmhc->bnhc', attn, vh).reshape(B, QL, DIM)
        return out @ Wo.T + bo

    def _L0_ffn_ref(hidden_states, gate_w, gate_bias, Wg, Wu, Wd, Ws_g, Ws_u, Ws_d):
        import jax, jax.numpy as jnp
        import numpy as np
        E = 16
        K = 4
        NG = 4
        TG = 2
        SCALE = 2.5
        NORM_TOPK = True
        H = 256
        I = 128
        SH_I = I * 2
        B, S = (2, 512)
        x = hidden_states
        b, s, h = x.shape
        n = b * s
        xf = x.reshape(n, h)
        logits = xf @ gate_w.T
        scores = jax.nn.sigmoid(logits)
        sfc = scores + gate_bias
        epg = E // NG
        grp = sfc.reshape(n, NG, epg)
        g_scores = jax.lax.top_k(grp, 2)[0].sum(-1)
        _, gidx = jax.lax.top_k(g_scores, TG)
        gmask = jax.nn.one_hot(gidx, NG, dtype=sfc.dtype).sum(1)
        emask = jnp.repeat(gmask, epg, axis=1)
        masked = jnp.where(emask > 0, sfc, -jnp.inf)
        _, topk_idx = jax.lax.top_k(masked, K)
        topk_w = jnp.take_along_axis(scores, topk_idx, axis=1)
        if K > 1 and NORM_TOPK:
            topk_w = topk_w / (topk_w.sum(-1, keepdims=True) + 1e-20)
        topk_w = topk_w * SCALE
        cw = (jax.nn.one_hot(topk_idx, E, dtype=topk_w.dtype) * topk_w[..., None]).sum(1)
        hg = jnp.einsum('nh,eih->nei', xf, Wg)
        hu = jnp.einsum('nh,eih->nei', xf, Wu)
        act = jax.nn.silu(hg) * hu
        y = jnp.einsum('nei,ne,ehi->nh', act, cw, Wd)
        shared = jax.nn.silu(xf @ Ws_g.T) * (xf @ Ws_u.T) @ Ws_d.T
        y = y + shared
        return (x + y.reshape(b, s, h)).astype(hidden_states.dtype)

    def _L1_xattn_ref(hidden_states, context, attention_mask, q_w, q_b, k_w, k_b, v_w, v_b):
        import jax, jax.numpy as jnp
        import numpy as np
        B, LQ, LK, D = (4, 512, 512, 256)
        H = 16
        HD = D // H

        def _split_heads(x):
            b, l, _ = x.shape
            return x.reshape(b, l, H, HD).transpose(0, 2, 1, 3)
        q = _split_heads(hidden_states @ q_w.T + q_b)
        k = _split_heads(context @ k_w.T + k_b)
        v = _split_heads(context @ v_w.T + v_b)
        scores = jnp.einsum('bhqd,bhkd->bhqk', q, k) / jnp.sqrt(jnp.float32(HD))
        mask = (attention_mask > 0)[:, None, None, :]
        scores = jnp.where(mask, -jnp.inf, scores)
        probs = jax.nn.softmax(scores, axis=-1)
        ctx = jnp.einsum('bhqk,bhkd->bhqd', probs, v)
        ctx = ctx.transpose(0, 2, 1, 3).reshape(ctx.shape[0], ctx.shape[2], H * HD)
        return ctx

    def _L1_ffn_ref(x, Wr, Wg, Wu, Wd, Sg, Su, Sd):
        import jax, jax.numpy as jnp
        import numpy as np
        B, S, D = (2, 512, 256)
        E, K, F = (16, 2, 128)
        FS = 256
        b, s, d = x.shape
        T = b * s
        xf = x.reshape(T, d)
        shared = jax.nn.silu(xf @ Sg) * (xf @ Su) @ Sd
        probs = jax.nn.softmax(xf @ Wr, axis=-1)
        topk_p, topk_i = jax.lax.top_k(probs, K)
        n_exp = Wr.shape[1]
        cw = jnp.zeros((T, n_exp), x.dtype).at[jnp.arange(T)[:, None], topk_i].add(topk_p)

        def step(acc, ew):
            wg, wu, wd, c = ew
            y = jax.nn.silu(xf @ wg) * (xf @ wu) @ wd
            return (acc + y * c[:, None], None)
        routed, _ = jax.lax.scan(step, jnp.zeros_like(xf), (Wg, Wu, Wd, cw.T))
        return (routed + shared).reshape(b, s, d)
    x = x + _L0_xattn_ref(_layernorm(x, axis=-1), ctx_1024, ctx_1024, L0_xattn_Wq, L0_xattn_Wk, L0_xattn_Wv, L0_xattn_Wo, L0_xattn_bo)
    x = x + _L0_ffn_ref(_layernorm(x, axis=-1), L0_ffn_gate_w, L0_ffn_gate_bias, L0_ffn_Wg, L0_ffn_Wu, L0_ffn_Wd, L0_ffn_Ws_g, L0_ffn_Ws_u, L0_ffn_Ws_d)
    x = x + _L1_xattn_ref(_layernorm(x, axis=-1), ctx_1024, mask_BxS2_ik0, L1_xattn_q_w, L1_xattn_q_b, L1_xattn_k_w, L1_xattn_k_b, L1_xattn_v_w, L1_xattn_v_b)
    x = x + _L1_ffn_ref(_layernorm(x, axis=-1), L1_ffn_Wr, L1_ffn_Wg, L1_ffn_Wu, L1_ffn_Wd, L1_ffn_Sg, L1_ffn_Su, L1_ffn_Sd)
    return x

_drawn_inputs = setup_inputs


def setup_inputs(seed=0):
    import zlib

    import numpy as np

    out = dict(_drawn_inputs(seed))
    spreads = {'L0_ffn_gate_bias': (0.0, 0.1),
     'L1_xattn_q_b': (0.0, 0.8),
     'L1_xattn_k_b': (0.0, 0.8),
     'L1_xattn_v_b': (0.0, 0.1)}
    factors = {'L1_xattn_q_w': 8.0, 'L1_xattn_k_w': 8.0}
    for name, (base, spread) in spreads.items():
        noise = np.random.default_rng([zlib.crc32(name.encode()), seed]).standard_normal(out[name].shape)
        drawn = base * np.exp(spread * noise) if base else spread * noise
        out[name] = jnp.asarray(drawn.astype(out[name].dtype))
    for name, factor in factors.items():
        out[name] = (out[name] * factor).astype(out[name].dtype)
    return out
```

```python
from contextlib import ExitStack

import concourse.bass as bass
import numpy as np
from concourse import mybir

ALU = mybir.AluOpType
ACT = mybir.ActivationFunctionType
AX = mybir.AxisListType
F32 = mybir.dt.float32
BF16 = mybir.dt.bfloat16
U32 = mybir.dt.uint32
I32 = mybir.dt.int32

P = 128
B, LQ, D = 32, 256, 256
LK = 120
H, HD = 16, 16
HP = 32
AUG, MSK = HD, HD + 1
QT = LQ // P
DC = D // P
G = P // HP
HT = H // G
E, F = 16, 128
NG = 4
TOPK = (4, 2)
NTOK = B * LQ
REG = NTOK + P
NT = tuple(NTOK * k // P + E for k in TOPK)
NTMAX = 3 * P
XROWS = E * REG + E * P
SCALE = HD ** -0.5
EPS = 1e-5
BIG = 1e30
ROUTED_SCALE = 2.5
NIT = B // 2

C_ID, C_TRI, C_ONE, C_MJ = 0, P, 2 * P, 3 * P
C_IOTA = C_MJ + G * LK
C_EBASE = C_IOTA + E
C_LOW = C_EBASE + E
C_J128 = C_LOW + E * E
C_T = C_J128 + 64
C_MH = C_T + 3
C_SEL = C_MH + 2
NCONST = C_SEL + P

PER = {
    "ld": (32, 32), "ga": (0, 128), "var": (2, 2), "rstd": (2, 2), "xn": (2, 2), "xnT_ps": (2, 2),
    "xnT": (2, 2), "K_ps": (1, 1), "V_ps": (1, 1), "Q_ps": (1, 1), "KB": (1, 1), "V": (1, 1),
    "Q": (1, 1), "S": (2, 2), "smax": (2, 2), "MT": (1, 1), "Qa": (1, 1), "ST": (4, 4),
    "Pr": (4, 4), "OT_ps": (1, 1), "OT": (1, 1), "O_ps": (1, 1), "O": (1, 1), "OnT_ps": (1, 0),
    "OnT": (1, 0), "Wo": (1, 0), "xb": (1, 0), "x1": (1, 0), "lg": (1, 1), "GU": (1, 1),
    "nm": (0, 1), "th": (1, 1), "TH": (1, 1), "HS": (1, 1), "SH": (1, 1), "base": (1, 1),
    "st": (16, 16), "mask": (1, 1), "rank": (1, 1), "slots": (1, 1), "sc": (128, 64),
    "yslot": (0, 1), "chain": (35, 31),
}


def consts():
    c = np.zeros((P, NCONST), np.float32)
    c[:, C_ID:C_ID + P] = np.eye(P)
    c[:, C_TRI:C_TRI + P] = np.triu(np.ones((P, P)), 1)
    c[:, C_ONE:C_ONE + P] = 1.0
    for j in range(G):
        c[j * HP:(j + 1) * HP, C_MJ + j * LK:C_MJ + (j + 1) * LK] = 1.0
    c[:, C_IOTA:C_IOTA + E] = np.arange(E)
    c[:, C_EBASE:C_EBASE + E] = np.arange(E) * REG
    c[:, C_LOW:C_LOW + E * E] = np.tril(np.ones((E, E))).reshape(-1)
    c[:, C_J128:C_J128 + 64] = np.arange(64) * P
    c[:, C_T:C_T + 3] = np.arange(3)[None] * P + np.arange(P)[:, None]
    c[:, C_MH:C_MH + 2] = -0.5
    c[0, C_SEL:C_SEL + P] = np.arange(P) % HP == MSK
    return c


def bc(ap, axis, n):
    a = ap.unsqueeze(axis)
    shape = list(a.shape)
    shape[axis] = n
    return a.broadcast_to(shape)


def build(nc, a, out):
    ctx = ExitStack()

    def sb(name, shape, dt=F32):
        return ctx.enter_context(nc.sbuf_tensor(name, shape, dt))

    def sem(name):
        return ctx.enter_context(nc.semaphore(name))

    with ctx:
        ps = ctx.enter_context(nc.psum_tensor("ps", [P, 8, 512], F32))
        xsort = nc.dram_tensor("xsort", [XROWS, D], F32).ap()
        ysort = nc.dram_tensor("ysort", [NT[0] * P, D], F32).ap()
        based = nc.dram_tensor("based", [B, P, QT, D], F32).ap()
        tabd = [nc.dram_tensor(f"tabd{L}", [2, NTMAX], I32).ap() for L in range(2)]
        cntd = [nc.dram_tensor(f"cntd{L}", [1, E], I32).ap() for L in range(2)]

        cst = sb("cst", [P, NCONST])
        tri16 = sb("tri16", [P, 2 * P], BF16)
        gw = [sb(f"gw{L}", [P, DC, E]) for L in range(2)]
        gbias = sb("gbias", [P, E])
        bo_bc = sb("bo_bc", [P, D])
        bv_bc = sb("bv_bc", [P, D])
        bq = [sb(f"bq{L}", [P, HT]) for L in range(2)]
        bk = [sb(f"bk{L}", [P, HT]) for L in range(2)]
        wq = sb("wq", [P, DC, HT * P])
        wk = sb("wk", [P, DC, HT * P])
        wv = sb("wv", [P, DC, D])
        wo = sb("wo", [P, DC, D])
        wsgu = sb("wsgu", [P, DC, 512])
        wsd = sb("wsd", [P, DC, D])
        wgu = sb("wgu", [P, E * DC * 2 * F])
        wd = sb("wd", [P, E * D])
        mrow = sb("mrow", [1, B * LK])
        zero = sb("zero", [P, D])
        meta = sb("meta", [P, B + 2, 3, QT * 4])
        cnt = sb("cnt", [P, E])
        delta = sb("delta", [P, E])

        X = [sb(f"X{s}", [P, QT, D]) for s in range(2)]
        ctxT = [sb(f"ctxT{s}", [P, DC, LK]) for s in range(2)]
        xn2 = [sb(f"xn2{s}", [P, QT, D]) for s in range(2)]
        xnT = [sb(f"xnT{s}", [P, DC, LQ]) for s in range(2)]
        Q = [sb(f"Q{s}", [P, HT, LQ]) for s in range(2)]
        KB = [sb(f"KB{s}", [P, HT, G, LK]) for s in range(2)]
        V = [sb(f"V{s}", [LK, H, HP]) for s in range(2)]
        W = [sb(f"W{s}", [P, H, LQ]) for s in range(2)]
        O = [sb(f"O{s}", [P, QT, D]) for s in range(2)]
        xn = O
        Mp = [sb(f"Mp{s}", [P, QT, HT, G, HP]) for s in range(2)]
        ygath = [sb(f"ygath{s}", [P, QT * 4, D]) for s in range(2)]
        xb = [ygath[s][:, 0:QT, :] for s in range(2)]
        yidx = [sb(f"yidx{s}", [P, QT * 4], U32) for s in range(2)]
        xidx = [sb(f"xidx{s}", [P, QT * 4], U32) for s in range(2)]
        st6 = [sb(f"st6{s}", [P, QT, 6]) for s in range(2)]
        mv = [sb(f"mv{s}", [P, QT, 2]) for s in range(2)]
        ve = [sb(f"ve{s}", [P, QT]) for s in range(2)]
        rstd = [sb(f"rstd{s}", [P, QT]) for s in range(2)]
        nmr = [sb(f"nmr{s}", [P, QT]) for s in range(2)]
        rsum = [sb(f"rsum{s}", [P, QT, H]) for s in range(2)]
        th = [sb(f"th{s}", [P, QT, E]) for s in range(2)]
        rt = [sb(f"rt{s}", [P, 640]) for s in range(2)]
        ru = [sb(f"ru{s}", [P, QT, 8], U32) for s in range(2)]
        m16 = [sb(f"m16{s}", [P, QT, E], BF16) for s in range(2)]
        mt = [sb(f"mt{s}", [P, 3, QT * 4]) for s in range(2)]
        mg = [sb(f"mg{s}", [P, 3, QT * 4]) for s in range(2)]

        xt = [ygath[0][:, r, :] for r in range(4)]
        xtT = [ygath[1][:, r, :].rearrange("p (c q) -> p c q", c=DC) for r in range(2)]
        hg = [ygath[1][:, 2 + r, 0:F] for r in range(2)]
        hm = [ygath[1][:, 4 + r, 0:F] for r in range(2)]
        hT = [ygath[1][:, 6 + r, 0:P] for r in range(2)]
        yt = [ygath[0][:, 4 + r, :] for r in range(4)]
        mrow_i = W[0][0:1].rearrange("p h q -> p (h q)")[:, 0:B * LK].bitcast(I32)
        tb = sb("tb", [P, 160])
        tbo = sb("tbo", [P, 2, 3], I32)
        cnti = sb("cnti", [P, E], I32)
        tab = sb("tab", [1, 2, NTMAX], I32)
        cntr = sb("cntr", [1, E], I32)

        sig = {(n, s): sem(f"{n}{s}") for n in PER for s in range(2)}
        w_small = sem("w_small")
        w_small1 = sem("w_small1")
        w_exp = [sem("w_exp0"), sem("w_exp1")]
        init = sem("init")
        phase = sem("phase")
        zfill = sem("zfill")
        zero_ok = sem("zero_ok")
        cnt_s = sem("cnt_s")
        tb_s = sem("tb_s")
        tb_st, tb_ld = sem("tb_st"), sem("tb_ld")
        xl = [sem(f"xl{r}") for r in range(4)]
        yst = [sem(f"yst{r}") for r in range(4)]
        eT_ps, eT, eGU, eG, eH = sem("eT_ps"), sem("eT"), sem("eGU"), sem("eG"), sem("eH")
        eHT_ps, eHT, eD, eY = sem("eHT_ps"), sem("eHT"), sem("eD"), sem("eY")
        fin = [sem("fin0"), sem("fin1")]

        def at(n, L, u, k=None):
            per = PER[n][L]
            return (NIT * PER[n][0] if L else 0) + per * u + (per if k is None else k)

        def end_phase(e, n):
            e.drain().then_inc(phase, 1)
            e.wait_ge(phase, 5 * n)

        def cc(o, n, rows=P):
            return cst[0:rows, o:o + n]

        def apart(e):
            e.nop(nofuse=True)

        ident = cc(C_ID, P)
        NSMALL = 16 * 16
        NSMALL1 = 16 * 5

        def run_steps(e, lo, hi, fn):
            for n in range(lo, 4):
                fn(n, n)
            with e.Fori(1, hi // 4 - 1) as v:
                for i in range(4):
                    fn(v * 4 + i, i)
            for n in range(hi // 4 * 4 - 4, hi // 4 * 4):
                fn(n, n)

        block = ctx.enter_context(nc.Block())

        @block.sync
        def _(e):
            def load_small(pairs, s_):
                for dst, src in pairs:
                    e.dma_start(dst, src).then_inc(s_, 16)

            def load_exp(L):
                e.dma_start(wgu[:], a[f"wgu{L}"]).then_inc(w_exp[L], 16)
                e.dma_start(wd[:], a[f"wd{L}"]).then_inc(w_exp[L], 16)

            load_small([
                (cst[:], a["consts"]), (wk[:], a["wk0"]), (wq[:], a["wq0"]), (wv[:], a["wv0"]),
                (wo[:], a["wo0"]), (wsgu[:], a["wsgu0"]), (wsd[:], a["wsd0"]),
                (gw[0][:], a["gw0"]), (gw[1][:], a["gw1"]), (gbias[:], a["gbias"]),
                (bo_bc[:], a["bo"]), (bv_bc[:], a["bv"]), (bq[1][:], a["bq1"]),
                (bk[1][:], a["bk1"]), (bk[0][:], a["bk0"]), (mrow_i, a["mask"]),
            ], w_small)

            def attention_phase(L):
                with e.Fori(0, NIT) as u:
                    for s in range(2):
                        b = u * 2 + s
                        e.wait_ge(sig["st", s], at("st", L, u, 0))
                        apart(e)
                        e.wait_ge(sig["V_ps", s], at("V_ps", L, u, 0))
                        apart(e)
                        src = a["x"] if L == 0 else based
                        e.dma_start(X[s][:], src[bass.ds(b, 1)].rearrange("o p t d -> (o p) t d")
                                    ).then_inc(sig["ld", s], 16)
                        e.dma_start(ctxT[s][:], a["ctxT"][bass.ds(b, 1)].rearrange("o p c k -> (o p) c k")
                                    ).then_inc(sig["ld", s], 16)
                    for s in range(2):
                        b = u * 2 + s
                        e.wait_ge(sig["base", s], at("base", L, u))
                        apart(e)
                        e.dma_start(based[bass.ds(b, 1)].rearrange("o p t d -> (o p) t d"), X[s][:]
                                    ).then_inc(sig["st", s], 16)
                for s in range(2):
                    e.wait_ge(sig["st", s], at("st", L, NIT - 1))

            def tables(L):
                e.wait_ge(tb_s, TBN * L + TBN)
                e.dma_start(cntd[L], cnti[0:1, :]).then_inc(tb_st, 16)
                for k in range(2):
                    for c in range(3):
                        e.dma_start(tabd[L][k:k + 1, c * P:(c + 1) * P].rearrange("o p -> p o"),
                                    tbo[:, k, c:c + 1]).then_inc(tb_st, 16)
                e.wait_ge(tb_st, 16 * 7 * (L + 1))
                e.dma_start(cntr[:], cntd[L]).then_inc(tb_ld, 16)
                e.dma_start(tab[:], tabd[L]).then_inc(tb_ld, 16)
                e.wait_ge(tb_ld, 32 * (L + 1))
                with e.Fori(0, E) as x:
                    c = e.value_load(cntr[0:1, bass.ds(x, 1)], min_val=0, max_val=NTOK)
                    e.dma_start(xsort[bass.ds(c + x * REG, P), :], zero[:]).then_inc(zfill, 16)
                e.wait_ge(zfill, 16 * E + 16 * E * (L + 1))

            def expert_phase(L):
                n0, r0 = (0, 0) if L == 0 else (NT[0], NT[0] // 4)

                def load(n, r):
                    if not (isinstance(n, int) and n < 4 and L == 0):
                        e.wait_ge(eT_ps, n0 + n - 3)
                        apart(e)
                    row = e.value_load(tab[0:1, 0, bass.ds(n, 1)], min_val=0, max_val=XROWS - P)
                    e.dma_start(xt[r], xsort[bass.ds(row, P), :]).then_inc(xl[r], 16)

                def store(n, r):
                    e.wait_ge(eY, n0 + n + 1)
                    apart(e)
                    e.dma_start(ysort[bass.ds(n * P, P), :], yt[r]).then_inc(yst[r], 16)

                for n in range(4):
                    load(n, n)
                with e.Fori(0, NT[L] // 4 - 1) as v:
                    for r in range(4):
                        load(v * 4 + r + 4, r)
                        store(v * 4 + r, r)
                for r in range(4):
                    store(NT[L] - 4 + r, r)
                for r in range(4):
                    e.wait_ge(yst[r], 16 * (r0 + NT[L] // 4))

            e.wait_ge(zero_ok, 1)
            for n in range(E):
                e.dma_start(xsort[E * REG + n * P:E * REG + (n + 1) * P, :], zero[:]).then_inc(zfill, 16)
            load_exp(0)
            attention_phase(0)
            end_phase(e, 1)
            load_small([(wk[:], a["wk1"]), (wq[:], a["wq1"]), (wv[:], a["wv1"]),
                        (wsgu[:], a["wsgu1"]), (wsd[:], a["wsd1"])], w_small1)
            tables(0)
            end_phase(e, 2)
            expert_phase(0)
            end_phase(e, 3)
            load_exp(1)
            attention_phase(1)
            end_phase(e, 4)
            tables(1)
            end_phase(e, 5)
            expert_phase(1)
            end_phase(e, 6)
            with e.Fori(0, NIT) as u:
                for s in range(2):
                    b = u * 2 + s
                    e.wait_ge(fin[s], u)
                    apart(e)
                    e.wait_ge(sig["st", s], at("st", 1, NIT - 1) + u * 16)
                    apart(e)
                    e.dma_start(X[s][:], based[bass.ds(b, 1)].rearrange("o p t d -> (o p) t d")
                                ).then_inc(xl[s], 16)
                for s in range(2):
                    b = u * 2 + s
                    e.wait_ge(fin[s], u + 1)
                    apart(e)
                    e.dma_start(out[bass.ds(b, 1)].rearrange("o p t d -> (o p) t d"), X[s][:]
                                ).then_inc(sig["st", s], 16)
            for s in range(2):
                e.wait_ge(sig["st", s], at("st", 1, NIT - 1) + NIT * 16)

        @block.gpsimd
        def _(e):
            e.memset(zero[:], 0.0).then_inc(zero_ok, 1)
            for s in range(2):
                e.memset(Mp[s][:], 0.0).then_inc(init, 1)
                e.memset(V[s][:], 0.0)
                e.wait_ge(init, s + 1)
            e.memset(meta[:], 0.0).then_inc(init, 1)
            e.wait_ge(w_small, NSMALL)

            def scatter(L, s):
                for t in range(QT):
                    for k in range(TOPK[L]):
                        e.indirect_dma_start(
                            out=xsort, in_=xn2[s][:, t, :], in_offset=None,
                            out_offset=bass.IndirectOffsetOnAxis(
                                ap=xidx[s][:, t * 4 + k:t * 4 + k + 1], axis=0),
                        ).then_inc(sig["sc", s], 16)

            def gather(L, s, signal):
                for t in range(QT):
                    for k in range(TOPK[L]):
                        e.indirect_dma_start(
                            out=ygath[s][:, t * 4 + k, :], out_offset=None, in_=ysort,
                            in_offset=bass.IndirectOffsetOnAxis(
                                ap=yidx[s][:, t * 4 + k:t * 4 + k + 1], axis=0),
                        ).then_inc(signal, 16)

            def rstds(L, u, s, k):
                e.wait_ge(sig["var", s], at("var", L, u, k))
                e.tensor_tensor(rstd[s][:], ve[s][:], cc(C_MH, 2), ALU.pow).then_inc(sig["rstd", s], 1)

            def attention_phase(L):
                with e.Fori(0, NIT) as u:
                    if L == 1:
                        for s in range(2):
                            e.wait_ge(sig["yslot", s], at("yslot", L, u))
                            apart(e)
                            gather(0, s, sig["ga", s])
                    for s in range(2):
                        rstds(L, u, s, 1)
                    if L == 0:
                        for s in range(2):
                            e.wait_ge(sig["ld", s], at("ld", L, u))
                            e.wait_ge(sig["x1", s], at("x1", L, u, 0))
                            e.tensor_tensor(xb[s], X[s][:], bc(bo_bc[:], 1, QT), ALU.add
                                            ).then_inc(sig["xb", s], 1)
                    for s in range(2):
                        rstds(L, u, s, 2)
                    for s in range(2):
                        e.wait_ge(sig["slots", s], at("slots", L, u))
                        apart(e)
                        scatter(L, s)
                for s in range(2):
                    e.wait_ge(sig["sc", s], at("sc", L, NIT - 1))

            for L in range(2):
                attention_phase(L)
                for k in range(3):
                    end_phase(e, 3 * L + 1 + k)
            with e.Fori(0, NIT) as u:
                for s in range(2):
                    e.wait_ge(sig["yslot", s], at("yslot", 1, NIT - 1) + 1 + u)
                    apart(e)
                    gather(1, s, sig["ga", s])

        @block.scalar
        def _(e):
            def attention_phase(L):
                e.wait_ge(w_small, NSMALL)
                with e.Fori(0, NIT) as u:
                    def copy_xnT(s, k):
                        e.wait_ge(sig["xnT_ps", s], at("xnT_ps", L, u, k))
                        e.activation(xnT[s][:], ps[:, 4 * s, :].rearrange("p (c q) -> p c q", c=DC),
                                     ACT.Copy).then_inc(sig["xnT", s], 1)

                    for s in range(2):
                        copy_xnT(s, 1)
                    for s in range(2):
                        e.wait_ge(sig["Q_ps", s], at("Q_ps", L, u))
                        if L == 0:
                            e.activation(Q[s][:], ps[:, 4 * s + 1:4 * s + 3, :].rearrange(
                                "p k (i q) -> p (k i) q", i=2), ACT.Copy).then_inc(sig["Q", s], 1)
                        else:
                            for i in range(HT):
                                ins = e.activation(
                                    Q[s][:, i, :], ps[:, 4 * s + 1 + i // 2, i % 2 * LQ:(i % 2 + 1) * LQ],
                                    ACT.Identity, bias=bq[L][:, i:i + 1])
                            ins.then_inc(sig["Q", s], 1)
                    for s in range(2):
                        for i in range(HT):
                            bank = 4 * s + (2 if i % 2 == 0 else 0)
                            e.wait_ge(sig["ST", s], at("ST", L, u, i + 1))
                            e.activation(
                                W[s][0:LK, G * i:G * (i + 1), :],
                                ps[0:LK, bank:bank + 2, :].rearrange("p k (h q) -> p (k h) q", h=2),
                                ACT.Exp, scale=SCALE).then_inc(sig["Pr", s], 1)
                    for s in range(2):
                        e.wait_ge(sig["OT_ps", s], at("OT_ps", L, u))
                        e.activation(Q[s][:], ps[:, 4 * s + 2:4 * s + 4, :].rearrange(
                            "p k (i q) -> p (k i) q", i=2), ACT.Copy).then_inc(sig["OT", s], 1)
                    if L == 0:
                        for s in range(2):
                            e.wait_ge(sig["OnT_ps", s], at("OnT_ps", L, u))
                            e.activation(xnT[s][:], ps[:, 4 * s + 2, :].rearrange(
                                "p (c q) -> p c q", c=DC), ACT.Copy).then_inc(sig["OnT", s], 1)
                    for s in range(2):
                        copy_xnT(s, 2)
                    for s in range(2):
                        lg = ps[:, 4 * s + 1, 0:QT * E].rearrange("p (t e) -> p t e", t=QT)
                        if L == 0:
                            e.wait_ge(sig["lg", s], at("lg", L, u))
                            e.activation(th[s][:], lg, ACT.Tanh, scale=0.5).then_inc(sig["th", s], 1)
                        e.wait_ge(sig["GU", s], at("GU", L, u))
                        e.activation(W[s][:, 0:2, :], ps[:, 4 * s + 2, :].rearrange(
                            "p (c q) -> p c q", c=2), ACT.Tanh, scale=0.5).then_inc(sig["TH", s], 1)
                        if L == 1:
                            e.wait_ge(sig["nm", s], at("nm", L, u))
                            for t in range(QT):
                                ins = e.activation(th[s][:, t, :], lg[:, t, :], ACT.Exp,
                                                   bias=rt[s][:, t:t + 1])
                            ins.then_inc(sig["th", s], 1)

            def expert_phase(L):
                n0 = 0 if L == 0 else NT[0]

                def copy_x(n, r):
                    e.wait_ge(eT_ps, n0 + n + 1)
                    if not (isinstance(n, int) and n < 2 and L == 0):
                        e.wait_ge(eGU, n0 + n - 1)
                    e.activation(xtT[r % 2], ps[:, r % 2, 0:D].rearrange("p (c q) -> p c q", c=DC),
                                 ACT.Copy).then_inc(eT, 1)

                def gate(n, r):
                    e.wait_ge(eGU, n0 + n + 1)
                    if not (isinstance(n, int) and n < 2 and L == 0):
                        e.wait_ge(eH, n0 + n - 1)
                    e.activation(hg[r % 2], ps[:, 2 + r % 2, 0:F], ACT.Silu).then_inc(eG, 1)

                def step(n, r):
                    if not (isinstance(n, int) and n == NT[L] - 1):
                        copy_x(n + 1, r + 1)
                    gate(n, r)

                copy_x(0, 0)
                run_steps(e, 0, NT[L], step)

            for L in range(2):
                attention_phase(L)
                end_phase(e, 3 * L + 1)
                end_phase(e, 3 * L + 2)
                expert_phase(L)
                end_phase(e, 3 * L + 3)

        @block.vector
        def _(e):
            count = {}

            def link(ins, s, L, u):
                k = count[s] = count[s] + 1
                ins.then_inc(sig["chain", s], 1)
                e.wait_ge(sig["chain", s], at("chain", L, u, k))

            def link_apart(ins, s, L, u):
                link(ins, s, L, u)
                apart(e)

            for s in range(2):
                e.memset(rt[s][:], -BIG)
            e.memset(cnt[:], 0.0)
            e.wait_ge(init, 3)
            for s in range(2):
                e.memset(V[s][:, :, HD:HD + 1], 1.0)
            e.wait_ge(w_small, NSMALL)
            e.tensor_copy(tri16[:], cc(C_TRI, 2 * P)).then_inc(init, 1)
            e.tensor_scalar(mrow[:], mrow_i, 0.0, -BIG, ALU.is_gt, ALU.mult).then_inc(init, 1)

            def yslots_chain(s, lk, b, K, signal):
                oh = rt[s][:, 256:256 + QT * 4 * E].rearrange("p (k e) -> p k e", e=E)
                lk(e.tensor_copy(mg[s][:], meta[:, bass.ds(b, 1)].rearrange("p o k t -> p (o k) t")))
                lk(e.tensor_tensor(oh, bc(mg[s][:, 2, :], 2, E), bc(cc(C_IOTA, E), 1, QT * 4), ALU.is_equal))
                lk(e.tensor_tensor(oh, oh, bc(delta[:], 1, QT * 4), ALU.mult))
                lk(e.tensor_reduce(mt[s][:, 0, :], oh, AX.X, ALU.add))
                e.tensor_tensor(yidx[s][:], mt[s][:, 0, :], mg[s][:, 1, :], ALU.add).then_inc(signal, 1)

            def combine(s, lk, K):
                for k in range(K):
                    for t in range(QT):
                        c = t * 4 + k
                        ins = e.scalar_tensor_tensor(out=X[s][:, t, :], in0=ygath[s][:, c, :],
                                                     scalar=mg[s][:, 0, c:c + 1], in1=X[s][:, t, :],
                                                     op0=ALU.mult, op1=ALU.add)
                        if t == QT - 1 and k < K - 1:
                            lk(ins)
                return ins

            def attention_phase(L):
                K = TOPK[L]
                with e.Fori(0, NIT) as u:
                    count[0] = count[1] = 0

                    def stats(s):
                        for t in range(QT):
                            ins = e.bn_stats(st6[s][:, t, :], X[s][:, t, :])
                        link_apart(ins, s, L, u)
                        for t in range(QT):
                            ins = e.bn_aggr(mv[s][:, t, :], st6[s][:, t, :])
                        link(ins, s, L, u)
                        e.tensor_scalar(ve[s][:], mv[s][:, :, 1], EPS, None, ALU.add
                                        ).then_inc(sig["var", s], 1)

                    def norm(s, dst, k):
                        e.wait_ge(sig["rstd", s], at("rstd", L, u, k))
                        link(e.scalar_tensor_tensor(out=nmr[s][:], in0=mv[s][:, :, 0], scalar=-1.0,
                                                    in1=rstd[s][:], op0=ALU.mult, op1=ALU.mult), s, L, u)
                        for t in range(QT):
                            ins = e.tensor_scalar(dst[:, t, :], X[s][:, t, :], rstd[s][:, t:t + 1],
                                                  nmr[s][:, t:t + 1], ALU.mult, ALU.add)
                        ins.then_inc(sig["xn", s], 1)

                    if L == 1:
                        for s in range(2):
                            yslots_chain(s, lambda i: link(i, s, L, u), u * 2 + s, TOPK[0],
                                         sig["yslot", s])
                    for s in range(2):
                        e.wait_ge(sig["ld", s], at("ld", L, u))
                        if L == 1:
                            e.wait_ge(sig["ga", s], at("ga", L, u))
                            link(combine(s, lambda i: link(i, s, L, u), TOPK[0]), s, L, u)
                        stats(s)
                    for s in range(2):
                        norm(s, xn[s], 1)
                    for s in range(2):
                        e.wait_ge(sig["K_ps", s], at("K_ps", L, u))
                        for i in range(HT):
                            ins = e.scalar_tensor_tensor(
                                out=KB[s][:, i, :, :], in0=bc(ps[:, 4 * s + 3, i * LK:(i + 1) * LK], 1, G),
                                scalar=bk[L][:, i:i + 1],
                                in1=cc(C_MJ, G * LK).rearrange("p (j k) -> p j k", j=G),
                                op0=ALU.add, op1=ALU.mult)
                        ins.then_inc(sig["KB", s], 1)
                        e.wait_ge(sig["V_ps", s], at("V_ps", L, u))
                        v_ps = ps[0:LK, 4 * s, 0:D].rearrange("p (h c) -> p h c", h=H)
                        if L == 0:
                            ins = e.tensor_copy(V[s][:, :, 0:HD], v_ps)
                        else:
                            ins = e.tensor_tensor(V[s][:, :, 0:HD], v_ps,
                                                  bv_bc[0:LK, :].rearrange("p (h c) -> p h c", h=H), ALU.add)
                        ins.then_inc(sig["V", s], 1)
                    for t in range(QT):
                        for s in range(2):
                            e.wait_ge(sig["S", s], at("S", L, u, t + 1))
                            e.tensor_reduce(
                                Mp[s][:, t, :, :, AUG],
                                ps[:, 4 * s:4 * s + 4, 0:G * LK].rearrange("p k (j c) -> p k j c", j=G),
                                AX.X, ALU.max).then_inc(sig["smax", s], 1)
                    for s in range(2):
                        e.wait_ge(sig["MT", s], at("MT", L, u))
                        e.tensor_tensor(Q[s][:], Q[s][:], ps[:, 4 * s:4 * s + 2, :].rearrange(
                            "p k (i q) -> p (k i) q", i=2), ALU.subtract).then_inc(sig["Qa", s], 1)
                    for s in range(2):
                        e.wait_ge(sig["O_ps", s], at("O_ps", L, u))
                        o_ps = ps[:, 4 * s:4 * s + 2, :].rearrange("p t (h c) -> p t h c", c=HP)
                        link(e.reciprocal(rsum[s][:], o_ps[:, :, :, AUG]), s, L, u)
                        o = O[s][:].rearrange("p t (h c) -> p t h c", c=HD)
                        ins = e.tensor_tensor(o, o_ps[:, :, :, 0:HD], bc(rsum[s][:], 3, HD), ALU.mult)
                        if L == 0:
                            ins.then_inc(sig["O", s], 1)
                        else:
                            link(ins, s, L, u)
                            e.tensor_tensor(X[s][:], X[s][:], O[s][:], ALU.add).then_inc(sig["O", s], 1)
                    for s in range(2):
                        if L == 0:
                            e.wait_ge(sig["Wo", s], at("Wo", L, u))
                            e.wait_ge(sig["xb", s], at("xb", L, u))
                            e.tensor_tensor(X[s][:], ps[:, 4 * s + 3, :].rearrange("p (t d) -> p t d", t=QT),
                                            xb[s], ALU.add).then_inc(sig["x1", s], 1)
                            e.wait_ge(sig["x1", s], at("x1", L, u))
                        else:
                            e.wait_ge(sig["O", s], at("O", L, u))
                        stats(s)
                    for s in range(2):
                        e.wait_ge(sig["sc", s], at("sc", L, u, 0))
                        norm(s, xn2[s], 2)
                    if L == 1:
                        for s in range(2):
                            e.wait_ge(sig["lg", s], at("lg", L, u))
                            apart(e)
                            for t in range(QT):
                                ins = e.max(rt[s][:, 16 + 8 * t:24 + 8 * t],
                                            ps[:, 4 * s + 1, t * E:(t + 1) * E])
                            link(ins, s, L, u)
                            e.tensor_scalar(rt[s][:, 0:2],
                                            rt[s][:, 16:32].rearrange("p (t m) -> p t m", t=2)[:, :, 0],
                                            -1.0, None, ALU.mult).then_inc(sig["nm", s], 1)
                    for s in range(2):
                        e.wait_ge(sig["TH", s], at("TH", L, u))
                        g_ps = ps[:, 4 * s + 2, :].rearrange("p (c q) -> p c q", c=2)
                        u_ps = ps[:, 4 * s + 3, :].rearrange("p (c q) -> p c q", c=2)
                        link(e.scalar_tensor_tensor(out=W[s][:, 2:4, :], in0=W[s][:, 0:2, :], scalar=1.0,
                                                    in1=g_ps, op0=ALU.add, op1=ALU.mult), s, L, u)
                        e.scalar_tensor_tensor(out=W[s][:, 4:6, :], in0=W[s][:, 2:4, :], scalar=0.5,
                                               in1=u_ps, op0=ALU.mult, op1=ALU.mult
                                               ).then_inc(sig["HS", s], 1)
                    for s in range(2):
                        e.wait_ge(sig["th", s], at("th", L, u))
                        route(L, u, s)
                    for s in range(2):
                        e.wait_ge(sig["SH", s], at("SH", L, u))
                        sh = ps[:, 4 * s, :].rearrange("p (t d) -> p t d", t=QT)
                        if L == 0:
                            link(e.tensor_tensor(X[s][:], sh, X[s][:], ALU.add), s, L, u)
                            e.tensor_tensor(X[s][:], X[s][:], xn2[s][:], ALU.add).then_inc(sig["base", s], 1)
                        else:
                            e.tensor_tensor(X[s][:], sh, X[s][:], ALU.add).then_inc(sig["base", s], 1)
                    for s in range(2):
                        place_rows(L, u, s)
                    for s in range(2):
                        assert count[s] == PER["chain"][L], (L, count)

            def route(L, u, s):
                K = TOPK[L]
                r = rt[s]
                lk = lambda i: link(i, s, L, u)
                lka = lambda i: link_apart(i, s, L, u)
                tv = r[:, 32:48].rearrange("p (t m) -> p t m", t=QT)
                oh = r[:, 256:256 + QT * 4 * E].rearrange("p (t k e) -> p t k e", t=QT, k=4)[:, :, 0:K, :]
                tmp = r[:, 384:384 + QT * 4 * E].rearrange("p (t k e) -> p t k e", t=QT, k=4)[:, :, 0:K, :]
                wk_, sk_, ek_ = (mt[s][:, i, :].rearrange("p (t k) -> p t k", t=QT)[:, :, 0:K] for i in range(3))
                iota = cc(C_IOTA, E)
                if L == 0:
                    sc = r[:, 48:80].rearrange("p (t e) -> p t e", t=QT)
                    sfc = r[:, 80:112].rearrange("p (t e) -> p t e", t=QT)
                    lk(e.tensor_scalar(sc, th[s][:], 0.5, 0.5, ALU.mult, ALU.add))
                    lk(e.tensor_tensor(sfc, sc, bc(gbias[:], 1, QT), ALU.add))
                    g4 = r[:, 80:112].rearrange("p (g m) -> p g m", m=4)
                    pr = r[:, 112:160].rearrange("p (g m) -> p g m", m=6)
                    e.tensor_tensor(pr[:, :, 0:3], g4[:, :, 0:3], g4[:, :, 1:4], ALU.add)
                    e.tensor_tensor(pr[:, :, 3:5], g4[:, :, 0:2], g4[:, :, 2:4], ALU.add)
                    lk(e.tensor_tensor(pr[:, :, 5:6], g4[:, :, 0:1], g4[:, :, 3:4], ALU.add))
                    gs = r[:, 160:176].rearrange("p (t m) -> p t m", t=QT)
                    lka(e.tensor_reduce(gs[:, :, 0:NG], pr.rearrange("p (t g) m -> p t g m", t=QT), AX.X, ALU.max))
                    gm = r[:, 176:192].rearrange("p (t m) -> p t m", t=QT)
                    for t in range(QT):
                        ins = e.max(gm[:, t, :], gs[:, t, :])
                    lka(ins)
                    for t in range(QT):
                        ins = e.max_index(ru[s][:, t, :], gm[:, t, :], gs[:, t, :])
                    lk(ins)
                    gi = r[:, 192:196].rearrange("p (t m) -> p t m", t=QT)
                    lk(e.tensor_copy(gi, ru[s][:, :, 0:2]))
                    eq = r[:, 196:212].rearrange("p (t m g) -> p t m g", t=QT, m=2)
                    lk(e.tensor_tensor(eq, bc(gi, 3, NG), bc(bc(iota[:, 0:NG], 1, 2), 1, QT), ALU.is_equal))
                    sel = r[:, 212:220].rearrange("p (t g) -> p t g", t=QT)
                    lk(e.tensor_tensor(sel, eq[:, :, 0, :], eq[:, :, 1, :], ALU.add))
                    lk(e.tensor_scalar(sel, sel, 2 * BIG, -BIG, ALU.mult, ALU.add))
                    mk = r[:, 220:252].rearrange("p (t g m) -> p t g m", t=QT, m=4)
                    lka(e.tensor_tensor(mk, sfc.rearrange("p t (g m) -> p t g m", m=4), bc(sel, 3, 4), ALU.min))
                    mk = r[:, 220:252].rearrange("p (t e) -> p t e", t=QT)
                else:
                    sc = r[:, 48:80].rearrange("p (t e) -> p t e", t=QT)
                    lk(e.tensor_reduce(r[:, 4:6], th[s][:], AX.X, ALU.add))
                    lk(e.reciprocal(r[:, 6:8], r[:, 4:6]))
                    lka(e.tensor_tensor(sc, th[s][:], bc(r[:, 6:8], 2, E), ALU.mult))
                    mk = sc
                for t in range(QT):
                    ins = e.max(tv[:, t, :], mk[:, t, :])
                lka(ins)
                for t in range(QT):
                    ins = e.max_index(ru[s][:, t, :], tv[:, t, :], mk[:, t, :])
                lk(ins)
                lk(e.tensor_copy(ek_, ru[s][:, :, 0:K]))
                lk(e.tensor_tensor(oh, bc(ek_, 3, E), bc(bc(iota, 1, K), 1, QT), ALU.is_equal))
                with nc.allow_low_precision(reason="a sum of at most one 1"):
                    e.tensor_reduce(m16[s][:], oh.rearrange("p t k e -> p t e k"), AX.X, ALU.add
                                    ).then_inc(sig["mask", s], 1)
                if L == 0:
                    lk(e.tensor_tensor(tmp, oh, bc(sc, 2, K), ALU.mult))
                    lk(e.tensor_reduce(wk_, tmp, AX.X, ALU.add))
                    lk(e.tensor_reduce(r[:, 4:6], wk_, AX.X, ALU.add))
                    lk(e.tensor_scalar(r[:, 4:6], r[:, 4:6], 1e-20, None, ALU.add))
                    lk(e.reciprocal(r[:, 6:8], r[:, 4:6]))
                    lk(e.scalar_tensor_tensor(out=wk_, in0=wk_, scalar=ROUTED_SCALE, in1=bc(r[:, 6:8], 2, K),
                                              op0=ALU.mult, op1=ALU.mult))
                else:
                    lk(e.tensor_copy(wk_, tv[:, :, 0:K]))

            def place_rows(L, u, s):
                K = TOPK[L]
                r = rt[s]
                lk = lambda i: link(i, s, L, u)
                lka = lambda i: link_apart(i, s, L, u)
                oh = r[:, 256:256 + QT * 4 * E].rearrange("p (t k e) -> p t k e", t=QT, k=4)[:, :, 0:K, :]
                tmp = r[:, 384:384 + QT * 4 * E].rearrange("p (t k e) -> p t k e", t=QT, k=4)[:, :, 0:K, :]
                sk_ = mt[s][:, 1, :].rearrange("p (t k) -> p t k", t=QT)[:, :, 0:K]
                pos = r[:, 48:80].rearrange("p (t e) -> p t e", t=QT)
                e.wait_ge(sig["rank", s], at("rank", L, u))
                cbase = 2 * NIT * L
                e.wait_ge(cnt_s, cbase + u * 2 + s)
                lk(e.tensor_tensor(pos, ps[:, 4 * s + 1, 64:96].rearrange("p (t e) -> p t e", t=QT),
                                   bc(cnt[:], 1, QT), ALU.add))
                e.tensor_tensor(cnt[:], ps[:, 4 * s + 1, 96:112], cnt[:], ALU.add).then_inc(cnt_s, 1)
                lk(e.tensor_tensor(pos, pos, bc(cc(C_EBASE, E), 1, QT), ALU.add))
                lk(e.tensor_tensor(tmp, oh, bc(pos, 2, K), ALU.mult))
                lka(e.tensor_reduce(sk_, tmp, AX.X, ALU.add))
                lk(e.tensor_copy(meta[:, bass.ds(u * 2 + s, 1)].rearrange("p o k t -> p (o k) t"), mt[s][:]))
                e.tensor_copy(xidx[s][:].rearrange("p (t k) -> p t k", t=QT)[:, :, 0:K], sk_
                              ).then_inc(sig["slots", s], 1)

            def tables(L):
                n = [TBN * L]

                def lk(ins):
                    n[0] += 1
                    ins.then_inc(tb_s, 1)
                    e.wait_ge(tb_s, n[0])

                nt, ci = tb[:, 0:E], tb[:, E:2 * E]
                et, ct = tb[:, 32:35], tb[:, 35:38]
                low = cc(C_LOW, E * E).rearrange("p (e f) -> p e f", f=E)
                big = rt[0][:, 0:0]
                cmpb = ygath[0][:].rearrange("p k d -> p (k d)")[:, 0:E * 64].rearrange("p (e j) -> p e j", j=64)
                sq = ygath[0][:].rearrange("p k d -> p (k d)")[:, 1024:1280].rearrange("p (e f) -> p e f", f=E)
                le = tb[:, 64:112].rearrange("p (c e) -> p c e", e=E)
                ln = tb[:, 112:160].rearrange("p (c e) -> p c e", e=E)
                tt = cc(C_T, 3)
                lk(e.tensor_copy(cnti[:], cnt[:]))
                lk(e.tensor_tensor(cmpb, bc(cnt[:], 2, 64), bc(cc(C_J128, 64), 1, E), ALU.is_gt))
                lk(e.tensor_reduce(nt, cmpb, AX.X, ALU.add))
                lk(e.tensor_tensor(sq, low, bc(nt, 1, E), ALU.mult))
                lk(e.tensor_reduce(ci, sq, AX.X, ALU.add))
                lk(e.tensor_tensor(le, bc(ci, 1, 3), bc(tt, 2, E), ALU.is_le))
                lk(e.tensor_tensor(ln, le, bc(nt, 1, 3), ALU.mult))
                lk(e.tensor_reduce(et, le, AX.X, ALU.add))
                lk(e.tensor_reduce(ct, ln, AX.X, ALU.add))
                lk(e.tensor_tensor(ct, tt, ct, ALU.subtract))
                lk(e.tensor_scalar(tb[:, 38:41], et, float(REG), None, ALU.mult))
                lk(e.scalar_tensor_tensor(out=tbo[:, 0, :], in0=ct, scalar=float(P), in1=tb[:, 38:41],
                                          op0=ALU.mult, op1=ALU.add))
                lk(e.tensor_scalar(tbo[:, 1, :], et, float(E - 1), None, ALU.min))
                lk(e.tensor_tensor(delta[:], ci, nt, ALU.subtract))
                lk(e.scalar_tensor_tensor(out=delta[:], in0=delta[:], scalar=float(P), in1=cc(C_EBASE, E),
                                          op0=ALU.mult, op1=ALU.subtract))
                lk(e.memset(cnt[:], 0.0))
                assert n[0] == TBN * (L + 1), n

            def expert_phase(L):
                n0, r0 = (0, 0) if L == 0 else (NT[0], NT[0] // 4)

                def early(n, k):
                    return isinstance(n, int) and n < k and L == 0

                def mul(n, r):
                    e.wait_ge(eG, n0 + n + 1)
                    if not early(n, 2):
                        e.wait_ge(eHT_ps, n0 + n - 1)
                    e.tensor_tensor(hm[r % 2], hg[r % 2], ps[:, 2 + r % 2, F:2 * F], ALU.mult
                                    ).then_inc(eH, 1)

                def copy_h(n, r):
                    e.wait_ge(eHT_ps, n0 + n + 1)
                    if not early(n, 2):
                        e.wait_ge(eD, n0 + n - 1)
                    e.tensor_copy(hT[r % 2], ps[:, 4 + r % 2, 0:P]).then_inc(eHT, 1)

                def copy_y(n, r, v):
                    e.wait_ge(eD, n0 + n + 1)
                    if not early(n, 4):
                        e.wait_ge(yst[r % 4], 16 * (r0 + v))
                    e.tensor_copy(yt[r % 4], ps[:, 6 + r % 2, 0:D]).then_inc(eY, 1)

                def step(n, i, v):
                    last = isinstance(n, int) and n >= NT[L]
                    if not last:
                        mul(n, i)
                    if not (isinstance(n, int) and n < 2):
                        copy_y(n - 2, i + 2, v if i >= 2 else v - 1)
                    if not (isinstance(n, int) and (n < 1 or n > NT[L])):
                        copy_h(n - 1, i + 3)

                for n in range(4):
                    step(n, n, 0)
                with e.Fori(1, NT[L] // 4 - 1) as v:
                    for i in range(4):
                        step(v * 4 + i, i, v)
                for n in range(NT[L] - 4, NT[L] + 2):
                    step(n, n % 4, n // 4)

            for L in range(2):
                attention_phase(L)
                end_phase(e, 3 * L + 1)
                tables(L)
                end_phase(e, 3 * L + 2)
                expert_phase(L)
                end_phase(e, 3 * L + 3)

            cb = at("chain", 1, NIT - 1)
            with e.Fori(0, NIT) as u:
                num = {0: 0, 1: 0}

                def lkf(s):
                    def f(ins):
                        num[s] += 1
                        ins.then_inc(sig["chain", s], 1)
                        e.wait_ge(sig["chain", s], cb + u * C1N + num[s])
                    return f

                for s in range(2):
                    yslots_chain(s, lkf(s), u * 2 + s, TOPK[1], sig["yslot", s])
                for s in range(2):
                    e.wait_ge(xl[s], 16 * (NT[0] + NT[1]) // 4 + 16 * (u + 1))
                    e.wait_ge(sig["ga", s], at("ga", 1, NIT - 1) + 64 * (u + 1))
                    combine(s, lkf(s), TOPK[1]).then_inc(fin[s], 1)
                assert num[0] == C1N, num

        @block.tensor
        def _(e):
            def attention_phase(L):
                e.wait_ge(init, 5)
                e.wait_ge(w_small, NSMALL)
                if L == 1:
                    e.wait_ge(w_small1, NSMALL1)
                with e.Fori(0, NIT) as u:
                    def transpose_x(s, src, k):
                        e.wait_ge(sig["xn", s], at("xn", L, u, k))
                        for t in range(QT):
                            for c in range(DC):
                                mm = e.transpose(ps[:, 4 * s, c * LQ + t * P:c * LQ + (t + 1) * P],
                                                 src[:, t, c * P:(c + 1) * P], ident)
                        mm.then_inc(sig["xnT_ps", s], 1)

                    for s in range(2):
                        e.wait_ge(sig["base", s], at("base", L, u, 0))
                        e.wait_ge(sig["slots", s], at("slots", L, u, 0))
                        transpose_x(s, xn[s], 1)
                    for s in range(2):
                        k0 = 4 * s
                        b = u * 2 + s
                        e.wait_ge(sig["ld", s], at("ld", L, u))
                        for i in range(HT):
                            for c in range(DC):
                                mm = e.matmul(ps[:, k0 + 3, i * LK:(i + 1) * LK],
                                              wk[:, c, i * P:(i + 1) * P], ctxT[s][:, c, :],
                                              start=(c == 0), stop=(c == DC - 1 and L == 0))
                            if L == 1:
                                mm = e.matmul(ps[:, k0 + 3, i * LK:(i + 1) * LK], cc(C_SEL, P, 1),
                                              mrow[0:1, bass.ds(b * LK, LK)], start=False, stop=True)
                        mm.then_inc(sig["K_ps", s], 1)
                        e.wait_ge(sig["xnT", s], at("xnT", L, u, 1))
                        for c in range(DC):
                            mm = e.matmul(ps[0:LK, k0, 0:D], ctxT[s][:, c, :], wv[:, c, :],
                                          start=(c == 0), stop=(c == DC - 1))
                        mm.then_inc(sig["V_ps", s], 1)
                        for i in range(HT):
                            for c in range(DC):
                                mm = e.matmul(ps[:, k0 + 1 + i // 2, i % 2 * LQ:(i % 2 + 1) * LQ],
                                              wq[:, c, i * P:(i + 1) * P], xnT[s][:, c, :],
                                              start=(c == 0), stop=(c == DC - 1))
                        mm.then_inc(sig["Q_ps", s], 1)
                    for t in range(QT):
                        for s in range(2):
                            if t == 0:
                                e.wait_ge(sig["KB", s], at("KB", L, u))
                                e.wait_ge(sig["V", s], at("V", L, u))
                                e.wait_ge(sig["Q", s], at("Q", L, u))
                            else:
                                e.wait_ge(sig["smax", s], at("smax", L, u, 1))
                            for i in range(HT):
                                mm = e.matmul(ps[:, 4 * s + i, 0:G * LK], Q[s][:, i, t * P:(t + 1) * P],
                                              KB[s][:, i, :, :].rearrange("p j k -> p (j k)"),
                                              start=True, stop=True)
                            mm.then_inc(sig["S", s], 1)
                    for s in range(2):
                        e.wait_ge(sig["smax", s], at("smax", L, u, 2))
                        for i in range(HT):
                            for t in range(QT):
                                mm = e.transpose(
                                    ps[:, 4 * s + i // 2, i % 2 * LQ + t * P:i % 2 * LQ + (t + 1) * P],
                                    Mp[s][:, t, i, :, :].rearrange("p j c -> p (j c)"), ident)
                        mm.then_inc(sig["MT", s], 1)
                    for s in range(2):
                        e.wait_ge(sig["Qa", s], at("Qa", L, u))
                        for i in range(HT):
                            bank = 4 * s + (2 if i % 2 == 0 else 0)
                            if i >= 2:
                                e.wait_ge(sig["Pr", s], at("Pr", L, u, i - 1))
                            for j in range(G):
                                mm = e.matmul(ps[0:LK, bank + j // 2, j % 2 * LQ:(j % 2 + 1) * LQ],
                                              KB[s][:, i, j, :], Q[s][:, i, :], start=True, stop=True)
                            mm.then_inc(sig["ST", s], 1)
                    for s in range(2):
                        e.wait_ge(sig["Pr", s], at("Pr", L, u, 3))
                        for i in range(HT):
                            if i == HT - 1:
                                e.wait_ge(sig["Pr", s], at("Pr", L, u, 4))
                            for j in range(G):
                                h = G * i + j
                                mm = e.matmul(
                                    ps[j * HP:(j + 1) * HP, 4 * s + 2 + i // 2, i % 2 * LQ:(i % 2 + 1) * LQ],
                                    V[s][:, h, :], W[s][0:LK, h, :], start=True, stop=True)
                        mm.then_inc(sig["OT_ps", s], 1)
                    for s in range(2):
                        e.wait_ge(sig["OT", s], at("OT", L, u))
                        for t in range(QT):
                            for i in range(HT):
                                mm = e.transpose(ps[:, 4 * s + t, i * P:(i + 1) * P],
                                                 Q[s][:, i, t * P:(t + 1) * P], ident)
                        mm.then_inc(sig["O_ps", s], 1)
                    if L == 0:
                        for s in range(2):
                            e.wait_ge(sig["O", s], at("O", L, u))
                            for t in range(QT):
                                for c in range(DC):
                                    mm = e.transpose(ps[:, 4 * s + 2, c * LQ + t * P:c * LQ + (t + 1) * P],
                                                     O[s][:, t, c * P:(c + 1) * P], ident)
                            mm.then_inc(sig["OnT_ps", s], 1)
                        for s in range(2):
                            e.wait_ge(sig["OnT", s], at("OnT", L, u))
                            for t in range(QT):
                                for c in range(DC):
                                    mm = e.matmul(ps[:, 4 * s + 3, t * D:(t + 1) * D],
                                                  xnT[s][:, c, t * P:(t + 1) * P], wo[:, c, :],
                                                  start=(c == 0), stop=(c == DC - 1))
                            mm.then_inc(sig["Wo", s], 1)
                    for s in range(2):
                        e.wait_ge(sig["O", s], at("O", L, u))
                        transpose_x(s, xn2[s], 2)
                    for s in range(2):
                        e.wait_ge(sig["xnT", s], at("xnT", L, u, 2))
                        for t in range(QT):
                            for c in range(DC):
                                mm = e.matmul(ps[:, 4 * s + 1, t * E:(t + 1) * E],
                                              xnT[s][:, c, t * P:(t + 1) * P], gw[L][:, c, :],
                                              start=(c == 0), stop=(c == DC - 1))
                        mm.then_inc(sig["lg", s], 1)
                        for m in range(4):
                            for c in range(DC):
                                mm = e.matmul(ps[:, 4 * s + 2 + m // 2, m % 2 * LQ:(m % 2 + 1) * LQ],
                                              wsgu[:, c, m * P:(m + 1) * P], xnT[s][:, c, :],
                                              start=(c == 0), stop=(c == DC - 1))
                        mm.then_inc(sig["GU", s], 1)
                    for s in range(2):
                        e.wait_ge(sig["HS", s], at("HS", L, u))
                        for t in range(QT):
                            for c in range(2):
                                mm = e.matmul(ps[:, 4 * s, t * D:(t + 1) * D],
                                              W[s][:, 4 + c, t * P:(t + 1) * P], wsd[:, c, :],
                                              start=(c == 0), stop=(c == 1))
                        mm.then_inc(sig["SH", s], 1)
                    for s in range(2):
                        e.wait_ge(sig["mask", s], at("mask", L, u))
                        e.wait_ge(sig["th", s], at("th", L, u))
                        tri, one = tri16[:, 0:P], tri16[:, P:2 * P]
                        bank = ps[:, 4 * s + 1, :]
                        e.matmul(bank[:, 64:80], tri, m16[s][:, 0, :], start=True, stop=True)
                        e.matmul(bank[:, 80:96], tri, m16[s][:, 1, :], start=True, stop=False)
                        e.matmul(bank[:, 80:96], one, m16[s][:, 0, :], start=False, stop=True)
                        e.matmul(bank[:, 96:112], one, m16[s][:, 0, :], start=True, stop=False)
                        e.matmul(bank[:, 96:112], one, m16[s][:, 1, :], start=False, stop=True
                                 ).then_inc(sig["rank", s], 1)

            def expert_phase(L):
                n0, r0 = (0, 0) if L == 0 else (NT[0], NT[0] // 4)

                def early(n, k):
                    return isinstance(n, int) and n < k and L == 0

                def trans(n, r, v):
                    e.wait_ge(xl[r % 4], 16 * (r0 + v + 1))
                    if not early(n, 2):
                        e.wait_ge(eT, n0 + n - 1)
                    for c in range(DC):
                        mm = e.transpose(ps[:, r % 2, c * P:(c + 1) * P], xt[r % 4][:, c * P:(c + 1) * P], ident)
                    mm.then_inc(eT_ps, 1)

                def gate_up(n, r):
                    x = e.value_load(tab[0:1, 1, bass.ds(n, 1)], min_val=0, max_val=E - 1)
                    e.wait_ge(eT, n0 + n + 1)
                    if not early(n, 2):
                        e.wait_ge(eH, n0 + n - 1)
                    for c in range(DC):
                        mm = e.matmul(ps[:, 2 + r % 2, 0:2 * F], xtT[r % 2][:, c, :],
                                      wgu[:, bass.ds(x * (DC * 2 * F) + c * 2 * F, 2 * F)],
                                      start=(c == 0), stop=(c == DC - 1))
                    mm.then_inc(eGU, 1)

                def down(n, r):
                    x = e.value_load(tab[0:1, 1, bass.ds(n, 1)], min_val=0, max_val=E - 1)
                    e.wait_ge(eHT, n0 + n + 1)
                    if not early(n, 2):
                        e.wait_ge(eY, n0 + n - 1)
                    e.matmul(ps[:, 6 + r % 2, 0:D], hT[r % 2], wd[:, bass.ds(x * D, D)],
                             start=True, stop=True).then_inc(eD, 1)

                def trans_h(n, r):
                    e.wait_ge(eH, n0 + n + 1)
                    if not early(n, 2):
                        e.wait_ge(eHT, n0 + n - 1)
                    e.transpose(ps[:, 4 + r % 2, 0:P], hm[r % 2], ident).then_inc(eHT_ps, 1)

                def step(n, i, v):
                    peeled = isinstance(n, int)
                    if not (peeled and n >= NT[L] - 1):
                        trans(n + 1, i + 1, v if i < 3 else v + 1)
                    if not (peeled and n >= NT[L]):
                        gate_up(n, i)
                    if not (peeled and n < 2):
                        down(n - 2, i + 2)
                    if not (peeled and (n < 1 or n > NT[L])):
                        trans_h(n - 1, i + 3)

                e.wait_ge(w_exp[L], 32)
                trans(0, 0, 0)
                for n in range(4):
                    step(n, n, 0)
                with e.Fori(1, NT[L] // 4 - 1) as v:
                    for i in range(4):
                        step(v * 4 + i, i, v)
                for n in range(NT[L] - 4, NT[L] + 2):
                    step(n, n % 4, n // 4)

            for L in range(2):
                attention_phase(L)
                end_phase(e, 3 * L + 1)
                end_phase(e, 3 * L + 2)
                expert_phase(L)
                end_phase(e, 3 * L + 3)


TBN = 16
C1N = 5


def _pad_heads(w):
    t = np.zeros((D, H, HP), w.dtype)
    t[:, :, :HD] = w.T.reshape(D, H, HD)
    return _chunks(t.reshape(D, H * HP))


def _chunks(w):
    return np.ascontiguousarray(w.reshape(-1, P, w.shape[1]).transpose(1, 0, 2))


def _column(b, row):
    t = np.zeros((H, HP), np.float32)
    if b is not None:
        t[:, :HD] = b.reshape(H, HD)
    if row is not None:
        t[:, row] = 1.0
    return np.ascontiguousarray(t.reshape(HT, P).T)


def _experts(g, u, d):
    gu = np.concatenate([g, u], axis=2).reshape(E, DC, P, 2 * F).transpose(2, 0, 1, 3)
    return (np.ascontiguousarray(gu.reshape(P, -1)),
            np.ascontiguousarray(d.transpose(1, 0, 2).reshape(P, -1)))


def layout(i):
    i = {k: np.asarray(v) for k, v in i.items()}
    rows = lambda v: np.ascontiguousarray(np.broadcast_to(v[None], (P, v.shape[0])))
    r = {
        "x": np.ascontiguousarray(i["x"].reshape(B, QT, P, D).transpose(0, 2, 1, 3)),
        "ctxT": np.ascontiguousarray(i["ctx_1024"].transpose(0, 2, 1).reshape(B, DC, P, LK).transpose(0, 2, 1, 3)),
        "mask": np.ascontiguousarray(i["mask_BxS2_ik0"].reshape(1, B * LK)),
        "consts": consts(),
        "wq0": _pad_heads(i["L0_xattn_Wq"]), "wk0": _pad_heads(i["L0_xattn_Wk"]),
        "wv0": _chunks(i["L0_xattn_Wv"].T), "wo0": _chunks(i["L0_xattn_Wo"].T),
        "bo": rows(i["L0_xattn_bo"]), "bv": rows(i["L1_xattn_v_b"]), "gbias": rows(i["L0_ffn_gate_bias"]),
        "wq1": _pad_heads(i["L1_xattn_q_w"]), "wk1": _pad_heads(i["L1_xattn_k_w"]),
        "wv1": _chunks(i["L1_xattn_v_w"].T),
        "bk0": _column(None, AUG), "bk1": _column(i["L1_xattn_k_b"], AUG),
        "bq1": _column(i["L1_xattn_q_b"], MSK),
        "gw0": _chunks(i["L0_ffn_gate_w"].T), "gw1": _chunks(i["L1_ffn_Wr"]),
        "wsgu0": _chunks(np.concatenate([i["L0_ffn_Ws_g"].T, i["L0_ffn_Ws_u"].T], axis=1)),
        "wsd0": _chunks(i["L0_ffn_Ws_d"].T),
        "wsgu1": _chunks(np.concatenate([i["L1_ffn_Sg"], i["L1_ffn_Su"]], axis=1)),
        "wsd1": _chunks(i["L1_ffn_Sd"]),
    }
    r["wgu0"], r["wd0"] = _experts(i["L0_ffn_Wg"].transpose(0, 2, 1), i["L0_ffn_Wu"].transpose(0, 2, 1),
                                   i["L0_ffn_Wd"].transpose(0, 2, 1))
    r["wgu1"], r["wd1"] = _experts(i["L1_ffn_Wg"], i["L1_ffn_Wu"], i["L1_ffn_Wd"])
    return r


def kernel(**inputs):
    import concourse.bacc as bacc
    from concourse.bass_utils import run_bass_kernel_spmd as run

    nc = bacc.Bacc("TRN2", target_bir_lowering=False, num_devices=1)
    arrays = {f"in_{k}": v for k, v in layout(inputs).items()}
    a = {k[3:]: nc.dram_tensor(k, v.shape, mybir.dt.from_np(v.dtype), kind="ExternalInput").ap()
         for k, v in arrays.items()}
    out = nc.dram_tensor("out_x", (B, P, QT, D), F32, kind="ExternalOutput").ap()
    build(nc, a, out)
    r = run(nc, [arrays], core_ids=[0])
    y = r.results[0]["out_x"]
    return np.ascontiguousarray(y.transpose(0, 2, 1, 3).reshape(B, LQ, D))
```

```python
from contextlib import ExitStack

import concourse.bass as bass
import numpy as np
from concourse import mybir

ALU = mybir.AluOpType
ACT = mybir.ActivationFunctionType
AX = mybir.AxisListType
F32 = mybir.dt.float32
BF16 = mybir.dt.bfloat16
U32 = mybir.dt.uint32
I32 = mybir.dt.int32

P = 128
B, LQ, D = 32, 256, 256
LK = 120
H, HD = 16, 16
HP = 32
AUG, MSK = HD, HD + 1
QT = LQ // P
DC = D // P
G = P // HP
HT = H // G
E, F = 16, 128
NG = 4
TOPK = (4, 2)
NTOK = B * LQ
REG = NTOK + P
NT = tuple(NTOK * k // P + E for k in TOPK)
NTMAX = 3 * P
XROWS = E * REG + E * P
SCALE = HD ** -0.5
EPS = 1e-5
BIG = 1e30
ROUTED_SCALE = 2.5
NIT = B // 2

C_ID, C_TRI, C_ONE, C_MJ = 0, P, 2 * P, 3 * P
C_IOTA = C_MJ + G * LK
C_EBASE = C_IOTA + E
C_LOW = C_EBASE + E
C_J128 = C_LOW + E * E
C_T = C_J128 + 64
C_MH = C_T + 3
C_SEL = C_MH + 2
NCONST = C_SEL + P

PER = {
    "ld": (32, 48), "ga": (0, 128), "var": (2, 2), "rstd": (2, 2), "xn": (2, 2), "xnT_ps": (2, 2),
    "xnT": (2, 2), "K_ps": (1, 1), "V_ps": (1, 1), "Q_ps": (1, 1), "KB": (1, 1), "V": (1, 1),
    "Q": (1, 1), "S": (2, 2), "smax": (2, 2), "MT": (1, 1), "Qa": (1, 1), "ST": (4, 4),
    "Pr": (4, 4), "OT_ps": (1, 1), "OT": (1, 1), "O_ps": (1, 1), "O": (1, 1), "OnT_ps": (1, 0),
    "OnT": (1, 0), "Wo": (1, 0), "xb": (1, 0), "x1": (1, 0), "lg": (1, 1), "GU": (1, 1),
    "nm": (0, 1), "th": (1, 1), "TH": (1, 1), "HS": (1, 1), "SH": (1, 1), "base": (1, 1),
    "st": (16, 16), "mask": (1, 1), "rank": (1, 1), "slots": (1, 1), "sc": (128, 64),
    "yslot": (0, 1), "c_ln": (3, 11), "c_at": (6, 7), "c_rt": (26, 13),
}


ORDER = {
    "SP": (("load", "n"), ("store", "b")),
    "Pool": (("rstd2", "b"), ("rstd1", "n"), ("xb", "n"), ("gather", "n"), ("scatter", "b")),
    "ACT": (("OT", "b"), ("xnT1", "a"), ("Q", "a"), ("OnT", "b"), ("xnT2", "b"), ("gates", "b"),
            ("exp", "a")),
    "DVE": (("out", "b"), ("KV", "a"), ("max0", "a"), ("x1", "b"), ("xn2", "b"), ("max1", "a"),
            ("Qa", "a"), ("nm", "b"), ("HS", "b"), ("ln1", "n"), ("route", "b"), ("xn1", "n"),
            ("base", "b"), ("place", "b")),
    "PE": (("PV", "b"), ("T1", "a"), ("OX", "b"), ("KVQ", "a"), ("OT2", "b"), ("S0", "a"), ("Wo", "b"),
           ("S1", "a"), ("T2", "b"), ("MT", "a"), ("GU", "b"), ("ST", "a"), ("SH", "b"), ("rank", "b")),
}


def run_halves(e, engine, stages):
    def half(u, s, first=False, last=False):
        v = u if s == 1 else u - 1
        for name, role in ORDER[engine]:
            if name not in stages:
                continue
            if role == "a" and not last:
                stages[name](u, s)
            if role == "b" and not first:
                stages[name](v, 1 - s)
            if role == "n" and not last and not (isinstance(v, int) and v == NIT - 1):
                stages[name](v + 1, 1 - s)

    half(0, 0, first=True)
    with e.Fori(0, NIT - 1) as u:
        half(u, 1)
        half(u + 1, 0)
    half(NIT - 1, 1)
    half(NIT, 0, last=True)


def consts():
    c = np.zeros((P, NCONST), np.float32)
    c[:, C_ID:C_ID + P] = np.eye(P)
    c[:, C_TRI:C_TRI + P] = np.triu(np.ones((P, P)), 1)
    c[:, C_ONE:C_ONE + P] = 1.0
    for j in range(G):
        c[j * HP:(j + 1) * HP, C_MJ + j * LK:C_MJ + (j + 1) * LK] = 1.0
    c[:, C_IOTA:C_IOTA + E] = np.arange(E)
    c[:, C_EBASE:C_EBASE + E] = np.arange(E) * REG
    c[:, C_LOW:C_LOW + E * E] = np.tril(np.ones((E, E))).reshape(-1)
    c[:, C_J128:C_J128 + 64] = np.arange(64) * P
    c[:, C_T:C_T + 3] = np.arange(3)[None] * P + np.arange(P)[:, None]
    c[:, C_MH:C_MH + 2] = -0.5
    c[0, C_SEL:C_SEL + P] = np.arange(P) % HP == MSK
    return c


def bc(ap, axis, n):
    a = ap.unsqueeze(axis)
    shape = list(a.shape)
    shape[axis] = n
    return a.broadcast_to(shape)


def build(nc, a, out):
    ctx = ExitStack()

    def sb(name, shape, dt=F32):
        return ctx.enter_context(nc.sbuf_tensor(name, shape, dt))

    def sem(name):
        return ctx.enter_context(nc.semaphore(name))

    with ctx:
        ps = ctx.enter_context(nc.psum_tensor("ps", [P, 8, 512], F32))
        xsort = nc.dram_tensor("xsort", [XROWS, D], F32).ap()
        ysort = nc.dram_tensor("ysort", [NT[0] * P, D], F32).ap()
        based = nc.dram_tensor("based", [B, P, QT, D], F32).ap()
        mrowd = nc.dram_tensor("mrowd", [B, LK], F32).ap()
        tabd = [nc.dram_tensor(f"tabd{L}", [2, NTMAX], I32).ap() for L in range(2)]
        cntd = [nc.dram_tensor(f"cntd{L}", [1, E], I32).ap() for L in range(2)]

        cst = sb("cst", [P, NCONST])
        tri16 = sb("tri16", [P, 2 * P], BF16)
        gw = [sb(f"gw{L}", [P, DC, E]) for L in range(2)]
        gbias = sb("gbias", [P, E])
        bo_bc = sb("bo_bc", [P, D])
        bv_bc = sb("bv_bc", [P, D])
        bq = [sb(f"bq{L}", [P, HT]) for L in range(2)]
        bk = [sb(f"bk{L}", [P, HT]) for L in range(2)]
        wq = sb("wq", [P, DC, HT * P])
        wk = sb("wk", [P, DC, HT * P])
        wv = sb("wv", [P, DC, D])
        wo = sb("wo", [P, DC, D])
        wsgu = sb("wsgu", [P, DC, 512])
        wsd = sb("wsd", [P, DC, D])
        wgu = sb("wgu", [P, E * DC * 2 * F])
        wd = sb("wd", [P, E * D])
        mrow = [sb(f"mrow{s}", [1, LK]) for s in range(2)]
        mask_i, mask_f = sb("mask_i", [B, LK], I32), sb("mask_f", [B, LK])
        zero = sb("zero", [P, D])
        meta = sb("meta", [P, B + 2, 3, QT * 4])
        cnt = sb("cnt", [P, E])
        delta = sb("delta", [P, E])

        X = [sb(f"X{s}", [P, QT, D]) for s in range(2)]
        XL = [sb(f"XL{s}", [P, QT, D]) for s in range(2)]
        XO = [sb(f"XO{s}", [P, QT, D]) for s in range(2)]
        ctxT = [sb(f"ctxT{s}", [P, DC, LK]) for s in range(2)]
        xn2 = [sb(f"xn2{s}", [P, QT, D]) for s in range(2)]
        xnT = [sb(f"xnT{s}", [P, DC, LQ]) for s in range(2)]
        Q = [sb(f"Q{s}", [P, HT, LQ]) for s in range(2)]
        KB = [sb(f"KB{s}", [P, HT, G, LK]) for s in range(2)]
        V = [sb(f"V{s}", [LK, H, HP]) for s in range(2)]
        W = [sb(f"W{s}", [P, H, LQ]) for s in range(2)]
        O = [sb(f"O{s}", [P, QT, D]) for s in range(2)]
        xn = O
        Mp = [sb(f"Mp{s}", [P, QT, HT, G, HP]) for s in range(2)]
        ygath = [sb(f"ygath{s}", [P, QT * 4, D]) for s in range(2)]
        xb = [ygath[s][:, 0:QT, :] for s in range(2)]
        yidx = [sb(f"yidx{s}", [P, QT * 4], U32) for s in range(2)]
        xidx = [sb(f"xidx{s}", [P, QT * 4], U32) for s in range(2)]
        st6 = [sb(f"st6{s}", [P, QT, 6]) for s in range(2)]
        mv = [sb(f"mv{s}", [P, QT, 2]) for s in range(2)]
        ve = [sb(f"ve{s}", [P, QT]) for s in range(2)]
        rstd = [sb(f"rstd{s}", [P, QT]) for s in range(2)]
        nmr = [sb(f"nmr{s}", [P, QT]) for s in range(2)]
        rsum = [sb(f"rsum{s}", [P, QT, H]) for s in range(2)]
        th = [sb(f"th{s}", [P, QT, E]) for s in range(2)]
        rt = [sb(f"rt{s}", [P, 640]) for s in range(2)]
        ru = [sb(f"ru{s}", [P, QT, 8], U32) for s in range(2)]
        m16 = [sb(f"m16{s}", [P, QT, E], BF16) for s in range(2)]
        mt = [sb(f"mt{s}", [P, 3, QT * 4]) for s in range(2)]
        mg = [sb(f"mg{s}", [P, 3, QT * 4]) for s in range(2)]

        xt = [ygath[0][:, r, :] for r in range(4)]
        xtT = [ygath[1][:, r, :].rearrange("p (c q) -> p c q", c=DC) for r in range(2)]
        hg = [ygath[1][:, 2 + r, 0:F] for r in range(2)]
        hm = [ygath[1][:, 4 + r, 0:F] for r in range(2)]
        hT = [ygath[1][:, 6 + r, 0:P] for r in range(2)]
        yt = [ygath[0][:, 4 + r, :] for r in range(4)]
        tb = sb("tb", [P, 160])
        tbo = sb("tbo", [P, 2, 3], I32)
        cnti = sb("cnti", [P, E], I32)
        tab = sb("tab", [1, 2, NTMAX], I32)
        cntr = sb("cntr", [1, E], I32)

        sig = {(n, s): sem(f"{n}{s}") for n in PER for s in range(2)}
        w_small = sem("w_small")
        w_small1 = sem("w_small1")
        w_exp = [sem("w_exp0"), sem("w_exp1")]
        init = sem("init")
        phase = sem("phase")
        zfill = sem("zfill")
        zero_ok = sem("zero_ok")
        cnt_s = sem("cnt_s")
        tb_s = sem("tb_s")
        tb_st, tb_ld = sem("tb_st"), sem("tb_ld")
        xl = [sem(f"xl{r}") for r in range(4)]
        yst = [sem(f"yst{r}") for r in range(4)]
        eT_ps, eT, eGU, eG, eH = sem("eT_ps"), sem("eT"), sem("eGU"), sem("eG"), sem("eH")
        eHT_ps, eHT, eD, eY = sem("eHT_ps"), sem("eHT"), sem("eD"), sem("eY")
        fin = [sem("fin0"), sem("fin1")]
        mrow_st = sem("mrow_st")
        yfirst = sem("yfirst")
        f_slot, f_ga, f_c, f_ld, f_st = ([sem(f"{n}{s}") for s in range(2)]
                                         for n in ("f_slot", "f_ga", "f_c", "f_ld", "f_st"))

        def at(n, L, u, k=None):
            per = PER[n][L]
            return (NIT * PER[n][0] if L else 0) + per * u + (per if k is None else k)

        def first(L, u):
            return L == 0 and isinstance(u, int) and u == 0

        def end_phase(e, n):
            e.drain().then_inc(phase, 1)
            e.wait_ge(phase, 5 * n)

        def cc(o, n, rows=P):
            return cst[0:rows, o:o + n]

        def apart(e):
            e.nop(nofuse=True)

        ident = cc(C_ID, P)
        NSMALL = 16 * 16
        NSMALL1 = 16 * 5

        def run_steps(e, lo, hi, fn):
            for n in range(lo, 4):
                fn(n, n)
            with e.Fori(1, hi // 4 - 1) as v:
                for i in range(4):
                    fn(v * 4 + i, i)
            for n in range(hi // 4 * 4 - 4, hi // 4 * 4):
                fn(n, n)

        block = ctx.enter_context(nc.Block())

        @block.sync
        def _(e):
            def load_small(pairs, s_):
                for dst, src in pairs:
                    e.dma_start(dst, src).then_inc(s_, 16)

            def load_exp(L):
                e.dma_start(wgu[:], a[f"wgu{L}"]).then_inc(w_exp[L], 16)
                e.dma_start(wd[:], a[f"wd{L}"]).then_inc(w_exp[L], 16)

            load_small([
                (cst[:], a["consts"]), (wk[:], a["wk0"]), (wq[:], a["wq0"]), (wv[:], a["wv0"]),
                (wo[:], a["wo0"]), (wsgu[:], a["wsgu0"]), (wsd[:], a["wsd0"]),
                (gw[0][:], a["gw0"]), (gw[1][:], a["gw1"]), (gbias[:], a["gbias"]),
                (bo_bc[:], a["bo"]), (bv_bc[:], a["bv"]), (bq[1][:], a["bq1"]),
                (bk[1][:], a["bk1"]), (bk[0][:], a["bk0"]), (mask_i[:], a["mask"]),
            ], w_small)

            def attention_phase(L):
                def wait(n, s, v):
                    e.wait_ge(sig[n, s], v)
                    apart(e)

                def load(u, s):
                    b = u * 2 + s
                    wait("xn", s, at("xn", L, u, 0))
                    wait("xb" if L == 0 else "O", s, at("xb" if L == 0 else "O", L, u, 0))
                    wait("V_ps", s, at("V_ps", L, u, 0))
                    src = a["x"] if L == 0 else based
                    e.dma_start(XL[s][:], src[bass.ds(b, 1)].rearrange("o p t d -> (o p) t d")
                                ).then_inc(sig["ld", s], 16)
                    e.dma_start(ctxT[s][:], a["ctxT"][bass.ds(b, 1)].rearrange("o p c k -> (o p) c k")
                                ).then_inc(sig["ld", s], 16)
                    if L == 1:
                        e.dma_start(mrow[s][:], mrowd[bass.ds(b, 1), :]).then_inc(sig["ld", s], 16)

                def store(u, s):
                    wait("base", s, at("base", L, u))
                    e.dma_start(based[bass.ds(u * 2 + s, 1)].rearrange("o p t d -> (o p) t d"), XO[s][:]
                                ).then_inc(sig["st", s], 16)

                load(0, 0)
                run_halves(e, "SP", {"load": load, "store": store})
                for s in range(2):
                    e.wait_ge(sig["st", s], at("st", L, NIT - 1))

            def tables(L):
                e.wait_ge(tb_s, TBN * L + TBN)
                e.dma_start(cntd[L], cnti[0:1, :]).then_inc(tb_st, 16)
                for k in range(2):
                    for c in range(3):
                        e.dma_start(tabd[L][k:k + 1, c * P:(c + 1) * P].rearrange("o p -> p o"),
                                    tbo[:, k, c:c + 1]).then_inc(tb_st, 16)
                e.wait_ge(tb_st, 16 * 7 * (L + 1))
                e.dma_start(cntr[:], cntd[L]).then_inc(tb_ld, 16)
                e.dma_start(tab[:], tabd[L]).then_inc(tb_ld, 16)
                e.wait_ge(tb_ld, 32 * (L + 1))
                with e.Fori(0, E) as x:
                    c = e.value_load(cntr[0:1, bass.ds(x, 1)], min_val=0, max_val=NTOK)
                    e.dma_start(xsort[bass.ds(c + x * REG, P), :], zero[:]).then_inc(zfill, 16)
                e.wait_ge(zfill, 16 * E + 16 * E * (L + 1))

            def expert_phase(L):
                n0, r0 = (0, 0) if L == 0 else (NT[0], NT[0] // 4)

                def load(n, r):
                    if not (isinstance(n, int) and n < 4 and L == 0):
                        e.wait_ge(eT_ps, n0 + n - 3)
                        apart(e)
                    row = e.value_load(tab[0:1, 0, bass.ds(n, 1)], min_val=0, max_val=XROWS - P)
                    e.dma_start(xt[r], xsort[bass.ds(row, P), :]).then_inc(xl[r], 16)

                def store(n, r):
                    e.wait_ge(eY, n0 + n + 1)
                    apart(e)
                    e.dma_start(ysort[bass.ds(n * P, P), :], yt[r]).then_inc(yst[r], 16)

                for n in range(4):
                    load(n, n)
                with e.Fori(0, NT[L] // 4 - 1) as v:
                    for r in range(4):
                        load(v * 4 + r + 4, r)
                        store(v * 4 + r, r)
                for r in range(4):
                    store(NT[L] - 4 + r, r)
                for r in range(4):
                    e.wait_ge(yst[r], 16 * (r0 + NT[L] // 4))

            e.wait_ge(zero_ok, 1)
            for n in range(E):
                e.dma_start(xsort[E * REG + n * P:E * REG + (n + 1) * P, :], zero[:]).then_inc(zfill, 16)
            load_exp(0)
            e.wait_ge(init, 5)
            e.dma_start(mrowd, mask_f[:]).then_inc(mrow_st, 16)
            e.wait_ge(mrow_st, 16)
            attention_phase(0)
            end_phase(e, 1)
            load_small([(wk[:], a["wk1"]), (wq[:], a["wq1"]), (wv[:], a["wv1"]),
                        (wsgu[:], a["wsgu1"]), (wsd[:], a["wsd1"])], w_small1)
            tables(0)
            end_phase(e, 2)
            expert_phase(0)
            end_phase(e, 3)
            load_exp(1)
            attention_phase(1)
            end_phase(e, 4)
            tables(1)
            end_phase(e, 5)
            expert_phase(1)
            end_phase(e, 6)
            with e.Fori(0, NIT) as u:
                for s in range(2):
                    e.wait_ge(f_st[s], u * 16)
                    apart(e)
                    e.dma_start(X[s][:], based[bass.ds(u * 2 + s, 1)].rearrange("o p t d -> (o p) t d")
                                ).then_inc(f_ld[s], 16)
                for s in range(2):
                    e.wait_ge(fin[s], u + 1)
                    apart(e)
                    e.dma_start(out[bass.ds(u * 2 + s, 1)].rearrange("o p t d -> (o p) t d"), X[s][:]
                                ).then_inc(f_st[s], 16)
            for s in range(2):
                e.wait_ge(f_st[s], NIT * 16)

        @block.gpsimd
        def _(e):
            e.memset(zero[:], 0.0).then_inc(zero_ok, 1)
            for s in range(2):
                e.memset(Mp[s][:], 0.0).then_inc(init, 1)
                e.memset(V[s][:], 0.0)
                e.wait_ge(init, s + 1)
            e.memset(meta[:], 0.0).then_inc(init, 1)
            e.wait_ge(w_small, NSMALL)

            def scatter(L, s):
                for t in range(QT):
                    for k in range(TOPK[L]):
                        e.indirect_dma_start(
                            out=xsort, in_=xn2[s][:, t, :], in_offset=None,
                            out_offset=bass.IndirectOffsetOnAxis(
                                ap=xidx[s][:, t * 4 + k:t * 4 + k + 1], axis=0),
                        ).then_inc(sig["sc", s], 16)

            def gather(L, s, signal):
                for t in range(QT):
                    for k in range(TOPK[L]):
                        e.indirect_dma_start(
                            out=ygath[s][:, t * 4 + k, :], out_offset=None, in_=ysort,
                            in_offset=bass.IndirectOffsetOnAxis(
                                ap=yidx[s][:, t * 4 + k:t * 4 + k + 1], axis=0),
                        ).then_inc(signal, 16)

            def attention_phase(L):
                def rstds(u, s, k):
                    e.wait_ge(sig["var", s], at("var", L, u, k))
                    e.tensor_tensor(rstd[s][:], ve[s][:], cc(C_MH, 2), ALU.pow).then_inc(sig["rstd", s], 1)

                def add_bo(u, s):
                    e.wait_ge(sig["ld", s], at("ld", L, u))
                    e.wait_ge(sig["x1", s], at("x1", L, u, 0))
                    e.tensor_tensor(xb[s], XL[s][:], bc(bo_bc[:], 1, QT), ALU.add
                                    ).then_inc(sig["xb", s], 1)

                def scatter_rows(u, s):
                    e.wait_ge(sig["slots", s], at("slots", L, u))
                    apart(e)
                    scatter(L, s)

                def gather_rows(u, s):
                    e.wait_ge(sig["yslot", s], at("yslot", L, u + 1))
                    apart(e)
                    gather(0, s, sig["ga", s])

                stages = {"rstd1": lambda u, s: rstds(u, s, 1), "rstd2": lambda u, s: rstds(u, s, 2),
                          "scatter": scatter_rows}
                stages.update({"xb": add_bo} if L == 0 else {"gather": gather_rows})
                if L == 1:
                    for s in range(2):
                        gather_rows(-1, s)
                rstds(0, 0, 1)
                if L == 0:
                    add_bo(0, 0)
                else:
                    gather_rows(0, 0)
                run_halves(e, "Pool", stages)
                for s in range(2):
                    e.wait_ge(sig["sc", s], at("sc", L, NIT - 1))
                    if L == 1:
                        e.wait_ge(sig["ga", s], at("ga", L, NIT))

            for L in range(2):
                attention_phase(L)
                for k in range(3):
                    end_phase(e, 3 * L + 1 + k)
            with e.Fori(0, NIT) as u:
                for s in range(2):
                    e.wait_ge(f_slot[s], u + 1)
                    apart(e)
                    gather(1, s, f_ga[s])

        @block.scalar
        def _(e):
            def attention_phase(L):
                e.wait_ge(w_small, NSMALL)

                def copy_xnT(u, s, k):
                    e.wait_ge(sig["xnT_ps", s], at("xnT_ps", L, u, k))
                    e.activation(xnT[s][:], ps[:, 4 * s, :].rearrange("p (c q) -> p c q", c=DC),
                                 ACT.Copy).then_inc(sig["xnT", s], 1)

                def queries(u, s):
                    e.wait_ge(sig["Q_ps", s], at("Q_ps", L, u))
                    if L == 0:
                        e.activation(Q[s][:], ps[:, 4 * s + 1:4 * s + 3, :].rearrange(
                            "p k (i q) -> p (k i) q", i=2), ACT.Copy).then_inc(sig["Q", s], 1)
                    else:
                        for i in range(HT):
                            ins = e.activation(
                                Q[s][:, i, :], ps[:, 4 * s + 1 + i // 2, i % 2 * LQ:(i % 2 + 1) * LQ],
                                ACT.Identity, bias=bq[L][:, i:i + 1])
                        ins.then_inc(sig["Q", s], 1)

                def exps(u, s):
                    for i in range(HT):
                        bank = 4 * s + (2 if i % 2 == 0 else 0)
                        e.wait_ge(sig["ST", s], at("ST", L, u, i + 1))
                        e.activation(
                            W[s][0:LK, G * i:G * (i + 1), :],
                            ps[0:LK, bank:bank + 2, :].rearrange("p k (h q) -> p (k h) q", h=2),
                            ACT.Exp, scale=SCALE).then_inc(sig["Pr", s], 1)

                def outputs_T(u, s):
                    e.wait_ge(sig["OT_ps", s], at("OT_ps", L, u))
                    e.activation(Q[s][:], ps[:, 4 * s + 2:4 * s + 4, :].rearrange(
                        "p k (i q) -> p (k i) q", i=2), ACT.Copy).then_inc(sig["OT", s], 1)

                def outputs_nT(u, s):
                    e.wait_ge(sig["OnT_ps", s], at("OnT_ps", L, u))
                    e.activation(xnT[s][:], ps[:, 4 * s + 2, :].rearrange(
                        "p (c q) -> p c q", c=DC), ACT.Copy).then_inc(sig["OnT", s], 1)

                def gates(u, s):
                    lg = ps[:, 4 * s + 1, 0:QT * E].rearrange("p (t e) -> p t e", t=QT)
                    if L == 0:
                        e.wait_ge(sig["lg", s], at("lg", L, u))
                        e.activation(th[s][:], lg, ACT.Tanh, scale=0.5).then_inc(sig["th", s], 1)
                    e.wait_ge(sig["GU", s], at("GU", L, u))
                    e.activation(W[s][:, 0:2, :], ps[:, 4 * s + 2, :].rearrange(
                        "p (c q) -> p c q", c=2), ACT.Tanh, scale=0.5).then_inc(sig["TH", s], 1)
                    if L == 1:
                        e.wait_ge(sig["nm", s], at("nm", L, u))
                        for t in range(QT):
                            ins = e.activation(th[s][:, t, :], lg[:, t, :], ACT.Exp,
                                               bias=rt[s][:, t:t + 1])
                        ins.then_inc(sig["th", s], 1)

                stages = {"OT": outputs_T, "xnT1": lambda u, s: copy_xnT(u, s, 1), "Q": queries,
                          "xnT2": lambda u, s: copy_xnT(u, s, 2), "gates": gates, "exp": exps}
                if L == 0:
                    stages["OnT"] = outputs_nT
                run_halves(e, "ACT", stages)

            def expert_phase(L):
                n0 = 0 if L == 0 else NT[0]

                def copy_x(n, r):
                    e.wait_ge(eT_ps, n0 + n + 1)
                    if not (isinstance(n, int) and n < 2 and L == 0):
                        e.wait_ge(eGU, n0 + n - 1)
                    e.activation(xtT[r % 2], ps[:, r % 2, 0:D].rearrange("p (c q) -> p c q", c=DC),
                                 ACT.Copy).then_inc(eT, 1)

                def gate(n, r):
                    e.wait_ge(eGU, n0 + n + 1)
                    if not (isinstance(n, int) and n < 2 and L == 0):
                        e.wait_ge(eH, n0 + n - 1)
                    e.activation(hg[r % 2], ps[:, 2 + r % 2, 0:F], ACT.Silu).then_inc(eG, 1)

                def step(n, r):
                    if not (isinstance(n, int) and n == NT[L] - 1):
                        copy_x(n + 1, r + 1)
                    gate(n, r)

                copy_x(0, 0)
                run_steps(e, 0, NT[L], step)

            for L in range(2):
                attention_phase(L)
                end_phase(e, 3 * L + 1)
                end_phase(e, 3 * L + 2)
                expert_phase(L)
                end_phase(e, 3 * L + 3)

        @block.vector
        def _(e):
            count = {}
            yfirst_n = []

            def link(ins, c, s, L, u):
                k = count[c, s] = count.get((c, s), 0) + 1
                ins.then_inc(sig[c, s], 1)
                e.wait_ge(sig[c, s], at(c, L, u, k))

            def link_apart(ins, c, s, L, u):
                link(ins, c, s, L, u)
                apart(e)

            for s in range(2):
                e.memset(rt[s][:], -BIG)
            e.memset(cnt[:], 0.0)
            e.wait_ge(init, 3)
            for s in range(2):
                e.memset(V[s][:, :, HD:HD + 1], 1.0)
            e.wait_ge(w_small, NSMALL)
            e.tensor_copy(tri16[:], cc(C_TRI, 2 * P)).then_inc(init, 1)
            e.tensor_scalar(mask_f[:], mask_i[:], 0.0, -BIG, ALU.is_gt, ALU.mult).then_inc(init, 1)

            def yslots_chain(s, lk, b, K, signal):
                oh = rt[s][:, 256:256 + QT * 4 * E].rearrange("p (k e) -> p k e", e=E)
                lk(e.tensor_copy(mg[s][:], meta[:, bass.ds(b, 1)].rearrange("p o k t -> p (o k) t")))
                lk(e.tensor_tensor(oh, bc(mg[s][:, 2, :], 2, E), bc(cc(C_IOTA, E), 1, QT * 4), ALU.is_equal))
                lk(e.tensor_tensor(oh, oh, bc(delta[:], 1, QT * 4), ALU.mult))
                lk(e.tensor_reduce(mt[s][:, 0, :], oh, AX.X, ALU.add))
                e.tensor_tensor(yidx[s][:], mt[s][:, 0, :], mg[s][:, 1, :], ALU.add).then_inc(signal, 1)

            def combine(s, acc, lk, K):
                for k in range(K):
                    for t in range(QT):
                        c = t * 4 + k
                        ins = e.scalar_tensor_tensor(out=acc[s][:, t, :], in0=ygath[s][:, c, :],
                                                     scalar=mg[s][:, 0, c:c + 1], in1=acc[s][:, t, :],
                                                     op0=ALU.mult, op1=ALU.add)
                        if t == QT - 1 and k < K - 1:
                            lk(ins)
                return ins

            def attention_phase(L):
                def stats(c, u, s, x):
                    for t in range(QT):
                        ins = e.bn_stats(st6[s][:, t, :], x[s][:, t, :])
                    link_apart(ins, c, s, L, u)
                    for t in range(QT):
                        ins = e.bn_aggr(mv[s][:, t, :], st6[s][:, t, :])
                    link(ins, c, s, L, u)
                    e.tensor_scalar(ve[s][:], mv[s][:, :, 1], EPS, None, ALU.add
                                    ).then_inc(sig["var", s], 1)

                def norm(c, u, s, x, dst, k):
                    e.wait_ge(sig["rstd", s], at("rstd", L, u, k))
                    link(e.scalar_tensor_tensor(out=nmr[s][:], in0=mv[s][:, :, 0], scalar=-1.0,
                                                in1=rstd[s][:], op0=ALU.mult, op1=ALU.mult), c, s, L, u)
                    for t in range(QT):
                        ins = e.tensor_scalar(dst[:, t, :], x[s][:, t, :], rstd[s][:, t:t + 1],
                                              nmr[s][:, t:t + 1], ALU.mult, ALU.add)
                    ins.then_inc(sig["xn", s], 1)

                def ln1(u, s):
                    count["c_ln", s] = 0
                    lk = lambda i: link(i, "c_ln", s, L, u)
                    e.wait_ge(sig["ld", s], at("ld", L, u))
                    if L == 1:
                        e.wait_ge(sig["ga", s], at("ga", L, u))
                        lk(combine(s, XL, lk, TOPK[0]))
                    stats("c_ln", u, s, XL)
                    if L == 1:
                        yslots_chain(s, lk, (u + 1) * 2 + s, TOPK[0], sig["yslot", s])

                def xn1(u, s):
                    norm("c_ln", u, s, XL, xn[s], 1)
                    assert count["c_ln", s] == PER["c_ln"][L], count

                def keys_values(u, s):
                    e.wait_ge(sig["K_ps", s], at("K_ps", L, u))
                    for i in range(HT):
                        ins = e.scalar_tensor_tensor(
                            out=KB[s][:, i, :, :], in0=bc(ps[:, 4 * s + 3, i * LK:(i + 1) * LK], 1, G),
                            scalar=bk[L][:, i:i + 1],
                            in1=cc(C_MJ, G * LK).rearrange("p (j k) -> p j k", j=G),
                            op0=ALU.add, op1=ALU.mult)
                    ins.then_inc(sig["KB", s], 1)
                    e.wait_ge(sig["V_ps", s], at("V_ps", L, u))
                    v_ps = ps[0:LK, 4 * s, 0:D].rearrange("p (h c) -> p h c", h=H)
                    if L == 0:
                        ins = e.tensor_copy(V[s][:, :, 0:HD], v_ps)
                    else:
                        ins = e.tensor_tensor(V[s][:, :, 0:HD], v_ps,
                                              bv_bc[0:LK, :].rearrange("p (h c) -> p h c", h=H), ALU.add)
                    ins.then_inc(sig["V", s], 1)

                def maxima(u, s, t):
                    e.wait_ge(sig["S", s], at("S", L, u, t + 1))
                    e.tensor_reduce(
                        Mp[s][:, t, :, :, AUG],
                        ps[:, 4 * s:4 * s + 4, 0:G * LK].rearrange("p k (j c) -> p k j c", j=G),
                        AX.X, ALU.max).then_inc(sig["smax", s], 1)

                def shift(u, s):
                    e.wait_ge(sig["MT", s], at("MT", L, u))
                    e.tensor_tensor(Q[s][:], Q[s][:], ps[:, 4 * s:4 * s + 2, :].rearrange(
                        "p k (i q) -> p (k i) q", i=2), ALU.subtract).then_inc(sig["Qa", s], 1)

                def outputs(u, s):
                    count["c_at", s] = 0
                    e.wait_ge(sig["O_ps", s], at("O_ps", L, u))
                    o_ps = ps[:, 4 * s:4 * s + 2, :].rearrange("p t (h c) -> p t h c", c=HP)
                    link(e.reciprocal(rsum[s][:], o_ps[:, :, :, AUG]), "c_at", s, L, u)
                    o = O[s][:].rearrange("p t (h c) -> p t h c", c=HD)
                    ins = e.tensor_tensor(o, o_ps[:, :, :, 0:HD], bc(rsum[s][:], 3, HD), ALU.mult)
                    if L == 0:
                        ins.then_inc(sig["O", s], 1)
                    else:
                        link(ins, "c_at", s, L, u)
                        e.tensor_tensor(X[s][:], XL[s][:], O[s][:], ALU.add).then_inc(sig["O", s], 1)

                def x1(u, s):
                    if L == 0:
                        e.wait_ge(sig["Wo", s], at("Wo", L, u))
                        e.wait_ge(sig["xb", s], at("xb", L, u))
                        e.tensor_tensor(X[s][:], ps[:, 4 * s + 3, :].rearrange("p (t d) -> p t d", t=QT),
                                        xb[s], ALU.add).then_inc(sig["x1", s], 1)
                        e.wait_ge(sig["x1", s], at("x1", L, u))
                    else:
                        e.wait_ge(sig["O", s], at("O", L, u))
                    stats("c_at", u, s, X)

                def xn2s(u, s):
                    e.wait_ge(sig["sc", s], at("sc", L, u, 0))
                    norm("c_at", u, s, X, xn2[s], 2)

                def greatest_logit(u, s):
                    e.wait_ge(sig["lg", s], at("lg", L, u))
                    apart(e)
                    for t in range(QT):
                        ins = e.max(rt[s][:, 16 + 8 * t:24 + 8 * t], ps[:, 4 * s + 1, t * E:(t + 1) * E])
                    link(ins, "c_at", s, L, u)
                    e.tensor_scalar(rt[s][:, 0:2],
                                    rt[s][:, 16:32].rearrange("p (t m) -> p t m", t=2)[:, :, 0],
                                    -1.0, None, ALU.mult).then_inc(sig["nm", s], 1)

                def hidden(u, s):
                    e.wait_ge(sig["TH", s], at("TH", L, u))
                    g_ps = ps[:, 4 * s + 2, :].rearrange("p (c q) -> p c q", c=2)
                    u_ps = ps[:, 4 * s + 3, :].rearrange("p (c q) -> p c q", c=2)
                    link(e.scalar_tensor_tensor(out=W[s][:, 2:4, :], in0=W[s][:, 0:2, :], scalar=1.0,
                                                in1=g_ps, op0=ALU.add, op1=ALU.mult), "c_at", s, L, u)
                    e.scalar_tensor_tensor(out=W[s][:, 4:6, :], in0=W[s][:, 2:4, :], scalar=0.5,
                                           in1=u_ps, op0=ALU.mult, op1=ALU.mult
                                           ).then_inc(sig["HS", s], 1)

                def base(u, s):
                    e.wait_ge(sig["SH", s], at("SH", L, u))
                    e.wait_ge(sig["st", s], at("st", L, u, 0))
                    sh = ps[:, 4 * s, :].rearrange("p (t d) -> p t d", t=QT)
                    if L == 0:
                        link(e.tensor_tensor(XO[s][:], sh, X[s][:], ALU.add), "c_at", s, L, u)
                        e.tensor_tensor(XO[s][:], XO[s][:], xn2[s][:], ALU.add).then_inc(sig["base", s], 1)
                    else:
                        e.tensor_tensor(XO[s][:], sh, X[s][:], ALU.add).then_inc(sig["base", s], 1)
                    assert count["c_at", s] == PER["c_at"][L], count

                def router(u, s):
                    count["c_rt", s] = 0
                    e.wait_ge(sig["th", s], at("th", L, u))
                    route(L, u, s)

                def place(u, s):
                    place_rows(L, u, s)
                    assert count["c_rt", s] == PER["c_rt"][L], count

                stages = {
                    "out": outputs, "KV": keys_values, "max0": lambda u, s: maxima(u, s, 0), "x1": x1,
                    "xn2": xn2s, "max1": lambda u, s: maxima(u, s, 1), "Qa": shift, "HS": hidden,
                    "ln1": ln1, "route": router, "xn1": xn1, "base": base, "place": place,
                }
                if L == 1:
                    stages["nm"] = greatest_logit
                    for s in range(2):
                        yslots_chain(s, lambda i: (i.then_inc(yfirst, 1), e.wait_ge(
                            yfirst, yfirst_n.append(0) or len(yfirst_n))), s, TOPK[0], sig["yslot", s])
                ln1(0, 0)
                xn1(0, 0)
                run_halves(e, "DVE", stages)

            def route(L, u, s):
                K = TOPK[L]
                r = rt[s]
                lk = lambda i: link(i, "c_rt", s, L, u)
                lka = lambda i: link_apart(i, "c_rt", s, L, u)
                tv = r[:, 32:48].rearrange("p (t m) -> p t m", t=QT)
                oh = r[:, 256:256 + QT * 4 * E].rearrange("p (t k e) -> p t k e", t=QT, k=4)[:, :, 0:K, :]
                tmp = r[:, 384:384 + QT * 4 * E].rearrange("p (t k e) -> p t k e", t=QT, k=4)[:, :, 0:K, :]
                wk_, sk_, ek_ = (mt[s][:, i, :].rearrange("p (t k) -> p t k", t=QT)[:, :, 0:K] for i in range(3))
                iota = cc(C_IOTA, E)
                if L == 0:
                    sc = r[:, 48:80].rearrange("p (t e) -> p t e", t=QT)
                    sfc = r[:, 80:112].rearrange("p (t e) -> p t e", t=QT)
                    lk(e.tensor_scalar(sc, th[s][:], 0.5, 0.5, ALU.mult, ALU.add))
                    lk(e.tensor_tensor(sfc, sc, bc(gbias[:], 1, QT), ALU.add))
                    g4 = r[:, 80:112].rearrange("p (g m) -> p g m", m=4)
                    pr = r[:, 112:160].rearrange("p (g m) -> p g m", m=6)
                    e.tensor_tensor(pr[:, :, 0:3], g4[:, :, 0:3], g4[:, :, 1:4], ALU.add)
                    e.tensor_tensor(pr[:, :, 3:5], g4[:, :, 0:2], g4[:, :, 2:4], ALU.add)
                    lk(e.tensor_tensor(pr[:, :, 5:6], g4[:, :, 0:1], g4[:, :, 3:4], ALU.add))
                    gs = r[:, 160:176].rearrange("p (t m) -> p t m", t=QT)
                    lka(e.tensor_reduce(gs[:, :, 0:NG], pr.rearrange("p (t g) m -> p t g m", t=QT), AX.X, ALU.max))
                    gm = r[:, 176:192].rearrange("p (t m) -> p t m", t=QT)
                    for t in range(QT):
                        ins = e.max(gm[:, t, :], gs[:, t, :])
                    lka(ins)
                    for t in range(QT):
                        ins = e.max_index(ru[s][:, t, :], gm[:, t, :], gs[:, t, :])
                    lk(ins)
                    gi = r[:, 192:196].rearrange("p (t m) -> p t m", t=QT)
                    lk(e.tensor_copy(gi, ru[s][:, :, 0:2]))
                    eq = r[:, 196:212].rearrange("p (t m g) -> p t m g", t=QT, m=2)
                    lk(e.tensor_tensor(eq, bc(gi, 3, NG), bc(bc(iota[:, 0:NG], 1, 2), 1, QT), ALU.is_equal))
                    sel = r[:, 212:220].rearrange("p (t g) -> p t g", t=QT)
                    lk(e.tensor_tensor(sel, eq[:, :, 0, :], eq[:, :, 1, :], ALU.add))
                    lk(e.tensor_scalar(sel, sel, 2 * BIG, -BIG, ALU.mult, ALU.add))
                    mk = r[:, 220:252].rearrange("p (t g m) -> p t g m", t=QT, m=4)
                    lka(e.tensor_tensor(mk, sfc.rearrange("p t (g m) -> p t g m", m=4), bc(sel, 3, 4), ALU.min))
                    mk = r[:, 220:252].rearrange("p (t e) -> p t e", t=QT)
                else:
                    sc = r[:, 48:80].rearrange("p (t e) -> p t e", t=QT)
                    lk(e.tensor_reduce(r[:, 4:6], th[s][:], AX.X, ALU.add))
                    lk(e.reciprocal(r[:, 6:8], r[:, 4:6]))
                    lka(e.tensor_tensor(sc, th[s][:], bc(r[:, 6:8], 2, E), ALU.mult))
                    mk = sc
                for t in range(QT):
                    ins = e.max(tv[:, t, :], mk[:, t, :])
                lka(ins)
                for t in range(QT):
                    ins = e.max_index(ru[s][:, t, :], tv[:, t, :], mk[:, t, :])
                lk(ins)
                lk(e.tensor_copy(ek_, ru[s][:, :, 0:K]))
                lk(e.tensor_tensor(oh, bc(ek_, 3, E), bc(bc(iota, 1, K), 1, QT), ALU.is_equal))
                with nc.allow_low_precision(reason="a sum of at most one 1"):
                    e.tensor_reduce(m16[s][:], oh.rearrange("p t k e -> p t e k"), AX.X, ALU.add
                                    ).then_inc(sig["mask", s], 1)
                if L == 0:
                    lk(e.tensor_tensor(tmp, oh, bc(sc, 2, K), ALU.mult))
                    lk(e.tensor_reduce(wk_, tmp, AX.X, ALU.add))
                    lk(e.tensor_reduce(r[:, 4:6], wk_, AX.X, ALU.add))
                    lk(e.tensor_scalar(r[:, 4:6], r[:, 4:6], 1e-20, None, ALU.add))
                    lk(e.reciprocal(r[:, 6:8], r[:, 4:6]))
                    lk(e.scalar_tensor_tensor(out=wk_, in0=wk_, scalar=ROUTED_SCALE, in1=bc(r[:, 6:8], 2, K),
                                              op0=ALU.mult, op1=ALU.mult))
                else:
                    lk(e.tensor_copy(wk_, tv[:, :, 0:K]))

            def place_rows(L, u, s):
                K = TOPK[L]
                r = rt[s]
                lk = lambda i: link(i, "c_rt", s, L, u)
                lka = lambda i: link_apart(i, "c_rt", s, L, u)
                oh = r[:, 256:256 + QT * 4 * E].rearrange("p (t k e) -> p t k e", t=QT, k=4)[:, :, 0:K, :]
                tmp = r[:, 384:384 + QT * 4 * E].rearrange("p (t k e) -> p t k e", t=QT, k=4)[:, :, 0:K, :]
                sk_ = mt[s][:, 1, :].rearrange("p (t k) -> p t k", t=QT)[:, :, 0:K]
                pos = r[:, 48:80].rearrange("p (t e) -> p t e", t=QT)
                e.wait_ge(sig["rank", s], at("rank", L, u))
                cbase = 2 * NIT * L
                e.wait_ge(cnt_s, cbase + u * 2 + s)
                lk(e.tensor_tensor(pos, ps[:, 4 * s + 1, 64:96].rearrange("p (t e) -> p t e", t=QT),
                                   bc(cnt[:], 1, QT), ALU.add))
                e.tensor_tensor(cnt[:], ps[:, 4 * s + 1, 96:112], cnt[:], ALU.add).then_inc(cnt_s, 1)
                lk(e.tensor_tensor(pos, pos, bc(cc(C_EBASE, E), 1, QT), ALU.add))
                lk(e.tensor_tensor(tmp, oh, bc(pos, 2, K), ALU.mult))
                lka(e.tensor_reduce(sk_, tmp, AX.X, ALU.add))
                lk(e.tensor_copy(meta[:, bass.ds(u * 2 + s, 1)].rearrange("p o k t -> p (o k) t"), mt[s][:]))
                e.tensor_copy(xidx[s][:].rearrange("p (t k) -> p t k", t=QT)[:, :, 0:K], sk_
                              ).then_inc(sig["slots", s], 1)

            def tables(L):
                n = [TBN * L]

                def lk(ins):
                    n[0] += 1
                    ins.then_inc(tb_s, 1)
                    e.wait_ge(tb_s, n[0])

                nt, ci = tb[:, 0:E], tb[:, E:2 * E]
                et, ct = tb[:, 32:35], tb[:, 35:38]
                low = cc(C_LOW, E * E).rearrange("p (e f) -> p e f", f=E)
                big = rt[0][:, 0:0]
                cmpb = ygath[0][:].rearrange("p k d -> p (k d)")[:, 0:E * 64].rearrange("p (e j) -> p e j", j=64)
                sq = ygath[0][:].rearrange("p k d -> p (k d)")[:, 1024:1280].rearrange("p (e f) -> p e f", f=E)
                le = tb[:, 64:112].rearrange("p (c e) -> p c e", e=E)
                ln = tb[:, 112:160].rearrange("p (c e) -> p c e", e=E)
                tt = cc(C_T, 3)
                lk(e.tensor_copy(cnti[:], cnt[:]))
                lk(e.tensor_tensor(cmpb, bc(cnt[:], 2, 64), bc(cc(C_J128, 64), 1, E), ALU.is_gt))
                lk(e.tensor_reduce(nt, cmpb, AX.X, ALU.add))
                lk(e.tensor_tensor(sq, low, bc(nt, 1, E), ALU.mult))
                lk(e.tensor_reduce(ci, sq, AX.X, ALU.add))
                lk(e.tensor_tensor(le, bc(ci, 1, 3), bc(tt, 2, E), ALU.is_le))
                lk(e.tensor_tensor(ln, le, bc(nt, 1, 3), ALU.mult))
                lk(e.tensor_reduce(et, le, AX.X, ALU.add))
                lk(e.tensor_reduce(ct, ln, AX.X, ALU.add))
                lk(e.tensor_tensor(ct, tt, ct, ALU.subtract))
                lk(e.tensor_scalar(tb[:, 38:41], et, float(REG), None, ALU.mult))
                lk(e.scalar_tensor_tensor(out=tbo[:, 0, :], in0=ct, scalar=float(P), in1=tb[:, 38:41],
                                          op0=ALU.mult, op1=ALU.add))
                lk(e.tensor_scalar(tbo[:, 1, :], et, float(E - 1), None, ALU.min))
                lk(e.tensor_tensor(delta[:], ci, nt, ALU.subtract))
                lk(e.scalar_tensor_tensor(out=delta[:], in0=delta[:], scalar=float(P), in1=cc(C_EBASE, E),
                                          op0=ALU.mult, op1=ALU.subtract))
                lk(e.memset(cnt[:], 0.0))
                assert n[0] == TBN * (L + 1), n

            def expert_phase(L):
                n0, r0 = (0, 0) if L == 0 else (NT[0], NT[0] // 4)

                def early(n, k):
                    return isinstance(n, int) and n < k and L == 0

                def mul(n, r):
                    e.wait_ge(eG, n0 + n + 1)
                    if not early(n, 2):
                        e.wait_ge(eHT_ps, n0 + n - 1)
                    e.tensor_tensor(hm[r % 2], hg[r % 2], ps[:, 2 + r % 2, F:2 * F], ALU.mult
                                    ).then_inc(eH, 1)

                def copy_h(n, r):
                    e.wait_ge(eHT_ps, n0 + n + 1)
                    if not early(n, 2):
                        e.wait_ge(eD, n0 + n - 1)
                    e.tensor_copy(hT[r % 2], ps[:, 4 + r % 2, 0:P]).then_inc(eHT, 1)

                def copy_y(n, r, v):
                    e.wait_ge(eD, n0 + n + 1)
                    if not early(n, 4):
                        e.wait_ge(yst[r % 4], 16 * (r0 + v))
                    e.tensor_copy(yt[r % 4], ps[:, 6 + r % 2, 0:D]).then_inc(eY, 1)

                def step(n, i, v):
                    last = isinstance(n, int) and n >= NT[L]
                    if not last:
                        mul(n, i)
                    if not (isinstance(n, int) and n < 2):
                        copy_y(n - 2, i + 2, v if i >= 2 else v - 1)
                    if not (isinstance(n, int) and (n < 1 or n > NT[L])):
                        copy_h(n - 1, i + 3)

                for n in range(4):
                    step(n, n, 0)
                with e.Fori(1, NT[L] // 4 - 1) as v:
                    for i in range(4):
                        step(v * 4 + i, i, v)
                for n in range(NT[L] - 4, NT[L] + 2):
                    step(n, n % 4, n // 4)

            for L in range(2):
                attention_phase(L)
                end_phase(e, 3 * L + 1)
                tables(L)
                end_phase(e, 3 * L + 2)
                expert_phase(L)
                end_phase(e, 3 * L + 3)

            with e.Fori(0, NIT) as u:
                num = [0, 0]

                def lkf(s):
                    def f(ins):
                        num[s] += 1
                        ins.then_inc(f_c[s], 1)
                        e.wait_ge(f_c[s], u * C1N + num[s])
                    return f

                for s in range(2):
                    yslots_chain(s, lkf(s), u * 2 + s, TOPK[1], f_slot[s])
                for s in range(2):
                    e.wait_ge(f_ld[s], 16 * (u + 1))
                    e.wait_ge(f_ga[s], 64 * (u + 1))
                    combine(s, X, lkf(s), TOPK[1]).then_inc(fin[s], 1)
                assert num[0] == C1N, num

        @block.tensor
        def _(e):
            def attention_phase(L):
                e.wait_ge(init, 5)
                e.wait_ge(w_small, NSMALL)
                if L == 1:
                    e.wait_ge(w_small1, NSMALL1)

                def transpose_x(u, s, src, k):
                    e.wait_ge(sig["xn", s], at("xn", L, u, k))
                    for t in range(QT):
                        for c in range(DC):
                            mm = e.transpose(ps[:, 4 * s, c * LQ + t * P:c * LQ + (t + 1) * P],
                                             src[:, t, c * P:(c + 1) * P], ident)
                    mm.then_inc(sig["xnT_ps", s], 1)

                def T1(u, s):
                    e.wait_ge(sig["base", s], at("base", L, u, 0))
                    transpose_x(u, s, xn[s], 1)

                def KVQ(u, s):
                    k0 = 4 * s
                    e.wait_ge(sig["ld", s], at("ld", L, u))
                    for i in range(HT):
                        for c in range(DC):
                            mm = e.matmul(ps[:, k0 + 3, i * LK:(i + 1) * LK],
                                          wk[:, c, i * P:(i + 1) * P], ctxT[s][:, c, :],
                                          start=(c == 0), stop=(c == DC - 1 and L == 0))
                        if L == 1:
                            mm = e.matmul(ps[:, k0 + 3, i * LK:(i + 1) * LK], cc(C_SEL, P, 1),
                                          mrow[s][:], start=False, stop=True)
                    mm.then_inc(sig["K_ps", s], 1)
                    e.wait_ge(sig["xnT", s], at("xnT", L, u, 1))
                    for c in range(DC):
                        mm = e.matmul(ps[0:LK, k0, 0:D], ctxT[s][:, c, :], wv[:, c, :],
                                      start=(c == 0), stop=(c == DC - 1))
                    mm.then_inc(sig["V_ps", s], 1)
                    e.wait_ge(sig["slots", s], at("slots", L, u, 0))
                    for i in range(HT):
                        for c in range(DC):
                            mm = e.matmul(ps[:, k0 + 1 + i // 2, i % 2 * LQ:(i % 2 + 1) * LQ],
                                          wq[:, c, i * P:(i + 1) * P], xnT[s][:, c, :],
                                          start=(c == 0), stop=(c == DC - 1))
                    mm.then_inc(sig["Q_ps", s], 1)

                def S(u, s, t):
                    if t == 0:
                        e.wait_ge(sig["KB", s], at("KB", L, u))
                        e.wait_ge(sig["V", s], at("V", L, u))
                        e.wait_ge(sig["Q", s], at("Q", L, u))
                    else:
                        e.wait_ge(sig["smax", s], at("smax", L, u, 1))
                    for i in range(HT):
                        mm = e.matmul(ps[:, 4 * s + i, 0:G * LK], Q[s][:, i, t * P:(t + 1) * P],
                                      KB[s][:, i, :, :].rearrange("p j k -> p (j k)"),
                                      start=True, stop=True)
                    mm.then_inc(sig["S", s], 1)

                def MT(u, s):
                    e.wait_ge(sig["smax", s], at("smax", L, u, 2))
                    for i in range(HT):
                        for t in range(QT):
                            mm = e.transpose(
                                ps[:, 4 * s + i // 2, i % 2 * LQ + t * P:i % 2 * LQ + (t + 1) * P],
                                Mp[s][:, t, i, :, :].rearrange("p j c -> p (j c)"), ident)
                    mm.then_inc(sig["MT", s], 1)

                def ST(u, s):
                    e.wait_ge(sig["Qa", s], at("Qa", L, u))
                    for i in range(HT):
                        bank = 4 * s + (2 if i % 2 == 0 else 0)
                        if i >= 2:
                            e.wait_ge(sig["Pr", s], at("Pr", L, u, i - 1))
                        for j in range(G):
                            mm = e.matmul(ps[0:LK, bank + j // 2, j % 2 * LQ:(j % 2 + 1) * LQ],
                                          KB[s][:, i, j, :], Q[s][:, i, :], start=True, stop=True)
                        mm.then_inc(sig["ST", s], 1)

                def PV(u, s):
                    e.wait_ge(sig["Pr", s], at("Pr", L, u, 3))
                    for i in range(HT):
                        if i == HT - 1:
                            e.wait_ge(sig["Pr", s], at("Pr", L, u, 4))
                        for j in range(G):
                            h = G * i + j
                            mm = e.matmul(
                                ps[j * HP:(j + 1) * HP, 4 * s + 2 + i // 2, i % 2 * LQ:(i % 2 + 1) * LQ],
                                V[s][:, h, :], W[s][0:LK, h, :], start=True, stop=True)
                    mm.then_inc(sig["OT_ps", s], 1)

                def OX(u, s):
                    e.wait_ge(sig["OT", s], at("OT", L, u))
                    for t in range(QT):
                        for i in range(HT):
                            mm = e.transpose(ps[:, 4 * s + t, i * P:(i + 1) * P],
                                             Q[s][:, i, t * P:(t + 1) * P], ident)
                    mm.then_inc(sig["O_ps", s], 1)

                def OT2(u, s):
                    e.wait_ge(sig["O", s], at("O", L, u))
                    for t in range(QT):
                        for c in range(DC):
                            mm = e.transpose(ps[:, 4 * s + 2, c * LQ + t * P:c * LQ + (t + 1) * P],
                                             O[s][:, t, c * P:(c + 1) * P], ident)
                    mm.then_inc(sig["OnT_ps", s], 1)

                def Wo(u, s):
                    e.wait_ge(sig["OnT", s], at("OnT", L, u))
                    for t in range(QT):
                        for c in range(DC):
                            mm = e.matmul(ps[:, 4 * s + 3, t * D:(t + 1) * D],
                                          xnT[s][:, c, t * P:(t + 1) * P], wo[:, c, :],
                                          start=(c == 0), stop=(c == DC - 1))
                    mm.then_inc(sig["Wo", s], 1)

                def T2(u, s):
                    e.wait_ge(sig["O", s], at("O", L, u))
                    transpose_x(u, s, xn2[s], 2)

                def GU(u, s):
                    e.wait_ge(sig["xnT", s], at("xnT", L, u, 2))
                    for t in range(QT):
                        for c in range(DC):
                            mm = e.matmul(ps[:, 4 * s + 1, t * E:(t + 1) * E],
                                          xnT[s][:, c, t * P:(t + 1) * P], gw[L][:, c, :],
                                          start=(c == 0), stop=(c == DC - 1))
                    mm.then_inc(sig["lg", s], 1)
                    for m in range(4):
                        for c in range(DC):
                            mm = e.matmul(ps[:, 4 * s + 2 + m // 2, m % 2 * LQ:(m % 2 + 1) * LQ],
                                          wsgu[:, c, m * P:(m + 1) * P], xnT[s][:, c, :],
                                          start=(c == 0), stop=(c == DC - 1))
                    mm.then_inc(sig["GU", s], 1)

                def SH(u, s):
                    e.wait_ge(sig["HS", s], at("HS", L, u))
                    for t in range(QT):
                        for c in range(2):
                            mm = e.matmul(ps[:, 4 * s, t * D:(t + 1) * D],
                                          W[s][:, 4 + c, t * P:(t + 1) * P], wsd[:, c, :],
                                          start=(c == 0), stop=(c == 1))
                    mm.then_inc(sig["SH", s], 1)

                def rank(u, s):
                    e.wait_ge(sig["mask", s], at("mask", L, u))
                    e.wait_ge(sig["th", s], at("th", L, u))
                    tri, one = tri16[:, 0:P], tri16[:, P:2 * P]
                    bank = ps[:, 4 * s + 1, :]
                    e.matmul(bank[:, 64:80], tri, m16[s][:, 0, :], start=True, stop=True)
                    e.matmul(bank[:, 80:96], tri, m16[s][:, 1, :], start=True, stop=False)
                    e.matmul(bank[:, 80:96], one, m16[s][:, 0, :], start=False, stop=True)
                    e.matmul(bank[:, 96:112], one, m16[s][:, 0, :], start=True, stop=False)
                    e.matmul(bank[:, 96:112], one, m16[s][:, 1, :], start=False, stop=True
                             ).then_inc(sig["rank", s], 1)

                stages = {
                    "PV": PV, "T1": T1, "OX": OX, "KVQ": KVQ, "S0": lambda u, s: S(u, s, 0),
                    "S1": lambda u, s: S(u, s, 1), "T2": T2, "MT": MT, "GU": GU, "ST": ST, "SH": SH,
                    "rank": rank,
                }
                if L == 0:
                    stages.update({"OT2": OT2, "Wo": Wo})
                run_halves(e, "PE", stages)

            def expert_phase(L):
                n0, r0 = (0, 0) if L == 0 else (NT[0], NT[0] // 4)

                def early(n, k):
                    return isinstance(n, int) and n < k and L == 0

                def trans(n, r, v):
                    e.wait_ge(xl[r % 4], 16 * (r0 + v + 1))
                    if not early(n, 2):
                        e.wait_ge(eT, n0 + n - 1)
                    for c in range(DC):
                        mm = e.transpose(ps[:, r % 2, c * P:(c + 1) * P], xt[r % 4][:, c * P:(c + 1) * P], ident)
                    mm.then_inc(eT_ps, 1)

                def gate_up(n, r):
                    x = e.value_load(tab[0:1, 1, bass.ds(n, 1)], min_val=0, max_val=E - 1)
                    e.wait_ge(eT, n0 + n + 1)
                    if not early(n, 2):
                        e.wait_ge(eH, n0 + n - 1)
                    for c in range(DC):
                        mm = e.matmul(ps[:, 2 + r % 2, 0:2 * F], xtT[r % 2][:, c, :],
                                      wgu[:, bass.ds(x * (DC * 2 * F) + c * 2 * F, 2 * F)],
                                      start=(c == 0), stop=(c == DC - 1))
                    mm.then_inc(eGU, 1)

                def down(n, r):
                    x = e.value_load(tab[0:1, 1, bass.ds(n, 1)], min_val=0, max_val=E - 1)
                    e.wait_ge(eHT, n0 + n + 1)
                    if not early(n, 2):
                        e.wait_ge(eY, n0 + n - 1)
                    e.matmul(ps[:, 6 + r % 2, 0:D], hT[r % 2], wd[:, bass.ds(x * D, D)],
                             start=True, stop=True).then_inc(eD, 1)

                def trans_h(n, r):
                    e.wait_ge(eH, n0 + n + 1)
                    if not early(n, 2):
                        e.wait_ge(eHT, n0 + n - 1)
                    e.transpose(ps[:, 4 + r % 2, 0:P], hm[r % 2], ident).then_inc(eHT_ps, 1)

                def step(n, i, v):
                    peeled = isinstance(n, int)
                    if not (peeled and n >= NT[L] - 1):
                        trans(n + 1, i + 1, v if i < 3 else v + 1)
                    if not (peeled and n >= NT[L]):
                        gate_up(n, i)
                    if not (peeled and n < 2):
                        down(n - 2, i + 2)
                    if not (peeled and (n < 1 or n > NT[L])):
                        trans_h(n - 1, i + 3)

                e.wait_ge(w_exp[L], 32)
                trans(0, 0, 0)
                for n in range(4):
                    step(n, n, 0)
                with e.Fori(1, NT[L] // 4 - 1) as v:
                    for i in range(4):
                        step(v * 4 + i, i, v)
                for n in range(NT[L] - 4, NT[L] + 2):
                    step(n, n % 4, n // 4)

            for L in range(2):
                attention_phase(L)
                end_phase(e, 3 * L + 1)
                end_phase(e, 3 * L + 2)
                expert_phase(L)
                end_phase(e, 3 * L + 3)


TBN = 16
C1N = 5


def _pad_heads(w):
    t = np.zeros((D, H, HP), w.dtype)
    t[:, :, :HD] = w.T.reshape(D, H, HD)
    return _chunks(t.reshape(D, H * HP))


def _chunks(w):
    return np.ascontiguousarray(w.reshape(-1, P, w.shape[1]).transpose(1, 0, 2))


def _column(b, row):
    t = np.zeros((H, HP), np.float32)
    if b is not None:
        t[:, :HD] = b.reshape(H, HD)
    if row is not None:
        t[:, row] = 1.0
    return np.ascontiguousarray(t.reshape(HT, P).T)


def _experts(g, u, d):
    gu = np.concatenate([g, u], axis=2).reshape(E, DC, P, 2 * F).transpose(2, 0, 1, 3)
    return (np.ascontiguousarray(gu.reshape(P, -1)),
            np.ascontiguousarray(d.transpose(1, 0, 2).reshape(P, -1)))


def layout(i):
    i = {k: np.asarray(v) for k, v in i.items()}
    rows = lambda v: np.ascontiguousarray(np.broadcast_to(v[None], (P, v.shape[0])))
    r = {
        "x": np.ascontiguousarray(i["x"].reshape(B, QT, P, D).transpose(0, 2, 1, 3)),
        "ctxT": np.ascontiguousarray(i["ctx_1024"].transpose(0, 2, 1).reshape(B, DC, P, LK).transpose(0, 2, 1, 3)),
        "mask": np.ascontiguousarray(i["mask_BxS2_ik0"]),
        "consts": consts(),
        "wq0": _pad_heads(i["L0_xattn_Wq"]), "wk0": _pad_heads(i["L0_xattn_Wk"]),
        "wv0": _chunks(i["L0_xattn_Wv"].T), "wo0": _chunks(i["L0_xattn_Wo"].T),
        "bo": rows(i["L0_xattn_bo"]), "bv": rows(i["L1_xattn_v_b"]), "gbias": rows(i["L0_ffn_gate_bias"]),
        "wq1": _pad_heads(i["L1_xattn_q_w"]), "wk1": _pad_heads(i["L1_xattn_k_w"]),
        "wv1": _chunks(i["L1_xattn_v_w"].T),
        "bk0": _column(None, AUG), "bk1": _column(i["L1_xattn_k_b"], AUG),
        "bq1": _column(i["L1_xattn_q_b"], MSK),
        "gw0": _chunks(i["L0_ffn_gate_w"].T), "gw1": _chunks(i["L1_ffn_Wr"]),
        "wsgu0": _chunks(np.concatenate([i["L0_ffn_Ws_g"].T, i["L0_ffn_Ws_u"].T], axis=1)),
        "wsd0": _chunks(i["L0_ffn_Ws_d"].T),
        "wsgu1": _chunks(np.concatenate([i["L1_ffn_Sg"], i["L1_ffn_Su"]], axis=1)),
        "wsd1": _chunks(i["L1_ffn_Sd"]),
    }
    r["wgu0"], r["wd0"] = _experts(i["L0_ffn_Wg"].transpose(0, 2, 1), i["L0_ffn_Wu"].transpose(0, 2, 1),
                                   i["L0_ffn_Wd"].transpose(0, 2, 1))
    r["wgu1"], r["wd1"] = _experts(i["L1_ffn_Wg"], i["L1_ffn_Wu"], i["L1_ffn_Wd"])
    return r


def kernel(**inputs):
    import concourse.bacc as bacc
    from concourse.bass_utils import run_bass_kernel_spmd as run

    nc = bacc.Bacc("TRN2", target_bir_lowering=False, num_devices=1)
    arrays = {f"in_{k}": v for k, v in layout(inputs).items()}
    a = {k[3:]: nc.dram_tensor(k, v.shape, mybir.dt.from_np(v.dtype), kind="ExternalInput").ap()
         for k, v in arrays.items()}
    out = nc.dram_tensor("out_x", (B, P, QT, D), F32, kind="ExternalOutput").ap()
    build(nc, a, out)
    r = run(nc, [arrays], core_ids=[0])
    y = r.results[0]["out_x"]
    return np.ascontiguousarray(y.transpose(0, 2, 1, 3).reshape(B, LQ, D))
```

```python
from contextlib import ExitStack

import concourse.bass as bass
import numpy as np
from concourse import mybir

ALU = mybir.AluOpType
ACT = mybir.ActivationFunctionType
AX = mybir.AxisListType
F32 = mybir.dt.float32
BF16 = mybir.dt.bfloat16
U32 = mybir.dt.uint32
I32 = mybir.dt.int32

P = 128
B, LQ, D = 32, 256, 256
LK = 120
H, HD = 16, 16
HP = 32
MSK = HD
SUM = HD
QT = LQ // P
DC = D // P
G = P // HP
HT = H // G
E, F = 16, 128
NG = 4
TOPK = (4, 2)
NTOK = B * LQ
REG = NTOK + P
NT = tuple(NTOK * k // P + E for k in TOPK)
NTMAX = 3 * P
XROWS = E * REG + E * P
SCALE = HD ** -0.5
EPS = 1e-5
BIG = 1e30
ROUTED_SCALE = 2.5
NIT = B // 2

C_ID, C_TRI, C_ONE = 0, P, 2 * P
C_IOTA = C_ONE + P
C_EBASE = C_IOTA + E
C_LOW = C_EBASE + E
C_J128 = C_LOW + E * E
C_T = C_J128 + 64
C_MH = C_T + 3
NCONST = C_MH + 2

PER = {
    "ld": (32, 48), "ga": (0, 128), "yidx": (0, 1), "var": (2, 2), "rstd": (2, 2), "xn": (2, 2), "xnT_ps": (2, 2),
    "xnT": (2, 2), "K_ps": (1, 1), "V_ps": (1, 1), "Q_ps": (2, 2), "KB": (1, 1), "V": (1, 1),
    "Q": (2, 2), "S": (4, 4), "smax": (4, 4), "Pr": (4, 4), "PT_ps": (4, 4), "PT": (4, 4),
    "OT_ps": (1, 1), "OT": (1, 1), "O_ps": (1, 1), "O": (1, 1), "OnT_ps": (1, 0),
    "OnT": (1, 0), "Wo": (1, 0), "xb": (1, 0), "x1": (1, 0), "lg": (1, 1), "GU": (1, 1),
    "nm": (0, 1), "th": (1, 1), "TH": (1, 1), "HS": (1, 1), "SH": (1, 1), "base": (1, 1),
    "st": (16, 16), "mask": (1, 1), "rank": (1, 1), "slots": (1, 1), "sc": (128, 64),
    "c_ln": (3, 8), "c_sm": (4, 4), "c_at": (6, 7), "c_rt": (26, 13),
}


ORDER = {
    "SP": (("load", "n"), ("store", "b")),
    "Pool": (("rstd2", "b"), ("rstd1", "n"), ("xb", "n"), ("gather", "n"), ("scatter", "b")),
    "ACT": (("xnT1", "a"), ("OT", "b"), ("Q0", "a"), ("Q1", "a"), ("OnT", "b"), ("exp0", "a"),
            ("exp1", "a"), ("xnT2", "b"), ("exp2", "a"), ("th", "b"), ("exp3", "a"), ("TH", "b"),
            ("PT0", "a"), ("PT1", "a"), ("PT2", "a"), ("PT3", "a"), ("KB", "n")),
    "DVE": (("out", "b"), ("max0", "a"), ("max1", "a"), ("x1", "b"), ("max2", "a"), ("xn2", "b"),
            ("max3", "a"), ("nm", "b"), ("choose", "b"), ("HS", "b"), ("ln1", "n"), ("weigh", "b"),
            ("xn1", "n"), ("base", "b"), ("V", "n"), ("place", "b")),
    "PE": (("T1", "a"), ("PV", "b"), ("Q0", "a"), ("OX", "b"), ("Q1", "a"), ("S0", "a"), ("OT2", "b"),
           ("S1", "a"), ("Wo", "b"), ("S2", "a"), ("S3", "a"), ("T2", "b"), ("GU", "b"), ("PT0", "a"),
           ("PT1", "a"), ("PT2", "a"), ("PT3", "a"), ("SH", "b"), ("KV", "n"), ("rank", "b")),
}


def run_halves(e, engine, stages):
    def half(u, s, first=False, last=False):
        v = u if s == 1 else u - 1
        for name, role in ORDER[engine]:
            if name not in stages:
                continue
            if role == "a" and not last:
                stages[name](u, s)
            if role == "b" and not first:
                stages[name](v, 1 - s)
            if role == "n" and not last and not (isinstance(v, int) and v == NIT - 1):
                stages[name](v + 1, 1 - s)

    half(0, 0, first=True)
    half(0, 1)
    half(1, 0)
    with e.Fori(1, NIT - 1) as u:
        half(u, 1)
        half(u + 1, 0)
    half(NIT - 1, 1)
    half(NIT, 0, last=True)


def consts():
    c = np.zeros((P, NCONST), np.float32)
    c[:, C_ID:C_ID + P] = np.eye(P)
    c[:, C_TRI:C_TRI + P] = np.triu(np.ones((P, P)), 1)
    c[:, C_ONE:C_ONE + P] = 1.0
    c[:, C_IOTA:C_IOTA + E] = np.arange(E)
    c[:, C_EBASE:C_EBASE + E] = np.arange(E) * REG
    c[:, C_LOW:C_LOW + E * E] = np.tril(np.ones((E, E))).reshape(-1)
    c[:, C_J128:C_J128 + 64] = np.arange(64) * P
    c[:, C_T:C_T + 3] = np.arange(3)[None] * P + np.arange(P)[:, None]
    c[:, C_MH:C_MH + 2] = -0.5
    return c


def bc(ap, axis, n):
    a = ap.unsqueeze(axis)
    shape = list(a.shape)
    shape[axis] = n
    return a.broadcast_to(shape)


def build(nc, a, out):
    ctx = ExitStack()

    def sb(name, shape, dt=F32):
        return ctx.enter_context(nc.sbuf_tensor(name, shape, dt))

    def sem(name):
        return ctx.enter_context(nc.semaphore(name))

    with ctx:
        ps = ctx.enter_context(nc.psum_tensor("ps", [P, 8, 512], F32))
        xsort = nc.dram_tensor("xsort", [XROWS, D], F32).ap()
        ysort = nc.dram_tensor("ysort", [NT[0] * P, D], F32).ap()
        based = nc.dram_tensor("based", [B, P, QT, D], F32).ap()
        mrowd = nc.dram_tensor("mrowd", [B, LK], F32).ap()
        tabd = [nc.dram_tensor(f"tabd{L}", [2, NTMAX], I32).ap() for L in range(2)]

        cst = sb("cst", [P, NCONST])
        tri16 = sb("tri16", [P, 2 * P], BF16)
        gw = [sb(f"gw{L}", [P, DC, E]) for L in range(2)]
        gbias = sb("gbias", [P, E])
        bo_bc = sb("bo_bc", [P, D])
        bv_bc = sb("bv_bc", [P, D])
        bq = [sb(f"bq{L}", [P, HT]) for L in range(2)]
        kaug = sb("kaug", [2, HT * P])
        wq = sb("wq", [P, DC, HT * P])
        wk = sb("wk", [P, DC, HT * P])
        wv = sb("wv", [P, DC, D])
        wo = sb("wo", [P, DC, D])
        wsgu = sb("wsgu", [P, DC, 512])
        wsd = sb("wsd", [P, DC, D])
        wgu = sb("wgu", [P, E * DC * 2 * F])
        wd = sb("wd", [P, E * D])
        mrow = [sb(f"mrow{s}", [2, LK]) for s in range(2)]
        mask_i, mask_f = sb("mask_i", [B, LK], I32), sb("mask_f", [B, LK])
        zero = sb("zero", [P, D])
        meta = sb("meta", [P, B + 2, 3, QT * 4])
        cnt = sb("cnt", [P, E])
        delta = sb("delta", [P, E])

        X = [sb(f"X{s}", [P, QT, D]) for s in range(2)]
        XL = [sb(f"XL{s}", [P, QT, D]) for s in range(2)]
        XO = [sb(f"XO{s}", [P, QT, D]) for s in range(2)]
        ctxT = [sb(f"ctxT{s}", [P, DC, LK]) for s in range(2)]
        xn2 = [sb(f"xn2{s}", [P, QT, D]) for s in range(2)]
        xnT = [sb(f"xnT{s}", [P, DC, LQ]) for s in range(2)]
        Q = [sb(f"Q{s}", [P, HT, LQ]) for s in range(2)]
        KB = [sb(f"KB{s}", [P, HT, G, LK]) for s in range(2)]
        V = [sb(f"V{s}", [LK, H, HP]) for s in range(2)]
        W = [sb(f"W{s}", [P, H, LQ]) for s in range(2)]
        O = [sb(f"O{s}", [P, QT, D]) for s in range(2)]
        xn = O
        prob = [[W[s][:, G * i:G * (i + 1), :].rearrange("p h q -> p (h q)")[:, 0:QT * G * LK].rearrange(
            "p (t j k) -> p t j k", t=QT, j=G) for i in range(HT)] for s in range(2)]
        mx = [sb(f"mx{s}", [P, HT, QT, G]) for s in range(2)]
        nmx = [sb(f"nmx{s}", [P, HT, QT, G]) for s in range(2)]
        ygath = [sb(f"ygath{s}", [P, QT * 4, D]) for s in range(2)]
        xb = [ygath[s][:, 0:QT, :] for s in range(2)]
        yidx = [sb(f"yidx{s}", [P, QT * 4], U32) for s in range(2)]
        rows_of = sb("rows_of", [P, B + 2, QT * 4])
        is_e = sb("is_e", [P, B, QT * 4])
        xidx = [sb(f"xidx{s}", [P, QT * 4], U32) for s in range(2)]
        st6 = [sb(f"st6{s}", [P, QT, 6]) for s in range(2)]
        mv = [sb(f"mv{s}", [P, QT, 2]) for s in range(2)]
        ve = [sb(f"ve{s}", [P, QT]) for s in range(2)]
        rstd = [sb(f"rstd{s}", [P, QT]) for s in range(2)]
        nmr = [sb(f"nmr{s}", [P, QT]) for s in range(2)]
        rsum = [sb(f"rsum{s}", [P, QT, H]) for s in range(2)]
        th = [sb(f"th{s}", [P, QT, E]) for s in range(2)]
        rt = [sb(f"rt{s}", [P, 640]) for s in range(2)]
        ru = [sb(f"ru{s}", [P, QT, 8], U32) for s in range(2)]
        m16 = [sb(f"m16{s}", [P, QT, E], BF16) for s in range(2)]
        mt = [sb(f"mt{s}", [P, 3, QT * 4]) for s in range(2)]
        mg = [sb(f"mg{s}", [P, 3, QT * 4]) for s in range(2)]

        xt = [ygath[0][:, r, :] for r in range(4)]
        xtT = [ygath[1][:, r, :].rearrange("p (c q) -> p c q", c=DC) for r in range(2)]
        hg = [ygath[1][:, 2 + r, 0:F] for r in range(2)]
        hm = [ygath[1][:, 4 + r, 0:F] for r in range(2)]
        hT = [ygath[1][:, 6 + r, 0:P] for r in range(2)]
        yt4 = ygath[0][:, 4:8, :]
        yt = [yt4[:, r, :] for r in range(4)]
        tb = sb("tb", [P, 160])
        tbo = sb("tbo", [P, 2, 3], I32)
        cnti = sb("cnti", [P, E], I32)
        tab = sb("tab", [1, 2, NTMAX + 3], I32)

        sig = {(n, s): sem(f"{n}{s}") for n in PER for s in range(2)}
        w_small = sem("w_small")
        w_small1 = sem("w_small1")
        w_exp = [sem("w_exp0"), sem("w_exp1")]
        init = sem("init")
        phase = sem("phase")
        zfill = sem("zfill")
        zero_ok = sem("zero_ok")
        cnt_s = sem("cnt_s")
        tb_s = sem("tb_s")
        tb_st, tb_ld = sem("tb_st"), sem("tb_ld")
        xl = [sem(f"xl{r}") for r in range(4)]
        yst = [sem(f"yst{r}") for r in range(2)]
        eT_ps, eT, eGU, eG, eH, eHT_ps, eHT, eD, eY = (
            [sem(f"{n}{r}") for r in range(2)]
            for n in ("eT_ps", "eT", "eGU", "eG", "eH", "eHT_ps", "eHT", "eD", "eY"))
        fin = [sem("fin0"), sem("fin1")]
        mrow_st = sem("mrow_st")
        rows_s = sem("rows_s")

        def at(n, L, u, k=None):
            per = PER[n][L]
            return (NIT * PER[n][0] if L else 0) + per * u + (per if k is None else k)

        def end_phase(e, n):
            e.drain().then_inc(phase, 1)
            e.wait_ge(phase, 5 * n)

        def cc(o, n, rows=P):
            return cst[0:rows, o:o + n]

        def apart(e):
            e.nop(nofuse=True)

        def ended(n, s):
            return at(n, 1, NIT if n == "ga" else NIT - 1)

        def sbank(s, i):
            return 4 * s + (2 if i % 2 == 0 else 0)

        ident = cc(C_ID, P)
        NSMALL = 16 * 15
        NSMALL1 = 16 * 5

        def run_steps(e, L, step):
            t0, last = NT[0] // 4 * L, NT[L] // 4
            def four(w, regs, steps):
                n4 = (w - t0) * 4
                c2 = [2 * w + i for i in range(-1, 3)]
                if regs:
                    c2 = [e.snap(c) for c in c2]
                for r in range(steps):
                    step(n4 + r, r, w, c2)

            four(t0, False, 4)
            four(t0 + 1, False, 4)
            with e.Fori(t0 + 2, t0 + last) as w:
                four(e.snap(w), True, 4)
            four(t0 + last, False, 3)

        def tile(k, r, w, c2):
            m = r - k
            return m % 4, m % 2, c2[m // 2 + 2]

        block = ctx.enter_context(nc.Block())

        @block.sync
        def _(e):
            row_regs = [e.alloc_register(f"tile_row{r}") for r in range(4)]

            def load_small(pairs, s_):
                for dst, src in pairs:
                    e.dma_start(dst, src).then_inc(s_, 16)

            def load_exp(L):
                e.dma_start(wgu[:], a[f"wgu{L}"]).then_inc(w_exp[L], 16)
                e.dma_start(wd[:], a[f"wd{L}"]).then_inc(w_exp[L], 16)

            def wait(n, s, v):
                e.wait_ge(sig[n, s], v)
                apart(e)

            def load(L, u, s):
                b = u * 2 + s
                if not (isinstance(u, int) and L == 0 and u == 0):
                    wait("xn", s, at("xn", L, u, 0))
                    wait("xb" if L == 0 else "O", s, at("xb" if L == 0 else "O", L, u, 0))
                    wait("V_ps", s, at("V_ps", L, u, 0))
                src = a["x"] if L == 0 else based
                e.dma_start(XL[s][:], src[bass.ds(b, 1)].rearrange("o p t d -> (o p) t d")
                            ).then_inc(sig["ld", s], 16)
                e.dma_start(ctxT[s][:], a["ctxT"][bass.ds(b, 1)].rearrange("o p c k -> (o p) c k")
                            ).then_inc(sig["ld", s], 16)
                if L == 1:
                    e.dma_start(mrow[s][0:1, :], mrowd[bass.ds(b, 1), :]).then_inc(sig["ld", s], 16)

            def load_first(L):
                load(L, 0, 0)

            load_first(0)
            load_small([
                (cst[:], a["consts"]), (wk[:], a["wk0"]), (wq[:], a["wq0"]), (wv[:], a["wv0"]),
                (wo[:], a["wo0"]), (wsgu[:], a["wsgu0"]), (wsd[:], a["wsd0"]),
                (gw[0][:], a["gw0"]), (gw[1][:], a["gw1"]), (gbias[:], a["gbias"]),
                (bo_bc[:], a["bo"]), (bv_bc[:], a["bv"]), (bq[1][:], a["bq1"]),
                (kaug[:], a["kaug"]), (mask_i[:], a["mask"]),
            ], w_small)

            def attention_phase(L):
                def store(u, s):
                    wait("base", s, at("base", L, u))
                    e.dma_start(based[bass.ds(u * 2 + s, 1)].rearrange("o p t d -> (o p) t d"), XO[s][:]
                                ).then_inc(sig["st", s], 16)

                run_halves(e, "SP", {"load": lambda u, s: load(L, u, s), "store": store})
                for s in range(2):
                    e.wait_ge(sig["st", s], at("st", L, NIT - 1))

            def tables(L):
                e.wait_ge(tb_s, TBN * L + TBN)
                for k in range(2):
                    for c in range(3):
                        e.dma_start(tabd[L][k:k + 1, c * P:(c + 1) * P].rearrange("o p -> p o"),
                                    tbo[:, k, c:c + 1]).then_inc(tb_st, 16)
                e.wait_ge(tb_st, 16 * 6 * (L + 1))
                for k in range(2):
                    e.dma_start(tab[:, k, 3 * k:3 * k + NTMAX], tabd[L][k:k + 1, :]).then_inc(tb_ld, 16)
                e.wait_ge(tb_ld, 32 * (L + 1))

            def expert_phase(L):
                t0 = NT[0] // 4 * L

                def load(r, row):
                    e.dma_start(xt[r], xsort[bass.ds(row, P), :]).then_inc(xl[r], 16)

                def store(n, pair, c):
                    for h in range(2):
                        e.wait_ge(eY[h], c)
                    apart(e)
                    e.dma_start(ysort[bass.ds(n * P, 2 * P), :].rearrange("(t p) d -> p t d", p=P),
                                yt4[:, 2 * pair:2 * pair + 2, :]).then_inc(yst[pair], 16)

                def rows(n):
                    e.load(row_regs, tab[0:1, 0, bass.ds(n, 4)])
                    return [e.snap(x, min_val=0, max_val=XROWS - P) for x in row_regs]

                def four(w, regs):
                    n = (w - t0) * 4
                    c2 = [2 * w + i for i in range(-1, 3)]
                    if regs:
                        n, c2 = e.snap(n), [e.snap(c) for c in c2]
                    row = rows(n + 4)
                    for r in range(4):
                        e.wait_ge(eT_ps[r % 2], c2[2 + r // 2])
                        apart(e)
                        load(r, row[r])
                        if r % 2 == 1 and regs:
                            store(n - 5 + r, r // 2, c2[r // 2])

                row = rows(0)
                for r in range(4):
                    load(r, row[r])
                four(t0, False)
                with e.Fori(t0 + 1, t0 + NT[L] // 4 - 1) as w:
                    four(e.snap(w), True)
                for pair in range(4):
                    store(NT[L] - 8 + 2 * pair, pair % 2, 2 * (t0 + NT[L] // 4) - 3 + pair)
                for pair in range(2):
                    e.wait_ge(yst[pair], 16 * (t0 + NT[L] // 4))

            e.wait_ge(zero_ok, 1)
            e.dma_start(xsort[E * REG:XROWS, :].rearrange("(n p) d -> p n d", p=P), bc(zero[:], 1, E)
                        ).then_inc(zfill, 16)
            e.wait_ge(init, 5)
            e.dma_start(mrowd, mask_f[:]).then_inc(mrow_st, 16)
            load_exp(0)
            attention_phase(0)
            end_phase(e, 1)
            load_small([(wk[:], a["wk1"]), (wq[:], a["wq1"]), (wv[:], a["wv1"]),
                        (wsgu[:], a["wsgu1"]), (wsd[:], a["wsd1"])], w_small1)
            tables(0)
            end_phase(e, 2)
            expert_phase(0)
            end_phase(e, 3)
            e.wait_ge(mrow_st, 16)
            load_first(1)
            load_exp(1)
            attention_phase(1)
            end_phase(e, 4)
            tables(1)
            end_phase(e, 5)
            expert_phase(1)
            end_phase(e, 6)
            with e.Fori(0, NIT) as u:
                for s in range(2):
                    e.wait_ge(sig["st", s], ended("st", s) + u * 16)
                    apart(e)
                    e.dma_start(X[s][:], based[bass.ds(u * 2 + s, 1)].rearrange("o p t d -> (o p) t d")
                                ).then_inc(sig["ld", s], 16)
                for s in range(2):
                    e.wait_ge(fin[s], u + 1)
                    apart(e)
                    e.dma_start(out[bass.ds(u * 2 + s, 1)].rearrange("o p t d -> (o p) t d"), X[s][:]
                                ).then_inc(sig["st", s], 16)
            for s in range(2):
                e.wait_ge(sig["st", s], ended("st", s) + NIT * 16)

        @block.gpsimd
        def _(e):
            e.memset(zero[:], 0.0).then_inc(zero_ok, 1)
            for s in range(2):
                e.memset(KB[s][:], 0.0)
                e.memset(mrow[s][:], 1.0).then_inc(init, 1)
                e.memset(V[s][:], 0.0)
                e.wait_ge(init, s + 1)
            e.memset(rows_of[:], 0.0)
            e.memset(meta[:], 0.0).then_inc(init, 1)
            e.wait_ge(w_small, NSMALL)

            def scatter(L, s):
                for t in range(QT):
                    for k in range(TOPK[L]):
                        e.indirect_dma_start(
                            out=xsort, in_=xn2[s][:, t, :], in_offset=None,
                            out_offset=bass.IndirectOffsetOnAxis(
                                ap=xidx[s][:, t * 4 + k:t * 4 + k + 1], axis=0),
                        ).then_inc(sig["sc", s], 16)

            steps = [0]

            def link(ins):
                steps[0] += 1
                ins.then_inc(rows_s, 1)
                e.wait_ge(rows_s, steps[0])

            def all_rows():
                rows = rows_of[:, 0:B, :]
                link(e.tensor_copy(rows, meta[:, 0:B, 1, :]))
                for x in range(E):
                    link(e.tensor_scalar(is_e[:], meta[:, 0:B, 2, :], float(x), delta[:, x:x + 1],
                                         ALU.is_equal, ALU.mult))
                    link(e.tensor_tensor(rows, rows, is_e[:], ALU.add))

            def gather(L, s, u, k):
                e.tensor_copy(yidx[s][:], rows_of[:, bass.ds(u * 2 + s, 1), :].rearrange("p o t -> p (o t)")
                              ).then_inc(sig["yidx", s], 1)
                e.wait_ge(sig["yidx", s], k + 1)
                apart(e)
                for t in range(QT):
                    for k in range(TOPK[L]):
                        e.indirect_dma_start(
                            out=ygath[s][:, t * 4 + k, :], out_offset=None, in_=ysort,
                            in_offset=bass.IndirectOffsetOnAxis(
                                ap=yidx[s][:, t * 4 + k:t * 4 + k + 1], axis=0),
                        ).then_inc(sig["ga", s], 16)

            def attention_phase(L):
                def rstds(u, s, k):
                    e.wait_ge(sig["var", s], at("var", L, u, k))
                    e.tensor_tensor(rstd[s][:], ve[s][:], cc(C_MH, 2), ALU.pow).then_inc(sig["rstd", s], 1)

                def add_bo(u, s):
                    e.wait_ge(sig["ld", s], at("ld", L, u))
                    e.wait_ge(sig["x1", s], at("x1", L, u, 0))
                    e.tensor_tensor(xb[s], XL[s][:], bc(bo_bc[:], 1, QT), ALU.add
                                    ).then_inc(sig["xb", s], 1)

                def scatter_rows(u, s):
                    e.wait_ge(sig["slots", s], at("slots", L, u))
                    apart(e)
                    scatter(L, s)

                def gather_rows(u, s):
                    if not (isinstance(u, int) and u < 0):
                        e.wait_ge(sig["var", s], at("var", L, u, 1))
                    gather(0, s, u + 1, u + 1)

                stages = {"rstd1": lambda u, s: rstds(u, s, 1), "rstd2": lambda u, s: rstds(u, s, 2),
                          "scatter": scatter_rows}
                stages.update({"xb": add_bo} if L == 0 else {"gather": gather_rows})
                if L == 1:
                    for s in range(2):
                        gather_rows(-1, s)
                rstds(0, 0, 1)
                if L == 0:
                    add_bo(0, 0)
                else:
                    gather_rows(0, 0)
                run_halves(e, "Pool", stages)
                for s in range(2):
                    e.wait_ge(sig["sc", s], at("sc", L, NIT - 1))
                    if L == 1:
                        e.wait_ge(sig["ga", s], at("ga", L, NIT))

            for L in range(2):
                attention_phase(L)
                for k in range(3):
                    end_phase(e, 3 * L + 1 + k)
                    if k == 1:
                        all_rows()
            for s in range(2):
                gather(1, s, 0, NIT + 1)
            with e.Fori(1, NIT) as u:
                for s in range(2):
                    e.wait_ge(fin[s], u)
                    gather(1, s, u, NIT + 1 + u)

        @block.scalar
        def _(e):
            count_regs = [e.alloc_register(f"count{r}") for r in range(4)]

            def fill_up(L):
                e.wait_ge(tb_s, TBN * L + 1)
                apart(e)
                for x in range(0, E, 4):
                    e.load(count_regs, cnti[0:1, x:x + 4])
                    for r in range(4):
                        c = e.snap(count_regs[r], min_val=0, max_val=NTOK)
                        e.dma_start(xsort[bass.ds(c + (x + r) * REG, P), :], zero[:]).then_inc(zfill, 16)
                e.wait_ge(zfill, 16 + 16 * E * (L + 1))

            def attention_phase(L):
                e.wait_ge(w_small, NSMALL)

                def copy_xnT(u, s, k):
                    e.wait_ge(sig["xnT_ps", s], at("xnT_ps", L, u, k))
                    e.activation(xnT[s][:], ps[:, 4 * s, :].rearrange("p (c q) -> p c q", c=DC),
                                 ACT.Copy).then_inc(sig["xnT", s], 1)

                def keys(u, s):
                    e.wait_ge(sig["K_ps", s], at("K_ps", L, u))
                    for j in range(G):
                        rows = slice(j * HP, (j + 1) * HP)
                        ins = e.activation(KB[s][rows, :, j, :], ps[rows, 4 * s + 3, 0:HT * LK].rearrange(
                            "p (i k) -> p i k", i=HT), ACT.Copy)
                    ins.then_inc(sig["KB", s], 1)

                def queries(u, s, half):
                    e.wait_ge(sig["Q_ps", s], at("Q_ps", L, u, half + 1))
                    if L == 0:
                        ins = e.activation(Q[s][:, 2 * half:2 * half + 2, :],
                                           ps[:, 4 * s + 1 - half, :].rearrange("p (i q) -> p i q", i=2),
                                           ACT.Copy)
                    else:
                        for i in range(2 * half, 2 * half + 2):
                            ins = e.activation(
                                Q[s][:, i, :], ps[:, 4 * s + 1 - half, i % 2 * LQ:(i % 2 + 1) * LQ],
                                ACT.Identity, bias=bq[L][:, i:i + 1])
                    ins.then_inc(sig["Q", s], 1)

                def exps(u, s, i):
                    e.wait_ge(sig["smax", s], at("smax", L, u, i + 1))
                    for t in range(QT):
                        for j in range(G):
                            ins = e.activation(prob[s][i][:, t, j, :],
                                               ps[:, sbank(s, i) + t, j * LK:(j + 1) * LK],
                                               ACT.Exp, bias=nmx[s][:, i, t, j:j + 1], scale=SCALE)
                    ins.then_inc(sig["Pr", s], 1)

                def copy_PT(u, s, i):
                    e.wait_ge(sig["PT_ps", s], at("PT_ps", L, u, i + 1))
                    e.activation(W[s][0:LK, G * i:G * (i + 1), :],
                                 ps[0:LK, sbank(s, i):sbank(s, i) + 2, :].rearrange(
                                     "p k (h q) -> p (k h) q", h=2), ACT.Copy).then_inc(sig["PT", s], 1)

                def outputs_T(u, s):
                    e.wait_ge(sig["OT_ps", s], at("OT_ps", L, u))
                    e.activation(Q[s][:], ps[:, 4 * s + 2:4 * s + 4, :].rearrange(
                        "p k (i q) -> p (k i) q", i=2), ACT.Copy).then_inc(sig["OT", s], 1)

                def outputs_nT(u, s):
                    e.wait_ge(sig["OnT_ps", s], at("OnT_ps", L, u))
                    e.activation(xnT[s][:], ps[:, 4 * s + 2, :].rearrange(
                        "p (c q) -> p c q", c=DC), ACT.Copy).then_inc(sig["OnT", s], 1)

                def logits(u, s):
                    lg = ps[:, 4 * s + 1, 0:QT * E].rearrange("p (t e) -> p t e", t=QT)
                    e.wait_ge(sig["lg", s], at("lg", L, u))
                    if L == 0:
                        e.activation(th[s][:], lg, ACT.Tanh, scale=0.5).then_inc(sig["th", s], 1)
                    else:
                        e.wait_ge(sig["nm", s], at("nm", L, u))
                        for t in range(QT):
                            ins = e.activation(th[s][:, t, :], lg[:, t, :], ACT.Exp,
                                               bias=rt[s][:, t:t + 1])
                        ins.then_inc(sig["th", s], 1)

                def gates(u, s):
                    e.wait_ge(sig["GU", s], at("GU", L, u))
                    e.activation(W[s][:, 0:2, :], ps[:, 4 * s + 2, :].rearrange(
                        "p (c q) -> p c q", c=2), ACT.Tanh, scale=0.5).then_inc(sig["TH", s], 1)

                stages = {"OT": outputs_T, "xnT1": lambda u, s: copy_xnT(u, s, 1), "KB": keys,
                          "xnT2": lambda u, s: copy_xnT(u, s, 2), "th": logits, "TH": gates,
                          "Q0": lambda u, s: queries(u, s, 0), "Q1": lambda u, s: queries(u, s, 1)}
                for i in range(HT):
                    stages[f"exp{i}"] = lambda u, s, i=i: exps(u, s, i)
                    stages[f"PT{i}"] = lambda u, s, i=i: copy_PT(u, s, i)
                if L == 0:
                    stages["OnT"] = outputs_nT
                keys(0, 0)
                run_halves(e, "ACT", stages)

            def expert_phase(L):
                def step(n, r, w, c2):
                    edge = isinstance(n, int)
                    if not (edge and n >= NT[L]):
                        _, h, c = tile(0, r, w, c2)
                        e.wait_ge(eT_ps[h], c)
                        e.activation(xtT[r % 2], ps[:, r % 2, 0:D].rearrange("p (c q) -> p c q", c=DC),
                                     ACT.Copy).then_inc(eT[h], 1)
                    if not (edge and (n < 1 or n > NT[L])):
                        _, h, c = tile(1, r, w, c2)
                        e.wait_ge(eGU[h], c)
                        e.activation(hg[h], ps[:, 2 + h, 0:F], ACT.Silu).then_inc(eG[h], 1)

                run_steps(e, L, step)

            for L in range(2):
                attention_phase(L)
                end_phase(e, 3 * L + 1)
                fill_up(L)
                end_phase(e, 3 * L + 2)
                expert_phase(L)
                end_phase(e, 3 * L + 3)

        @block.vector
        def _(e):
            count = {}

            def link(ins, c, s, L, u):
                k = count[c, s] = count.get((c, s), 0) + 1
                ins.then_inc(sig[c, s], 1)
                e.wait_ge(sig[c, s], at(c, L, u, k))

            def link_apart(ins, c, s, L, u):
                link(ins, c, s, L, u)
                apart(e)

            for s in range(2):
                e.memset(rt[s][:], -BIG)
            e.memset(cnt[:], 0.0)
            e.memset(tab[:], 0)
            e.wait_ge(init, 3)
            for s in range(2):
                e.memset(V[s][:, :, HD:HD + 1], 1.0)
            e.wait_ge(w_small, NSMALL)
            e.tensor_copy(tri16[:], cc(C_TRI, 2 * P)).then_inc(init, 1)
            e.tensor_scalar(mask_f[:], mask_i[:], 0.0, -BIG, ALU.is_gt, ALU.mult).then_inc(init, 1)

            def combine(s, acc, lk, K):
                for k in range(K):
                    for t in range(QT):
                        c = t * 4 + k
                        ins = e.scalar_tensor_tensor(out=acc[s][:, t, :], in0=ygath[s][:, c, :],
                                                     scalar=mg[s][:, 0, c:c + 1], in1=acc[s][:, t, :],
                                                     op0=ALU.mult, op1=ALU.add)
                        if t == QT - 1 and k < K - 1:
                            lk(ins)
                return ins

            def attention_phase(L):
                def stats(c, u, s, x):
                    for t in range(QT):
                        ins = e.bn_stats(st6[s][:, t, :], x[s][:, t, :])
                    link_apart(ins, c, s, L, u)
                    for t in range(QT):
                        ins = e.bn_aggr(mv[s][:, t, :], st6[s][:, t, :])
                    link(ins, c, s, L, u)
                    e.tensor_scalar(ve[s][:], mv[s][:, :, 1], EPS, None, ALU.add
                                    ).then_inc(sig["var", s], 1)

                def norm(c, u, s, x, dst, k):
                    e.wait_ge(sig["rstd", s], at("rstd", L, u, k))
                    link(e.scalar_tensor_tensor(out=nmr[s][:], in0=mv[s][:, :, 0], scalar=-1.0,
                                                in1=rstd[s][:], op0=ALU.mult, op1=ALU.mult), c, s, L, u)
                    for t in range(QT):
                        ins = e.tensor_scalar(dst[:, t, :], x[s][:, t, :], rstd[s][:, t:t + 1],
                                              nmr[s][:, t:t + 1], ALU.mult, ALU.add)
                    ins.then_inc(sig["xn", s], 1)

                def ln1(u, s):
                    count["c_ln", s] = 0
                    lk = lambda i: link(i, "c_ln", s, L, u)
                    e.wait_ge(sig["ld", s], at("ld", L, u))
                    if L == 1:
                        e.wait_ge(sig["ga", s], at("ga", L, u))
                        lk(e.tensor_copy(mg[s][:], meta[:, bass.ds(u * 2 + s, 1)].rearrange("p o k t -> p (o k) t")))
                        lk(combine(s, XL, lk, TOPK[0]))
                    stats("c_ln", u, s, XL)

                def xn1(u, s):
                    norm("c_ln", u, s, XL, xn[s], 1)
                    assert count["c_ln", s] == PER["c_ln"][L], count

                def values(u, s):
                    e.wait_ge(sig["V_ps", s], at("V_ps", L, u))
                    v_ps = ps[0:LK, 4 * s + 2, 0:D].rearrange("p (h c) -> p h c", h=H)
                    if L == 0:
                        ins = e.tensor_copy(V[s][:, :, 0:HD], v_ps)
                    else:
                        ins = e.tensor_tensor(V[s][:, :, 0:HD], v_ps,
                                              bv_bc[0:LK, :].rearrange("p (h c) -> p h c", h=H), ALU.add)
                    ins.then_inc(sig["V", s], 1)

                def maxima(u, s, i):
                    if i == 0:
                        count["c_sm", s] = 0
                    e.wait_ge(sig["S", s], at("S", L, u, i + 1))
                    link(e.tensor_reduce(
                        mx[s][:, i], ps[:, sbank(s, i):sbank(s, i) + 2, 0:G * LK].rearrange(
                            "p t (j c) -> p t j c", j=G), AX.X, ALU.max), "c_sm", s, L, u)
                    e.tensor_scalar(nmx[s][:, i], mx[s][:, i], -SCALE, None, ALU.mult
                                    ).then_inc(sig["smax", s], 1)

                def outputs(u, s):
                    count["c_at", s] = 0
                    e.wait_ge(sig["O_ps", s], at("O_ps", L, u))
                    o_ps = ps[:, 4 * s:4 * s + 2, :].rearrange("p t (h c) -> p t h c", c=HP)
                    link(e.reciprocal(rsum[s][:], o_ps[:, :, :, SUM]), "c_at", s, L, u)
                    o = O[s][:].rearrange("p t (h c) -> p t h c", c=HD)
                    ins = e.tensor_tensor(o, o_ps[:, :, :, 0:HD], bc(rsum[s][:], 3, HD), ALU.mult)
                    if L == 0:
                        ins.then_inc(sig["O", s], 1)
                    else:
                        link(ins, "c_at", s, L, u)
                        e.tensor_tensor(X[s][:], XL[s][:], O[s][:], ALU.add).then_inc(sig["O", s], 1)

                def x1(u, s):
                    if L == 0:
                        e.wait_ge(sig["Wo", s], at("Wo", L, u))
                        e.wait_ge(sig["xb", s], at("xb", L, u))
                        e.tensor_tensor(X[s][:], ps[:, 4 * s + 3, :].rearrange("p (t d) -> p t d", t=QT),
                                        xb[s], ALU.add).then_inc(sig["x1", s], 1)
                        e.wait_ge(sig["x1", s], at("x1", L, u))
                    else:
                        e.wait_ge(sig["O", s], at("O", L, u))
                    stats("c_at", u, s, X)

                def xn2s(u, s):
                    e.wait_ge(sig["sc", s], at("sc", L, u, 0))
                    norm("c_at", u, s, X, xn2[s], 2)

                def greatest_logit(u, s):
                    e.wait_ge(sig["lg", s], at("lg", L, u))
                    apart(e)
                    for t in range(QT):
                        ins = e.max(rt[s][:, 16 + 8 * t:24 + 8 * t], ps[:, 4 * s + 1, t * E:(t + 1) * E])
                    link(ins, "c_at", s, L, u)
                    e.tensor_scalar(rt[s][:, 0:2],
                                    rt[s][:, 16:32].rearrange("p (t m) -> p t m", t=2)[:, :, 0],
                                    -1.0, None, ALU.mult).then_inc(sig["nm", s], 1)

                def hidden(u, s):
                    e.wait_ge(sig["TH", s], at("TH", L, u))
                    g_ps = ps[:, 4 * s + 2, :].rearrange("p (c q) -> p c q", c=2)
                    u_ps = ps[:, 4 * s + 3, :].rearrange("p (c q) -> p c q", c=2)
                    link(e.scalar_tensor_tensor(out=W[s][:, 2:4, :], in0=W[s][:, 0:2, :], scalar=1.0,
                                                in1=g_ps, op0=ALU.add, op1=ALU.mult), "c_at", s, L, u)
                    e.scalar_tensor_tensor(out=W[s][:, 4:6, :], in0=W[s][:, 2:4, :], scalar=0.5,
                                           in1=u_ps, op0=ALU.mult, op1=ALU.mult
                                           ).then_inc(sig["HS", s], 1)

                def base(u, s):
                    e.wait_ge(sig["SH", s], at("SH", L, u))
                    e.wait_ge(sig["st", s], at("st", L, u, 0))
                    sh = ps[:, 4 * s, :].rearrange("p (t d) -> p t d", t=QT)
                    if L == 0:
                        link(e.tensor_tensor(XO[s][:], sh, X[s][:], ALU.add), "c_at", s, L, u)
                        e.tensor_tensor(XO[s][:], XO[s][:], xn2[s][:], ALU.add).then_inc(sig["base", s], 1)
                    else:
                        e.tensor_tensor(XO[s][:], sh, X[s][:], ALU.add).then_inc(sig["base", s], 1)
                    assert count["c_at", s] == PER["c_at"][L], count

                def choose(u, s):
                    count["c_rt", s] = 0
                    e.wait_ge(sig["th", s], at("th", L, u))
                    choose_experts(L, u, s)

                def place(u, s):
                    place_rows(L, u, s)
                    assert count["c_rt", s] == PER["c_rt"][L], count

                stages = {
                    "out": outputs, "V": values, "x1": x1, "xn2": xn2s, "HS": hidden,
                    "ln1": ln1, "choose": choose, "weigh": lambda u, s: weigh_experts(L, u, s),
                    "xn1": xn1, "base": base, "place": place,
                }
                for i in range(HT):
                    stages[f"max{i}"] = lambda u, s, i=i: maxima(u, s, i)
                if L == 1:
                    stages["nm"] = greatest_logit
                ln1(0, 0)
                xn1(0, 0)
                values(0, 0)
                run_halves(e, "DVE", stages)

            def choose_experts(L, u, s):
                K = TOPK[L]
                r = rt[s]
                lk = lambda i: link(i, "c_rt", s, L, u)
                lka = lambda i: link_apart(i, "c_rt", s, L, u)
                tv = r[:, 32:48].rearrange("p (t m) -> p t m", t=QT)
                oh = r[:, 256:256 + QT * 4 * E].rearrange("p (t k e) -> p t k e", t=QT, k=4)[:, :, 0:K, :]
                tmp = r[:, 384:384 + QT * 4 * E].rearrange("p (t k e) -> p t k e", t=QT, k=4)[:, :, 0:K, :]
                wk_, sk_, ek_ = (mt[s][:, i, :].rearrange("p (t k) -> p t k", t=QT)[:, :, 0:K] for i in range(3))
                iota = cc(C_IOTA, E)
                if L == 0:
                    sc = r[:, 48:80].rearrange("p (t e) -> p t e", t=QT)
                    sfc = r[:, 80:112].rearrange("p (t e) -> p t e", t=QT)
                    lk(e.tensor_scalar(sc, th[s][:], 0.5, 0.5, ALU.mult, ALU.add))
                    lk(e.tensor_tensor(sfc, sc, bc(gbias[:], 1, QT), ALU.add))
                    g4 = r[:, 80:112].rearrange("p (g m) -> p g m", m=4)
                    pr = r[:, 112:160].rearrange("p (g m) -> p g m", m=6)
                    e.tensor_tensor(pr[:, :, 0:3], g4[:, :, 0:3], g4[:, :, 1:4], ALU.add)
                    e.tensor_tensor(pr[:, :, 3:5], g4[:, :, 0:2], g4[:, :, 2:4], ALU.add)
                    lk(e.tensor_tensor(pr[:, :, 5:6], g4[:, :, 0:1], g4[:, :, 3:4], ALU.add))
                    gs = r[:, 160:176].rearrange("p (t m) -> p t m", t=QT)
                    lka(e.tensor_reduce(gs[:, :, 0:NG], pr.rearrange("p (t g) m -> p t g m", t=QT), AX.X, ALU.max))
                    gm = r[:, 176:192].rearrange("p (t m) -> p t m", t=QT)
                    for t in range(QT):
                        ins = e.max(gm[:, t, :], gs[:, t, :])
                    lka(ins)
                    for t in range(QT):
                        ins = e.max_index(ru[s][:, t, :], gm[:, t, :], gs[:, t, :])
                    lk(ins)
                    gi = r[:, 192:196].rearrange("p (t m) -> p t m", t=QT)
                    lk(e.tensor_copy(gi, ru[s][:, :, 0:2]))
                    eq = r[:, 196:212].rearrange("p (t m g) -> p t m g", t=QT, m=2)
                    lk(e.tensor_tensor(eq, bc(gi, 3, NG), bc(bc(iota[:, 0:NG], 1, 2), 1, QT), ALU.is_equal))
                    sel = r[:, 212:220].rearrange("p (t g) -> p t g", t=QT)
                    lk(e.tensor_tensor(sel, eq[:, :, 0, :], eq[:, :, 1, :], ALU.add))
                    lk(e.tensor_scalar(sel, sel, 2 * BIG, -BIG, ALU.mult, ALU.add))
                    mk = r[:, 220:252].rearrange("p (t g m) -> p t g m", t=QT, m=4)
                    lka(e.tensor_tensor(mk, sfc.rearrange("p t (g m) -> p t g m", m=4), bc(sel, 3, 4), ALU.min))
                    mk = r[:, 220:252].rearrange("p (t e) -> p t e", t=QT)
                else:
                    sc = r[:, 48:80].rearrange("p (t e) -> p t e", t=QT)
                    lk(e.tensor_reduce(r[:, 4:6], th[s][:], AX.X, ALU.add))
                    lk(e.reciprocal(r[:, 6:8], r[:, 4:6]))
                    lka(e.tensor_tensor(sc, th[s][:], bc(r[:, 6:8], 2, E), ALU.mult))
                    mk = sc
                for t in range(QT):
                    ins = e.max(tv[:, t, :], mk[:, t, :])
                lka(ins)
                for t in range(QT):
                    ins = e.max_index(ru[s][:, t, :], tv[:, t, :], mk[:, t, :])
                lk(ins)
                lk(e.tensor_copy(ek_, ru[s][:, :, 0:K]))
                lk(e.tensor_tensor(oh, bc(ek_, 3, E), bc(bc(iota, 1, K), 1, QT), ALU.is_equal))
                with nc.allow_low_precision(reason="a sum of at most one 1"):
                    e.tensor_reduce(m16[s][:], oh.rearrange("p t k e -> p t e k"), AX.X, ALU.add
                                    ).then_inc(sig["mask", s], 1)

            def weigh_experts(L, u, s):
                K = TOPK[L]
                r = rt[s]
                lk = lambda i: link(i, "c_rt", s, L, u)
                tv = r[:, 32:48].rearrange("p (t m) -> p t m", t=QT)
                oh = r[:, 256:256 + QT * 4 * E].rearrange("p (t k e) -> p t k e", t=QT, k=4)[:, :, 0:K, :]
                tmp = r[:, 384:384 + QT * 4 * E].rearrange("p (t k e) -> p t k e", t=QT, k=4)[:, :, 0:K, :]
                wk_ = mt[s][:, 0, :].rearrange("p (t k) -> p t k", t=QT)[:, :, 0:K]
                sc = r[:, 48:80].rearrange("p (t e) -> p t e", t=QT)
                if L == 0:
                    lk(e.tensor_tensor(tmp, oh, bc(sc, 2, K), ALU.mult))
                    lk(e.tensor_reduce(wk_, tmp, AX.X, ALU.add))
                    lk(e.tensor_reduce(r[:, 4:6], wk_, AX.X, ALU.add))
                    lk(e.tensor_scalar(r[:, 4:6], r[:, 4:6], 1e-20, None, ALU.add))
                    lk(e.reciprocal(r[:, 6:8], r[:, 4:6]))
                    lk(e.scalar_tensor_tensor(out=wk_, in0=wk_, scalar=ROUTED_SCALE, in1=bc(r[:, 6:8], 2, K),
                                              op0=ALU.mult, op1=ALU.mult))
                else:
                    lk(e.tensor_copy(wk_, tv[:, :, 0:K]))

            def place_rows(L, u, s):
                K = TOPK[L]
                r = rt[s]
                lk = lambda i: link(i, "c_rt", s, L, u)
                lka = lambda i: link_apart(i, "c_rt", s, L, u)
                oh = r[:, 256:256 + QT * 4 * E].rearrange("p (t k e) -> p t k e", t=QT, k=4)[:, :, 0:K, :]
                tmp = r[:, 384:384 + QT * 4 * E].rearrange("p (t k e) -> p t k e", t=QT, k=4)[:, :, 0:K, :]
                sk_ = mt[s][:, 1, :].rearrange("p (t k) -> p t k", t=QT)[:, :, 0:K]
                pos = r[:, 48:80].rearrange("p (t e) -> p t e", t=QT)
                e.wait_ge(sig["rank", s], at("rank", L, u))
                cbase = 2 * NIT * L
                e.wait_ge(cnt_s, cbase + u * 2 + s)
                lk(e.tensor_tensor(pos, ps[:, 4 * s + 1, 64:96].rearrange("p (t e) -> p t e", t=QT),
                                   bc(cnt[:], 1, QT), ALU.add))
                e.tensor_tensor(cnt[:], ps[:, 4 * s + 1, 96:112], cnt[:], ALU.add).then_inc(cnt_s, 1)
                lk(e.tensor_tensor(pos, pos, bc(cc(C_EBASE, E), 1, QT), ALU.add))
                lk(e.tensor_tensor(tmp, oh, bc(pos, 2, K), ALU.mult))
                lka(e.tensor_reduce(sk_, tmp, AX.X, ALU.add))
                lk(e.tensor_copy(meta[:, bass.ds(u * 2 + s, 1)].rearrange("p o k t -> p (o k) t"), mt[s][:]))
                e.tensor_copy(xidx[s][:].rearrange("p (t k) -> p t k", t=QT)[:, :, 0:K], sk_
                              ).then_inc(sig["slots", s], 1)

            def tables(L):
                n = [TBN * L]

                def lk(ins):
                    n[0] += 1
                    ins.then_inc(tb_s, 1)
                    e.wait_ge(tb_s, n[0])

                nt, ci = tb[:, 0:E], tb[:, E:2 * E]
                et, ct = tb[:, 32:35], tb[:, 35:38]
                low = cc(C_LOW, E * E).rearrange("p (e f) -> p e f", f=E)
                big = rt[0][:, 0:0]
                cmpb = ygath[0][:].rearrange("p k d -> p (k d)")[:, 0:E * 64].rearrange("p (e j) -> p e j", j=64)
                sq = ygath[0][:].rearrange("p k d -> p (k d)")[:, 1024:1280].rearrange("p (e f) -> p e f", f=E)
                le = tb[:, 64:112].rearrange("p (c e) -> p c e", e=E)
                ln = tb[:, 112:160].rearrange("p (c e) -> p c e", e=E)
                tt = cc(C_T, 3)
                lk(e.tensor_copy(cnti[:], cnt[:]))
                lk(e.tensor_tensor(cmpb, bc(cnt[:], 2, 64), bc(cc(C_J128, 64), 1, E), ALU.is_gt))
                lk(e.tensor_reduce(nt, cmpb, AX.X, ALU.add))
                lk(e.tensor_tensor(sq, low, bc(nt, 1, E), ALU.mult))
                lk(e.tensor_reduce(ci, sq, AX.X, ALU.add))
                lk(e.tensor_tensor(le, bc(ci, 1, 3), bc(tt, 2, E), ALU.is_le))
                lk(e.tensor_tensor(ln, le, bc(nt, 1, 3), ALU.mult))
                lk(e.tensor_reduce(et, le, AX.X, ALU.add))
                lk(e.tensor_reduce(ct, ln, AX.X, ALU.add))
                lk(e.tensor_tensor(ct, tt, ct, ALU.subtract))
                lk(e.tensor_scalar(tb[:, 38:41], et, float(REG), None, ALU.mult))
                lk(e.scalar_tensor_tensor(out=tbo[:, 0, :], in0=ct, scalar=float(P), in1=tb[:, 38:41],
                                          op0=ALU.mult, op1=ALU.add))
                lk(e.tensor_scalar(tbo[:, 1, :], et, float(E - 1), None, ALU.min))
                lk(e.tensor_tensor(delta[:], ci, nt, ALU.subtract))
                lk(e.scalar_tensor_tensor(out=delta[:], in0=delta[:], scalar=float(P), in1=cc(C_EBASE, E),
                                          op0=ALU.mult, op1=ALU.subtract))
                lk(e.memset(cnt[:], 0.0))
                assert n[0] == TBN * (L + 1), n

            def expert_phase(L):
                def step(n, r, w, c2):
                    edge = isinstance(n, int)
                    if not (edge and (n < 1 or n > NT[L])):
                        _, h, c = tile(1, r, w, c2)
                        e.wait_ge(eG[h], c)
                        e.tensor_tensor(hm[h], hg[h], ps[:, 2 + h, F:2 * F], ALU.mult
                                        ).then_inc(eH[h], 1)
                    if not (edge and n < 3):
                        q, h, c = tile(3, r, w, c2)
                        e.wait_ge(eD[h], c)
                        if q % 2 == 0 and not (edge and n < 7 and L == 0):
                            e.wait_ge(yst[q // 2], (w if r == 3 else w - 1) * 16)
                        e.tensor_copy(yt[q], ps[:, 6 + h, 0:D]).then_inc(eY[h], 1)
                    if not (edge and (n < 2 or n > NT[L] + 1)):
                        _, h, c = tile(2, r, w, c2)
                        e.wait_ge(eHT_ps[h], c)
                        e.tensor_copy(hT[h], ps[:, 4 + h, 0:P]).then_inc(eHT[h], 1)

                run_steps(e, L, step)

            for L in range(2):
                attention_phase(L)
                end_phase(e, 3 * L + 1)
                tables(L)
                end_phase(e, 3 * L + 2)
                expert_phase(L)
                end_phase(e, 3 * L + 3)

            with e.Fori(0, NIT) as u:
                num = [0, 0]

                def lkf(s):
                    def f(ins):
                        num[s] += 1
                        ins.then_inc(sig["c_ln", s], 1)
                        e.wait_ge(sig["c_ln", s], ended("c_ln", s) + u * C1N + num[s])
                    return f

                for s in range(2):
                    e.wait_ge(sig["ld", s], ended("ld", s) + 16 * (u + 1))
                    e.wait_ge(sig["ga", s], ended("ga", s) + 64 * (u + 1))
                    lkf(s)(e.tensor_copy(mg[s][:], meta[:, bass.ds(u * 2 + s, 1)].rearrange("p o k t -> p (o k) t")))
                    combine(s, X, lkf(s), TOPK[1]).then_inc(fin[s], 1)
                assert num[0] == C1N, num

        @block.tensor
        def _(e):
            gate_regs = [e.alloc_register(f"gate_expert{r}") for r in range(4)]
            down_regs = [e.alloc_register(f"down_expert{r}") for r in range(4)]

            def attention_phase(L):
                e.wait_ge(init, 5)
                e.wait_ge(w_small, NSMALL)
                if L == 1:
                    e.wait_ge(w_small1, NSMALL1)

                def transpose_x(u, s, src, k):
                    e.wait_ge(sig["xn", s], at("xn", L, u, k))
                    for t in range(QT):
                        for c in range(DC):
                            mm = e.transpose(ps[:, 4 * s, c * LQ + t * P:c * LQ + (t + 1) * P],
                                             src[:, t, c * P:(c + 1) * P], ident)
                    mm.then_inc(sig["xnT_ps", s], 1)

                def T1(u, s):
                    e.wait_ge(sig["base", s], at("base", L, u, 0))
                    transpose_x(u, s, xn[s], 1)

                def KV(u, s):
                    k0 = 4 * s
                    e.wait_ge(sig["ld", s], at("ld", L, u))
                    for i in range(HT):
                        for c in range(DC):
                            mm = e.matmul(ps[:, k0 + 3, i * LK:(i + 1) * LK],
                                          wk[:, c, i * P:(i + 1) * P], ctxT[s][:, c, :],
                                          start=(c == 0), stop=(c == DC - 1 and L == 0))
                        if L == 1:
                            mm = e.matmul(ps[:, k0 + 3, i * LK:(i + 1) * LK],
                                          kaug[:, i * P:(i + 1) * P], mrow[s][:], start=False, stop=True)
                    mm.then_inc(sig["K_ps", s], 1)
                    for c in range(DC):
                        mm = e.matmul(ps[0:LK, k0 + 2, 0:D], ctxT[s][:, c, :], wv[:, c, :],
                                      start=(c == 0), stop=(c == DC - 1))
                    mm.then_inc(sig["V_ps", s], 1)

                def project_q(u, s, half):
                    if half == 0:
                        e.wait_ge(sig["xnT", s], at("xnT", L, u, 1))
                        e.wait_ge(sig["slots", s], at("slots", L, u, 0))
                    for i in range(2 * half, 2 * half + 2):
                        for c in range(DC):
                            mm = e.matmul(ps[:, 4 * s + 1 - half, i % 2 * LQ:(i % 2 + 1) * LQ],
                                          wq[:, c, i * P:(i + 1) * P], xnT[s][:, c, :],
                                          start=(c == 0), stop=(c == DC - 1))
                    mm.then_inc(sig["Q_ps", s], 1)

                def S(u, s, i):
                    if i == 0:
                        e.wait_ge(sig["KB", s], at("KB", L, u))
                        e.wait_ge(sig["V", s], at("V", L, u))
                    if i < 2:
                        e.wait_ge(sig["Q", s], at("Q", L, u, i + 1))
                    if i >= 2:
                        e.wait_ge(sig["Pr", s], at("Pr", L, u, i - 1))
                    for t in range(QT):
                        mm = e.matmul(ps[:, sbank(s, i) + t, 0:G * LK], Q[s][:, i, t * P:(t + 1) * P],
                                      KB[s][:, i, :, :].rearrange("p j k -> p (j k)"),
                                      start=True, stop=True)
                    mm.then_inc(sig["S", s], 1)

                def PT(u, s, i):
                    if i < 2:
                        e.wait_ge(sig["Pr", s], at("Pr", L, u, i + 3))
                    else:
                        e.wait_ge(sig["PT", s], at("PT", L, u, i - 1))
                    for j in range(G):
                        for t in range(QT):
                            col = j % 2 * LQ + t * P
                            mm = e.transpose(ps[0:LK, sbank(s, i) + j // 2, col:col + P],
                                             prob[s][i][:, t, j, :], ident)
                    mm.then_inc(sig["PT_ps", s], 1)

                def PV(u, s):
                    e.wait_ge(sig["PT", s], at("PT", L, u, 3))
                    for i in range(HT):
                        if i == HT - 1:
                            e.wait_ge(sig["PT", s], at("PT", L, u, 4))
                        for j in range(G):
                            h = G * i + j
                            mm = e.matmul(
                                ps[j * HP:(j + 1) * HP, 4 * s + 2 + i // 2, i % 2 * LQ:(i % 2 + 1) * LQ],
                                V[s][:, h, :], W[s][0:LK, h, :], start=True, stop=True)
                    mm.then_inc(sig["OT_ps", s], 1)

                def OX(u, s):
                    e.wait_ge(sig["OT", s], at("OT", L, u))
                    for t in range(QT):
                        for i in range(HT):
                            mm = e.transpose(ps[:, 4 * s + t, i * P:(i + 1) * P],
                                             Q[s][:, i, t * P:(t + 1) * P], ident)
                    mm.then_inc(sig["O_ps", s], 1)

                def OT2(u, s):
                    e.wait_ge(sig["O", s], at("O", L, u))
                    for t in range(QT):
                        for c in range(DC):
                            mm = e.transpose(ps[:, 4 * s + 2, c * LQ + t * P:c * LQ + (t + 1) * P],
                                             O[s][:, t, c * P:(c + 1) * P], ident)
                    mm.then_inc(sig["OnT_ps", s], 1)

                def Wo(u, s):
                    e.wait_ge(sig["OnT", s], at("OnT", L, u))
                    for t in range(QT):
                        for c in range(DC):
                            mm = e.matmul(ps[:, 4 * s + 3, t * D:(t + 1) * D],
                                          xnT[s][:, c, t * P:(t + 1) * P], wo[:, c, :],
                                          start=(c == 0), stop=(c == DC - 1))
                    mm.then_inc(sig["Wo", s], 1)

                def T2(u, s):
                    e.wait_ge(sig["O", s], at("O", L, u))
                    transpose_x(u, s, xn2[s], 2)

                def GU(u, s):
                    e.wait_ge(sig["xnT", s], at("xnT", L, u, 2))
                    for t in range(QT):
                        for c in range(DC):
                            mm = e.matmul(ps[:, 4 * s + 1, t * E:(t + 1) * E],
                                          xnT[s][:, c, t * P:(t + 1) * P], gw[L][:, c, :],
                                          start=(c == 0), stop=(c == DC - 1))
                    mm.then_inc(sig["lg", s], 1)
                    for m in range(4):
                        for c in range(DC):
                            mm = e.matmul(ps[:, 4 * s + 2 + m // 2, m % 2 * LQ:(m % 2 + 1) * LQ],
                                          wsgu[:, c, m * P:(m + 1) * P], xnT[s][:, c, :],
                                          start=(c == 0), stop=(c == DC - 1))
                    mm.then_inc(sig["GU", s], 1)

                def SH(u, s):
                    e.wait_ge(sig["HS", s], at("HS", L, u))
                    for t in range(QT):
                        for c in range(2):
                            mm = e.matmul(ps[:, 4 * s, t * D:(t + 1) * D],
                                          W[s][:, 4 + c, t * P:(t + 1) * P], wsd[:, c, :],
                                          start=(c == 0), stop=(c == 1))
                    mm.then_inc(sig["SH", s], 1)

                def rank(u, s):
                    e.wait_ge(sig["mask", s], at("mask", L, u))
                    e.wait_ge(sig["th", s], at("th", L, u))
                    tri, one = tri16[:, 0:P], tri16[:, P:2 * P]
                    bank = ps[:, 4 * s + 1, :]
                    e.matmul(bank[:, 64:80], tri, m16[s][:, 0, :], start=True, stop=True)
                    e.matmul(bank[:, 80:96], tri, m16[s][:, 1, :], start=True, stop=False)
                    e.matmul(bank[:, 80:96], one, m16[s][:, 0, :], start=False, stop=True)
                    e.matmul(bank[:, 96:112], one, m16[s][:, 0, :], start=True, stop=False)
                    e.matmul(bank[:, 96:112], one, m16[s][:, 1, :], start=False, stop=True
                             ).then_inc(sig["rank", s], 1)

                stages = {
                    "PV": PV, "T1": T1, "OX": OX, "KV": KV, "T2": T2, "GU": GU, "SH": SH, "rank": rank,
                }
                for i in range(HT):
                    stages[f"S{i}"] = lambda u, s, i=i: S(u, s, i)
                    stages[f"PT{i}"] = lambda u, s, i=i: PT(u, s, i)
                for half in range(2):
                    stages[f"Q{half}"] = lambda u, s, half=half: project_q(u, s, half)
                if L == 0:
                    stages.update({"OT2": OT2, "Wo": Wo})
                KV(0, 0)
                run_halves(e, "PE", stages)

            def expert_phase(L):
                def experts(n, regs):
                    e.load(regs, tab[0:1, 1, bass.ds(n, 4)])
                    return [e.snap(x, min_val=0, max_val=E - 1) for x in regs]

                tile_experts = [None, None]

                def step(n, r, w, c2):
                    edge = isinstance(n, int)
                    if r == 0:
                        tile_experts[:] = experts(n + 2, gate_regs), experts(n, down_regs)
                    if not (edge and n >= NT[L]):
                        e.wait_ge(xl[r], 16 * w + 16)
                        for c in range(DC):
                            mm = e.transpose(ps[:, r % 2, c * P:(c + 1) * P],
                                             xt[r][:, c * P:(c + 1) * P], ident)
                        mm.then_inc(eT_ps[r % 2], 1)
                    if not (edge and (n < 1 or n > NT[L])):
                        _, h, k = tile(1, r, w, c2)
                        x = tile_experts[0][r]
                        e.wait_ge(eT[h], k)
                        for c in range(DC):
                            mm = e.matmul(ps[:, 2 + h, 0:2 * F], xtT[h][:, c, :],
                                          wgu[:, bass.ds(x * (DC * 2 * F) + c * 2 * F, 2 * F)],
                                          start=(c == 0), stop=(c == DC - 1))
                        mm.then_inc(eGU[h], 1)
                    if not (edge and n < 3):
                        _, h, k = tile(3, r, w, c2)
                        x = tile_experts[1][r]
                        e.wait_ge(eHT[h], k)
                        e.matmul(ps[:, 6 + h, 0:D], hT[h], wd[:, bass.ds(x * D, D)],
                                 start=True, stop=True).then_inc(eD[h], 1)
                    if not (edge and (n < 2 or n > NT[L] + 1)):
                        _, h, k = tile(2, r, w, c2)
                        e.wait_ge(eH[h], k)
                        e.transpose(ps[:, 4 + h, 0:P], hm[h], ident).then_inc(eHT_ps[h], 1)

                e.wait_ge(w_exp[L], 32)
                run_steps(e, L, step)

            for L in range(2):
                attention_phase(L)
                end_phase(e, 3 * L + 1)
                end_phase(e, 3 * L + 2)
                expert_phase(L)
                end_phase(e, 3 * L + 3)


TBN = 16
C1N = 2


def _pad_heads(w):
    t = np.zeros((D, H, HP), w.dtype)
    t[:, :, :HD] = w.T.reshape(D, H, HD)
    return _chunks(t.reshape(D, H * HP))


def _chunks(w):
    return np.ascontiguousarray(w.reshape(-1, P, w.shape[1]).transpose(1, 0, 2))


def _padded(b, row):
    t = np.zeros((H, HP), np.float32)
    if b is not None:
        t[:, :HD] = b.reshape(H, HD)
    if row is not None:
        t[:, row] = 1.0
    return t.reshape(-1)


def _experts(g, u, d):
    gu = np.concatenate([g, u], axis=2).reshape(E, DC, P, 2 * F).transpose(2, 0, 1, 3)
    return (np.ascontiguousarray(gu.reshape(P, -1)),
            np.ascontiguousarray(d.transpose(1, 0, 2).reshape(P, -1)))


def layout(i):
    i = {k: np.asarray(v) for k, v in i.items()}
    rows = lambda v: np.ascontiguousarray(np.broadcast_to(v[None], (P, v.shape[0])))
    r = {
        "x": np.ascontiguousarray(i["x"].reshape(B, QT, P, D).transpose(0, 2, 1, 3)),
        "ctxT": np.ascontiguousarray(i["ctx_1024"].transpose(0, 2, 1).reshape(B, DC, P, LK).transpose(0, 2, 1, 3)),
        "mask": np.ascontiguousarray(i["mask_BxS2_ik0"]),
        "consts": consts(),
        "wq0": _pad_heads(i["L0_xattn_Wq"]), "wk0": _pad_heads(i["L0_xattn_Wk"]),
        "wv0": _chunks(i["L0_xattn_Wv"].T), "wo0": _chunks(i["L0_xattn_Wo"].T),
        "bo": rows(i["L0_xattn_bo"]), "bv": rows(i["L1_xattn_v_b"]), "gbias": rows(i["L0_ffn_gate_bias"]),
        "wq1": _pad_heads(i["L1_xattn_q_w"]), "wk1": _pad_heads(i["L1_xattn_k_w"]),
        "wv1": _chunks(i["L1_xattn_v_w"].T),
        "kaug": np.stack([_padded(None, MSK), _padded(i["L1_xattn_k_b"], None)]),
        "bq1": np.ascontiguousarray(_padded(i["L1_xattn_q_b"], MSK).reshape(HT, P).T),
        "gw0": _chunks(i["L0_ffn_gate_w"].T), "gw1": _chunks(i["L1_ffn_Wr"]),
        "wsgu0": _chunks(np.concatenate([i["L0_ffn_Ws_g"].T, i["L0_ffn_Ws_u"].T], axis=1)),
        "wsd0": _chunks(i["L0_ffn_Ws_d"].T),
        "wsgu1": _chunks(np.concatenate([i["L1_ffn_Sg"], i["L1_ffn_Su"]], axis=1)),
        "wsd1": _chunks(i["L1_ffn_Sd"]),
    }
    r["wgu0"], r["wd0"] = _experts(i["L0_ffn_Wg"].transpose(0, 2, 1), i["L0_ffn_Wu"].transpose(0, 2, 1),
                                   i["L0_ffn_Wd"].transpose(0, 2, 1))
    r["wgu1"], r["wd1"] = _experts(i["L1_ffn_Wg"], i["L1_ffn_Wu"], i["L1_ffn_Wd"])
    return r


def kernel(**inputs):
    import concourse.bacc as bacc
    from concourse.bass_utils import run_bass_kernel_spmd as run

    nc = bacc.Bacc("TRN2", target_bir_lowering=False, num_devices=1)
    arrays = {f"in_{k}": v for k, v in layout(inputs).items()}
    a = {k[3:]: nc.dram_tensor(k, v.shape, mybir.dt.from_np(v.dtype), kind="ExternalInput").ap()
         for k, v in arrays.items()}
    out = nc.dram_tensor("out_x", (B, P, QT, D), F32, kind="ExternalOutput").ap()
    build(nc, a, out)
    r = run(nc, [arrays], core_ids=[0])
    y = r.results[0]["out_x"]
    return np.ascontiguousarray(y.transpose(0, 2, 1, 3).reshape(B, LQ, D))
```
